# Optimizing a Trainium2 kernel written in Bass

```python
import numpy as np
import jax
import jax.numpy as jnp

def _softmax(x, axis=-1):
    return jax.nn.softmax(x, axis=axis)

def _gelu(x):
    return jax.nn.gelu(x, approximate=True)

def _silu(x):
    return jax.nn.silu(x)

def _sigmoid(x):
    return jax.nn.sigmoid(x)

def _layernorm(x, axis=-1, eps=1e-05):
    m = jnp.mean(x, axis=axis, keepdims=True)
    v = jnp.var(x, axis=axis, keepdims=True)
    return (x - m) / jnp.sqrt(v + eps)

def _scatter_add(tgt, idx, src, axis=0):
    return tgt.at[idx].add(src)

def _segment_sum(src, seg, n):
    return jax.ops.segment_sum(src, seg, n)
kernel_name = 'mk_xattn_seq_d2_seqx_r2_53fe7d'

def setup_inputs(seed: int=0):
    np.random.seed(seed)
    _w = jnp.asarray

    def _rec_inputs():
        import jax
        import jax.numpy as jnp
        _rk = jax.random.key(seed)
        x = -0.0001661 + 0.9999 * jax.random.normal(jax.random.fold_in(_rk, 1), (32, 100, 512), jnp.float32)
        _lenS = 100 - jax.random.randint(jax.random.fold_in(_rk, 7), (32,), 0, max(1, 100 // 4) + 1, jnp.int32)
        _lenS2 = 722 - jax.random.randint(jax.random.fold_in(_rk, 8), (32,), 0, max(1, 722 // 4) + 1, jnp.int32)
        _ctx_768P = jax.random.normal(jax.random.fold_in(_rk, 11), (32, 16, 384), jnp.float32)
        _ctx_768c = jax.random.dirichlet(jax.random.fold_in(_rk, 511), 0.3 * jnp.ones((16,), jnp.float32), (32, 722))
        _ctx_768t = jnp.einsum('bsk,bkd->bsd', _ctx_768c, _ctx_768P)
        _ctx_768t = _ctx_768t * jax.lax.rsqrt(jnp.mean(jnp.square(_ctx_768t)) + 1e-12) * 0.953939
        ctx_768 = 8.47981e-05 + 1.00068 * (_ctx_768t + 0.3 * jax.random.normal(jax.random.fold_in(_rk, 611), (32, 722, 384), jnp.float32))
        return (x, ctx_768)
    x, ctx_768 = _rec_inputs()

    def _L0_xattn_setup():
        import jax, jax.numpy as jnp
        import numpy as np
        LATENT = 512
        TEXT = 384
        HEADS = 16
        HEAD_DIM = LATENT // HEADS
        SCALE = HEAD_DIM ** (-0.5)
        LN_EPS = 1e-05
        key = jax.random.key(seed)
        ks = jax.random.split(key, 16)
        B, Tx, Txf = (4, 2048, 128)

        def lin(k, fan_in, fan_out):
            bound = 1.0 / np.sqrt(fan_in)
            kw, kb = jax.random.split(k)
            W = jax.random.uniform(kw, (fan_in, fan_out), jnp.float32, -bound, bound)
            b = jax.random.uniform(kb, (fan_out,), jnp.float32, -bound, bound)
            return (W, b)
        Wq, bq = lin(ks[0], LATENT, LATENT)
        Wk, bk = lin(ks[1], TEXT, LATENT)
        Wv, bv = lin(ks[2], TEXT, LATENT)
        Wo, bo = lin(ks[3], LATENT, LATENT)
        W1, b1 = lin(ks[4], LATENT, 4 * LATENT)
        W2, b2 = lin(ks[5], 4 * LATENT, LATENT)
        return {'x': jax.random.normal(ks[6], (B, Tx, LATENT), jnp.float32), 'xf': jax.random.normal(ks[7], (B, Txf, TEXT), jnp.float32), 'Wq': Wq, 'bq': bq, 'Wk': Wk, 'bk': bk, 'Wv': Wv, 'bv': bv, 'Wo': Wo, 'bo': bo, 'ln_g': jnp.ones((LATENT,), jnp.float32), 'ln_b': jnp.zeros((LATENT,), jnp.float32), 'W1': W1, 'b1': b1, 'W2': W2, 'b2': b2}
    _L0_xattn_all = _L0_xattn_setup()
    _L0_xattn_in = {k: v for k, v in _L0_xattn_all.items() if k in ('Wq', 'bq', 'Wk', 'bk', 'Wv', 'bv', 'Wo', 'bo', 'ln_g', 'ln_b', 'W1', 'b1', 'W2', 'b2')}
    del _L0_xattn_all

    def _L1_xattn_setup():
        import jax, jax.numpy as jnp
        import numpy as np
        EPS = 1e-05

        def _layer_norm(x, gamma, beta):
            mu = jnp.mean(x, axis=-1, keepdims=True)
            var = jnp.mean(jnp.square(x - mu), axis=-1, keepdims=True)
            return (x - mu) * jax.lax.rsqrt(var + EPS) * gamma + beta
        key = jax.random.key(seed)
        ks = jax.random.split(key, 12)
        B, Nq, Nkv = (8, 1024, 1024)
        E, Q, KV = (512, 512, 384)

        def lin(k, fan_in, shape):
            bound = 1.0 / np.sqrt(fan_in)
            return jax.random.uniform(k, shape, jnp.float32, -bound, bound)
        return {'q_feat': jax.random.normal(ks[0], (B, Nq, Q), jnp.float32), 'kv_feat': jax.random.normal(ks[1], (B, Nkv, KV), jnp.float32), 'Wq': lin(ks[2], Q, (E, Q)), 'bq': lin(ks[3], Q, (E,)), 'Wk': lin(ks[4], KV, (E, KV)), 'bk': lin(ks[5], KV, (E,)), 'Wv': lin(ks[6], KV, (E, KV)), 'bv': lin(ks[7], KV, (E,)), 'Wd': lin(ks[8], E, (E, E)), 'bd': lin(ks[9], E, (E,)), 'g_q': jnp.ones((Q,), jnp.float32), 'be_q': jnp.zeros((Q,), jnp.float32), 'g_kv': jnp.ones((KV,), jnp.float32), 'be_kv': jnp.zeros((KV,), jnp.float32)}
    _L1_xattn_all = _L1_xattn_setup()
    _L1_xattn_in = {k: v for k, v in _L1_xattn_all.items() if k in ('Wq', 'bq', 'Wk', 'bk', 'Wv', 'bv', 'Wd', 'bd', 'g_q', 'be_q', 'g_kv', 'be_kv')}
    del _L1_xattn_all
    return {'x': x, 'ctx_768': ctx_768, 'L0_xattn_Wq': _L0_xattn_in['Wq'], 'L0_xattn_bq': _L0_xattn_in['bq'], 'L0_xattn_Wk': _L0_xattn_in['Wk'], 'L0_xattn_bk': _L0_xattn_in['bk'], 'L0_xattn_Wv': _L0_xattn_in['Wv'], 'L0_xattn_bv': _L0_xattn_in['bv'], 'L0_xattn_Wo': _L0_xattn_in['Wo'], 'L0_xattn_bo': _L0_xattn_in['bo'], 'L0_xattn_ln_g': _L0_xattn_in['ln_g'], 'L0_xattn_ln_b': _L0_xattn_in['ln_b'], 'L0_xattn_W1': _L0_xattn_in['W1'], 'L0_xattn_b1': _L0_xattn_in['b1'], 'L0_xattn_W2': _L0_xattn_in['W2'], 'L0_xattn_b2': _L0_xattn_in['b2'], 'L1_xattn_Wq': _L1_xattn_in['Wq'], 'L1_xattn_bq': _L1_xattn_in['bq'], 'L1_xattn_Wk': _L1_xattn_in['Wk'], 'L1_xattn_bk': _L1_xattn_in['bk'], 'L1_xattn_Wv': _L1_xattn_in['Wv'], 'L1_xattn_bv': _L1_xattn_in['bv'], 'L1_xattn_Wd': _L1_xattn_in['Wd'], 'L1_xattn_bd': _L1_xattn_in['bd'], 'L1_xattn_g_q': _L1_xattn_in['g_q'], 'L1_xattn_be_q': _L1_xattn_in['be_q'], 'L1_xattn_g_kv': _L1_xattn_in['g_kv'], 'L1_xattn_be_kv': _L1_xattn_in['be_kv']}

def reference(x, ctx_768, L0_xattn_Wq, L0_xattn_bq, L0_xattn_Wk, L0_xattn_bk, L0_xattn_Wv, L0_xattn_bv, L0_xattn_Wo, L0_xattn_bo, L0_xattn_ln_g, L0_xattn_ln_b, L0_xattn_W1, L0_xattn_b1, L0_xattn_W2, L0_xattn_b2, L1_xattn_Wq, L1_xattn_bq, L1_xattn_Wk, L1_xattn_bk, L1_xattn_Wv, L1_xattn_bv, L1_xattn_Wd, L1_xattn_bd, L1_xattn_g_q, L1_xattn_be_q, L1_xattn_g_kv, L1_xattn_be_kv):
    import jax
    import jax.numpy as jnp

    def _L0_xattn_ref(x, xf, Wq, bq, Wk, bk, Wv, bv, Wo, bo, ln_g, ln_b, W1, b1, W2, b2):
        import jax, jax.numpy as jnp
        import numpy as np
        LATENT = 512
        TEXT = 384
        HEADS = 16
        HEAD_DIM = LATENT // HEADS
        SCALE = HEAD_DIM ** (-0.5)
        LN_EPS = 1e-05
        B, Tx, D = x.shape
        Txf = xf.shape[1]
        q = (x @ Wq + bq).reshape(B, Tx, HEADS, HEAD_DIM).transpose(0, 2, 1, 3)
        k = (xf @ Wk + bk).reshape(B, Txf, HEADS, HEAD_DIM).transpose(0, 2, 1, 3)
        v = (xf @ Wv + bv).reshape(B, Txf, HEADS, HEAD_DIM).transpose(0, 2, 1, 3)
        scores = jnp.einsum('bhqd,bhkd->bhqk', q * SCALE, k)
        probs = jax.nn.softmax(scores, axis=-1)
        attn = jnp.einsum('bhqk,bhkd->bhqd', probs, v)
        out = attn.transpose(0, 2, 1, 3).reshape(B, Tx, D)
        out = out @ Wo + bo
        mu = jnp.mean(out, axis=-1, keepdims=True)
        var = jnp.var(out, axis=-1, keepdims=True)
        h = (out - mu) * jax.lax.rsqrt(var + LN_EPS) * ln_g + ln_b
        h = jax.nn.gelu(h @ W1 + b1, approximate=False)
        ffn = h @ W2 + b2
        out = out + ffn
        return x + out

    def _L1_xattn_ref(q_feat, kv_feat, Wq, bq, Wk, bk, Wv, bv, Wd, bd, g_q, be_q, g_kv, be_kv):
        import jax, jax.numpy as jnp
        import numpy as np
        EPS = 1e-05

        def _layer_norm(x, gamma, beta):
            mu = jnp.mean(x, axis=-1, keepdims=True)
            var = jnp.mean(jnp.square(x - mu), axis=-1, keepdims=True)
            return (x - mu) * jax.lax.rsqrt(var + EPS) * gamma + beta
        qn = _layer_norm(q_feat, g_q, be_q)
        kvn = _layer_norm(kv_feat, g_kv, be_kv)
        q = jnp.einsum('bnq,eq->bne', qn, Wq) + bq
        k = jnp.einsum('bmk,ek->bme', kvn, Wk) + bk
        v = jnp.einsum('bmk,ek->bme', kvn, Wv) + bv
        scores = jnp.einsum('bne,bme->bnm', q, k)
        attn = jax.nn.softmax(scores, axis=-1)
        ctx = jnp.einsum('bnm,bme->bne', attn, v)
        hidden = jnp.einsum('bne,fe->bnf', ctx, Wd) + bd
        return q_feat + hidden
    x = _L0_xattn_ref(x, ctx_768, L0_xattn_Wq, L0_xattn_bq, L0_xattn_Wk, L0_xattn_bk, L0_xattn_Wv, L0_xattn_bv, L0_xattn_Wo, L0_xattn_bo, L0_xattn_ln_g, L0_xattn_ln_b, L0_xattn_W1, L0_xattn_b1, L0_xattn_W2, L0_xattn_b2)
    x = _L1_xattn_ref(x, ctx_768, L1_xattn_Wq, L1_xattn_bq, L1_xattn_Wk, L1_xattn_bk, L1_xattn_Wv, L1_xattn_bv, L1_xattn_Wd, L1_xattn_bd, L1_xattn_g_q, L1_xattn_be_q, L1_xattn_g_kv, L1_xattn_be_kv)
    return x

_drawn_inputs = setup_inputs


def setup_inputs(seed=0):
    import zlib

    import numpy as np

    out = dict(_drawn_inputs(seed))
    spreads = {'L0_xattn_ln_g': (1.0, 0.2),
     'L0_xattn_ln_b': (0.0, 0.367),
     'L1_xattn_g_q': (1.0, 0.2),
     'L1_xattn_be_q': (0.0, 0.1),
     'L1_xattn_g_kv': (1.0, 0.2),
     'L1_xattn_be_kv': (0.0, 0.1)}
    factors = {'L0_xattn_bq': 40.362,
     'L0_xattn_bk': 64.0,
     'L0_xattn_b1': 6.265,
     'L0_xattn_b2': 4.543,
     'L1_xattn_bq': 3.269,
     'L1_xattn_bk': 64.0,
     'L1_xattn_bv': 3.613}
    for name, (base, spread) in spreads.items():
        noise = np.random.default_rng([zlib.crc32(name.encode()), seed]).standard_normal(out[name].shape)
        drawn = base * np.exp(spread * noise) if base else spread * noise
        out[name] = jnp.asarray(drawn.astype(out[name].dtype))
    for name, factor in factors.items():
        out[name] = (out[name] * factor).astype(out[name].dtype)
    return out
```

```python
from contextlib import ExitStack

import concourse.bass as bass
from concourse import mybir

F32 = mybir.dt.float32
F32R = mybir.dt.float32r
ALU = mybir.AluOpType
ACT = mybir.ActivationFunctionType
AX = mybir.AxisListType

P = 128
BANK = 512
EPS = 1e-5
HEADS = 16
HI, LO = 0, 1
PASSES = ((HI, HI), (HI, LO), (LO, HI))


def wait(eng, sem, value):
    if isinstance(value, int) and value <= 0:
        return
    eng.wait_ge(sem, value)


def wait_alone(eng, sem, value, passed):
    wait(eng, sem, value)
    eng.sem_inc(passed, 1)


class Inputs:

    def __init__(self, t):
        self.x, self.ctx = t["x"], t["ctx_768"]
        self.Wq0, self.bq0, self.Wk0, self.bk0 = (t[f"L0_xattn_{n}"] for n in ("Wq", "bq", "Wk", "bk"))
        self.Wv0, self.bv0, self.Wo, self.bo = (t[f"L0_xattn_{n}"] for n in ("Wv", "bv", "Wo", "bo"))
        self.ln_g, self.ln_b, self.W1, self.b1 = (t[f"L0_xattn_{n}"] for n in ("ln_g", "ln_b", "W1", "b1"))
        self.W2, self.b2 = t["L0_xattn_W2"], t["L0_xattn_b2"]
        self.Wq1, self.bq1, self.Wk1, self.bk1 = (t[f"L1_xattn_{n}"] for n in ("Wq", "bq", "Wk", "bk"))
        self.Wv1, self.bv1, self.Wd, self.bd = (t[f"L1_xattn_{n}"] for n in ("Wv", "bv", "Wd", "bd"))
        self.g_q, self.be_q, self.g_kv, self.be_kv = (t[f"L1_xattn_{n}"] for n in ("g_q", "be_q", "g_kv", "be_kv"))
        self.out = t["out"]


class Shapes:
    def __init__(self, io):
        self.B, self.N, self.D = io.x.shape
        _, self.M, self.T = io.ctx.shape
        self.E, self.F = io.Wq1.shape[0], io.W1.shape[1]
        self.SCALE = float(self.D // HEADS) ** -0.5


class Kept:
    pass


class Scope:

    def __init__(self, nc, ctx):
        self.nc, self.ctx = nc, ctx

    def sb(self, name, shape, dt=F32):
        return self.ctx.enter_context(self.nc.sbuf_tensor(name, shape, dt))

    def psum(self, name, shape):
        return self.ctx.enter_context(self.nc.psum_tensor(name, shape, F32))

    def sem(self, name):
        return self.ctx.enter_context(self.nc.semaphore(name))

    def sems(self, name, n):
        return [self.sem(f"{name}{i}") for i in range(n)]


class Batch:

    def __init__(self, pair, par):
        self.pair, self.par = pair, par
        self.n = pair * 2 + par

    def next(self):
        return Batch(self.pair, 1) if self.par == 0 else Batch(self.pair + 1, 0)

    def prev(self):
        return Batch(self.pair, 0) if self.par == 1 else Batch(self.pair - 1, 1)


def column(ap):
    return ap.rearrange("(c p) -> p c", p=P)


def row(ap):
    return ap.partition_broadcast(P)


def chunks(ap):
    return ap.rearrange("(c p) n -> p c n", p=P)


def fold_phase(nc, d, io, keep):
    D, T, E = d.D, d.T, d.E
    DC, TC, EC = D // P, T // P, E // P
    with ExitStack() as ctx:
        s = Scope(nc, ctx)
        wq, wk, wv = s.sb("f_wq", [P, EC, D]), s.sb("f_wk", [P, EC, T]), s.sb("f_wv", [P, EC, T])
        wd, wdT = s.sb("f_wd", [P, EC, E]), s.sb("f_wdT", [P, EC, E])
        wo0 = s.sb("f_wo0", [P, DC, D])
        gkv_row, bekv_row = s.sb("f_gkv_row", [P, T]), s.sb("f_bekv_row", [P, T])
        gq_row, beq_row = s.sb("f_gq_row", [P, D]), s.sb("f_beq_row", [P, D])
        bd_row, bo_row = s.sb("f_bd_row", [P, E]), s.sb("f_bo_row", [P, D])
        gq, gkv, beq = s.sb("f_gq", [P, DC]), s.sb("f_gkv", [P, TC]), s.sb("f_beq", [P, DC])
        bq, bk, bv, bv0 = (s.sb(f"f_b{n}", [P, EC]) for n in ("q", "k", "v", "v0"))
        bks, bvs = s.sb("f_bks", [P, EC]), s.sb("f_bvs", [P, EC])
        junk = s.sb("f_junk", [P, D])
        bks_wide, bvs_wide, bv0_wide = (s.sb(f"f_{n}_wide", [P, EC, P]) for n in ("bks", "bvs", "bv0"))
        a_raw, a_s = s.sb("f_a_raw", [P, DC, T]), s.sb("f_a_s", [P, DC, T])
        a_hl, b_hl = s.sb("f_a_hl", [P, 2, DC, T], F32R), s.sb("f_b_hl", [P, 2, TC, E], F32R)
        b_s = s.sb("f_b_s", [P, TC, E])
        u, csum, qbk = s.sb("f_u", [P, D]), s.sb("f_csum", [P, 1]), s.sb("f_qbk", [P, 1])
        ps = [s.psum(f"f_ps{i}", [P, BANK]) for i in range(8)]
        loads, wo_loads, stores = s.sem("f_loads"), s.sem("f_wo_loads"), s.sem("f_stores")
        sums_ready = s.sem("f_sums_ready")
        wide_ready = s.sem("f_wide_ready")
        wdT_in_psum, wdT_ready = s.sem("f_wdT_in_psum"), s.sem("f_wdT_ready")
        a_in_psum, a_copied = s.sem("f_a_in_psum"), s.sem("f_a_copied")
        a_scaled, a_hi_ready, a_lo_ready = s.sem("f_a_scaled"), s.sem("f_a_hi_ready"), s.sem("f_a_lo_ready")
        b_in_psum, b_scaled, b_hi_ready, b_lo_ready = (
            s.sem(f"f_b_{n}") for n in ("in_psum", "scaled", "hi_ready", "lo_ready"))
        rows_in_psum, u_ready, rows_done = s.sem("f_rows_in_psum"), s.sem("f_u_ready"), s.sem("f_rows_done")
        ident_ready = s.sem("f_ident_ready")
        block = ctx.enter_context(nc.Block())
        W2C = d.F // D
        PIECES = [("wo", 0)] + [("w1", k) for k in range(DC)] + [("w2", k) for k in range(W2C)]
        pw, pw_hl = s.sb("f_pw", [P, 2, d.F]), s.sb("f_pw_hl", [P, 2, 2, d.F], F32R)
        ln_g, ln_b, b1, b1_sum = s.sb("f_ln_g", [P, DC]), s.sb("f_ln_b", [P, DC]), s.sb("f_b1", [P, d.F // P]), s.sb("f_b1_sum", [P, DC, d.F // P])
        piece_loaded, piece_stored = s.sems("f_piece_loaded", 2), s.sems("f_piece_stored", 2)
        piece_hi, piece_lo, ln_loaded = s.sem("f_piece_hi"), s.sem("f_piece_lo"), s.sem("f_ln_loaded")
        b1_in_psum, b1_done = s.sem("f_b1_in_psum"), s.sem("f_b1_done")
        VECTORS = ((gkv_row, row(io.g_kv)), (bekv_row, row(io.be_kv)), (gq_row, row(io.g_q)),
                   (beq_row, row(io.be_q)), (bd_row, row(io.bd)), (bo_row, row(io.bo)),
                   (gq, column(io.g_q)), (gkv, column(io.g_kv)), (beq, column(io.be_q)),
                   (bq, column(io.bq1)), (bk, column(io.bk1)), (bv, column(io.bv1)), (bv0, column(io.bv0)))
        ALL_LOADS = 16 * (4 + len(VECTORS))

        @block.sync
        def _(sp):
            for t, w in ((wq, io.Wq1), (wk, io.Wk1), (wv, io.Wv1), (wd, io.Wd)):
                sp.dma_start(t[:], chunks(w)).then_inc(loads, 16)
            for t, v in VECTORS:
                sp.dma_start(t[:], v, allow_slow_non_contiguous=True).then_inc(loads, 16)
            sp.dma_start(wo0[:], chunks(io.Wo)).then_inc(wo_loads, 16)

            def load(n):
                kind, k = PIECES[n]
                src = {"wo": lambda: chunks(io.Wo), "w1": lambda: io.W1[P * k:P * (k + 1), :],
                       "w2": lambda: chunks(io.W2[D * k:D * (k + 1), :])}[kind]()
                dst = pw[:, n % 2, :]
                if kind != "w1":
                    dst = dst.rearrange("p (c n) -> p c n", n=D)
                sp.dma_start(dst, src).then_inc(piece_loaded[n % 2], 16)

            for t, v in ((ln_g, io.ln_g), (ln_b, io.ln_b), (b1, io.b1)):
                sp.dma_start(t[:], column(v), allow_slow_non_contiguous=True).then_inc(ln_loaded, 16)
            load(0)
            load(1)
            for n, (kind, k) in enumerate(PIECES):
                sp.wait_ge(piece_hi, n + 1)
                sp.wait_ge(piece_lo, n + 1)
                for hl in range(2):
                    src = pw_hl[:, n % 2, hl, :].bitcast(F32)
                    if kind == "w1":
                        dst = keep.W1_dram[:, :, hl, k, :].rearrange("j p n -> p j n")
                        src = src.rearrange("p (j n) -> p j n", n=P)
                    else:
                        dst = (keep.Wo_dram[hl] if kind == "wo" else keep.W2_dram[hl, D * k:D * (k + 1), :])
                        dst = dst.rearrange("(c p) n -> p c n", p=P)
                        src = src.rearrange("p (c n) -> p c n", n=D)
                    sp.dma_start(dst, src).then_inc(piece_stored[n % 2], 16)
                if n + 2 < len(PIECES):
                    if kind == "w1":
                        sp.wait_ge(b1_in_psum, k + 1)
                    load(n + 2)
            for par in range(2):
                sp.wait_ge(piece_stored[par], 32 * len(range(par, len(PIECES), 2)))
            sp.wait_ge(a_hi_ready, 1)
            sp.wait_ge(a_lo_ready, 1)
            sp.dma_start(keep.A_dram.rearrange("h (c p) n -> p h c n", p=P), a_hl[:].bitcast(F32)).then_inc(stores, 16)
            sp.wait_ge(b_hi_ready, 1)
            sp.wait_ge(b_lo_ready, 1)
            sp.dma_start(keep.B_dram.rearrange("h (c p) n -> p h c n", p=P), b_hl[:].bitcast(F32)).then_inc(stores, 16)
            sp.wait_ge(stores, 32)

        @block.gpsimd
        def _(pool):
            nc.gpsimd.memset(keep.minus_half[:], -0.5)
            nc.gpsimd.memset(keep.ident[:], 0.0).then_inc(ident_ready, 1)
            pool.wait_ge(ident_ready, 1)
            nc.gpsimd.affine_select(out=keep.ident[:], in_=keep.ident[:], compare_op=ALU.not_equal, fill=1.0,
                                    base=0, pattern=[[-1, P]], channel_multiplier=1).then_inc(ident_ready, 1)

        @block.vector
        def _(dve):
            dve.wait_ge(loads, ALL_LOADS)
            for n, (w, b, out) in enumerate(((wk, bk, bks), (wv, bv, bvs))):
                for c in range(EC):
                    wait(dve, sums_ready, n * EC + c)
                    nc.vector.tensor_tensor_reduce(out=junk[:, 0:T], in0=w[:, c, :], in1=bekv_row[:], scale=1.0,
                                                   scalar=b[:, c:c + 1], op0=ALU.mult, op1=ALU.add,
                                                   accum_out=out[:, c:c + 1]).then_inc(sums_ready, 1)
            dve.wait_ge(sums_ready, 2 * EC)
            for src, dst in ((bks, bks_wide), (bvs, bvs_wide), (bv0, bv0_wide)):
                nc.vector.tensor_copy(dst[:], src[:].unsqueeze(2).to_broadcast([P, EC, P])).then_inc(wide_ready, 1)
            dve.wait_ge(wdT_in_psum, 1)
            for c in range(EC):
                nc.vector.tensor_copy(wdT[:, c, :], ps[c][:, 0:E]).then_inc(wdT_ready, 1)
            dve.wait_ge(a_in_psum, 1)
            for c in range(DC):
                nc.vector.tensor_copy(a_raw[:, c, :], ps[4 + c][:, 0:T]).then_inc(a_copied, 1)
                dve.wait_ge(a_copied, c + 1)
                nc.vector.scalar_tensor_tensor(out=a_s[:, c, :], in0=a_raw[:, c, :], scalar=gq[:, c:c + 1],
                                               in1=gkv_row[:], op0=ALU.mult, op1=ALU.mult).then_inc(a_scaled, 1)
            dve.wait_ge(a_hi_ready, 1)
            nc.vector.tensor_tensor(a_hl[:, LO], a_s[:], a_hl[:, HI].bitcast(F32), ALU.subtract).then_inc(a_lo_ready, 1)
            dve.wait_ge(b_in_psum, 1)
            for c in range(TC):
                nc.vector.tensor_scalar(b_s[:, c, :], ps[c][:, 0:E], gkv[:, c:c + 1], None, ALU.mult).then_inc(b_scaled, 1)
            dve.wait_ge(b_hi_ready, 1)
            nc.vector.tensor_tensor(b_hl[:, LO], b_s[:], b_hl[:, HI].bitcast(F32), ALU.subtract).then_inc(b_lo_ready, 1)
            dve.wait_ge(rows_in_psum, 1)
            nc.vector.tensor_copy(u[:], ps[4][:, 0:D]).then_inc(u_ready, 1)
            dve.wait_ge(u_ready, 1)
            nc.vector.tensor_tensor(keep.score_row[:], u[:], gq_row[:], ALU.mult).then_inc(rows_done, 1)
            nc.vector.tensor_tensor_reduce(out=junk[:], in0=u[:], in1=beq_row[:], scale=1.0, scalar=0.0,
                                           op0=ALU.mult, op1=ALU.add, accum_out=csum[:]).then_inc(rows_done, 1)
            dve.wait_ge(rows_done, 2)
            nc.vector.tensor_tensor(keep.score_const[:], ps[7][:, 0:1], csum[:], ALU.add).then_inc(rows_done, 1)
            nc.vector.tensor_tensor(keep.bd_row[:], ps[5][:, 0:E], bd_row[:], ALU.add).then_inc(rows_done, 1)
            nc.vector.tensor_tensor(keep.bo_row[:], ps[6][:, 0:D], bo_row[:], ALU.add).then_inc(rows_done, 1)
            nc.vector.tensor_tensor(keep.t_bias[:], ps[3][:, 0:TC], gkv[:], ALU.mult).then_inc(rows_done, 1)
            dve.wait_ge(rows_done, 6)
            dve.wait_ge(ln_loaded, 48)
            for n, (kind, k) in enumerate(PIECES):
                dve.wait_ge(piece_hi, n + 1)
                hi = pw_hl[:, n % 2, HI, :].bitcast(F32)
                if kind == "w1":
                    nc.vector.scalar_tensor_tensor(out=pw_hl[:, n % 2, LO, :], in0=pw[:, n % 2, :], scalar=ln_g[:, k:k + 1],
                                                   in1=hi, op0=ALU.mult, op1=ALU.subtract).then_inc(piece_lo, 1)
                else:
                    nc.vector.tensor_tensor(pw_hl[:, n % 2, LO, :], pw[:, n % 2, :], hi, ALU.subtract).then_inc(piece_lo, 1)
            dve.wait_ge(b1_in_psum, DC)
            nc.vector.tensor_copy(b1_sum[:], ps[0][:, 0:DC * (d.F // P)].rearrange("p (k j) -> p k j", k=DC)).then_inc(b1_done, 1)
            for k in range(DC):
                dve.wait_ge(b1_done, k + 1)
                nc.vector.tensor_tensor(keep.b1[:], b1_sum[:, k, :], (b1 if k == 0 else keep.b1)[:], ALU.add).then_inc(b1_done, 1)

        @block.scalar
        def _(act):
            act.wait_ge(a_scaled, DC)
            nc.scalar.activation(a_hl[:, HI], a_s[:], ACT.Copy).then_inc(a_hi_ready, 1)
            act.wait_ge(b_scaled, TC)
            nc.scalar.activation(b_hl[:, HI], b_s[:], ACT.Copy).then_inc(b_hi_ready, 1)
            act.wait_ge(ln_loaded, 48)
            for n, (kind, k) in enumerate(PIECES):
                act.wait_ge(piece_loaded[n % 2], 16 * (n // 2 + 1))
                wait(act, piece_stored[n % 2], 32 * (n // 2))
                act_scale = ln_g[:, k:k + 1] if kind == "w1" else 1.0
                nc.scalar.activation(pw_hl[:, n % 2, HI, :], pw[:, n % 2, :], ACT.Copy, scale=act_scale).then_inc(piece_hi, 1)

        @block.tensor
        def _(pe):
            pe.wait_ge(ident_ready, 2)
            pe.wait_ge(loads, ALL_LOADS)
            for c in range(EC):
                for f in range(EC):
                    last = nc.tensor.transpose(ps[c][:, P * f:P * (f + 1)], wd[:, f, P * c:P * (c + 1)], keep.ident[:])
            last.then_inc(wdT_in_psum, 1)
            for c in range(DC):
                for e in range(EC):
                    last = nc.tensor.matmul(ps[4 + c][:, 0:T], wq[:, e, P * c:P * (c + 1)], wk[:, e, :],
                                            start=e == 0, stop=e == EC - 1)
            last.then_inc(a_in_psum, 1)
            pe.wait_ge(wdT_ready, EC)
            for c in range(TC):
                for e in range(EC):
                    last = nc.tensor.matmul(ps[c][:, 0:E], wv[:, e, P * c:P * (c + 1)], wdT[:, e, :],
                                            start=e == 0, stop=e == EC - 1)
            last.then_inc(b_in_psum, 1)
            pe.wait_ge(wide_ready, 3)
            pe.wait_ge(wo_loads, 16)
            pe.wait_ge(a_copied, DC)
            for bank, lhs, rhs in ((4, bks_wide, wq), (5, bvs_wide, wdT), (6, bv0_wide, wo0), (7, bks_wide, bq)):
                n = 1 if rhs is bq else D
                for e in range(EC):
                    moving = bq[:, e:e + 1] if rhs is bq else rhs[:, e, :]
                    nc.tensor.matmul(ps[bank][:, 0:n], lhs[:, e, :], moving, start=e == 0, stop=e == EC - 1)
            for c in range(TC):
                for e in range(EC):
                    nc.tensor.matmul(ps[3][:, c:c + 1], wk[:, e, P * c:P * (c + 1)], bq[:, e:e + 1],
                                     start=e == 0, stop=False)
                for q in range(DC):
                    last = nc.tensor.matmul(ps[3][:, c:c + 1], a_raw[:, q, P * c:P * (c + 1)], beq[:, q:q + 1],
                                            start=False, stop=q == DC - 1)
            last.then_inc(rows_in_psum, 1)
            pe.wait_ge(ln_loaded, 48)
            pe.wait_ge(b_scaled, TC)
            for k in range(DC):
                n = PIECES.index(("w1", k))
                pe.wait_ge(piece_loaded[n % 2], 16 * (n // 2 + 1))
                for j in range(d.F // P):
                    at0 = k * (d.F // P) + j
                    last = nc.tensor.matmul(ps[0][:, at0:at0 + 1], pw[:, n % 2, P * j:P * (j + 1)], ln_b[:, k:k + 1],
                                            start=True, stop=True)
                last.then_inc(b1_in_psum, 1)


def queries_phase(nc, d, io, keep):
    D, T, N = d.D, d.T, d.N
    DC, TC = D // P, T // P
    PER = 4
    STEPS = d.B // PER
    TOK = PER * N
    with ExitStack() as ctx:
        s = Scope(nc, ctx)
        wq, wk, wv = s.sb("q_wq", [P, DC, D]), s.sb("q_wk", [P, TC, D]), s.sb("q_wv", [P, TC, D])
        wq_hl = s.sb("q_wq_hl", [P, 2, DC, D], F32R)
        bq, bqs = s.sb("q_bq", [P, DC]), s.sb("q_bqs", [P, DC])
        xn = s.sb("q_xn", [N, PER, D])
        xT = s.sb("q_xT", [P, 2, DC, TOK], F32R)
        q32 = s.sb("q_q32", [P, DC, TOK])
        q_hl = s.sb("q_q_hl", [P, 2, DC, TOK], F32R)
        pt = [s.psum(f"q_pt{i}", [P, BANK]) for i in range(4)]
        pq = [s.psum(f"q_pq{i}", [P, BANK]) for i in range(4)]
        passed = s.sem("q_passed")
        w_loads, x_loads, stores = s.sem("q_w_loads"), s.sem("q_x_loads"), s.sem("q_stores")
        w_hi, w_lo, bias_ready = s.sem("q_w_hi"), s.sem("q_w_lo"), s.sem("q_bias_ready")
        xT_in_psum, xT_hi, xT_lo = s.sem("q_xT_in_psum"), s.sem("q_xT_hi"), s.sem("q_xT_lo")
        q_in_psum, q_ready, q_hi, q_lo = (s.sem(f"q_q_{n}") for n in ("in_psum", "ready", "hi", "lo"))
        block = ctx.enter_context(nc.Block())
        WEIGHTS = ((wq, wq_hl), (wk, keep.wk_hl), (wv, keep.wv_hl))
        x_rows = io.x.rearrange("b n d -> (b n) d")

        def all_steps(eng, step):
            step(0)
            with eng.Fori(1, STEPS) as i:
                step(i)

        @block.sync
        def _(sp):
            sp.dma_start(wq[:], chunks(io.Wq0)).then_inc(w_loads, 16)
            sp.dma_start(bq[:], column(io.bq0), allow_slow_non_contiguous=True).then_inc(w_loads, 16)
            sp.dma_start(keep.bk0[:], column(io.bk0), allow_slow_non_contiguous=True).then_inc(w_loads, 16)
            sp.dma_start(wk[:], chunks(io.Wk0)).then_inc(w_loads, 16)
            sp.dma_start(wv[:], chunks(io.Wv0)).then_inc(w_loads, 16)
            def step(i):
                wait(sp, xT_in_psum, i * DC)
                sp.dma_start(xn[:], x_rows[bass.ds(i * TOK, TOK), :].rearrange("(t p) d -> p t d", p=N)).then_inc(x_loads, 16)
                wait_alone(sp, q_lo, (i + 1) * DC, passed)
                sp.dma_start(keep.q_dram[:, :, bass.ds(i * TOK, TOK)].rearrange("h (c p) n -> p h c n", p=P),
                             q_hl[:].bitcast(F32)).then_inc(stores, 16)

            all_steps(sp, step)
            sp.wait_ge(stores, 16 * STEPS)

        @block.tensor
        def _(pe):
            pe.wait_ge(w_lo, 3)
            def step(i):
                pe.wait_ge(x_loads, 16 * (i + 1))
                for k in range(DC):
                    wait(pe, xT_lo, i * DC)
                    for t in range(PER):
                        last = nc.tensor.transpose(pt[k][:, t * N:(t + 1) * N], xn[:, t, P * k:P * (k + 1)],
                                                   keep.ident[0:N, 0:N])
                    last.then_inc(xT_in_psum, 1)
                pe.wait_ge(xT_lo, (i + 1) * DC)
                wait(pe, q_ready, i * DC)
                for c in range(DC):
                    for k in range(DC):
                        for a, b in PASSES:
                            last = nc.tensor.matmul(pq[c][:, 0:TOK], wq_hl[:, a, k, P * c:P * (c + 1)], xT[:, b, k, :],
                                                    start=(k, a, b) == (0, HI, HI), stop=(k, a, b) == (DC - 1, LO, HI))
                    last.then_inc(q_in_psum, 1)

            all_steps(pe, step)

        @block.scalar
        def _(act):
            act.wait_ge(w_loads, 5 * 16)
            nc.scalar.mul(bqs[:], bq[:], d.SCALE).then_inc(bias_ready, 1)
            for w, hl in WEIGHTS:
                nc.scalar.activation(hl[:, HI], w[:], ACT.Copy).then_inc(w_hi, 1)
            act.wait_ge(bias_ready, 1)
            def step(i):
                for k in range(DC):
                    act.wait_ge(xT_in_psum, i * DC + k + 1)
                    wait(act, q_in_psum, i * DC)
                    nc.scalar.activation(xT[:, HI, k, :], pt[k][:, 0:TOK], ACT.Copy).then_inc(xT_hi, 1)
                wait(act, stores, i * 16)
                wait(act, q_lo, i * DC)
                for c in range(DC):
                    act.wait_ge(q_in_psum, i * DC + c + 1)
                    nc.scalar.activation(q32[:, c, :], pq[c][:, 0:TOK], ACT.Identity, bias=bqs[:, c:c + 1],
                                         scale=d.SCALE).then_inc(q_ready, 1)
                    act.wait_ge(q_ready, i * DC + c + 1)
                    nc.scalar.activation(q_hl[:, HI, c, :], q32[:, c, :], ACT.Copy).then_inc(q_hi, 1)

            all_steps(act, step)

        @block.vector
        def _(dve):
            for n, (w, hl) in enumerate(WEIGHTS):
                dve.wait_ge(w_hi, n + 1)
                nc.vector.tensor_tensor(hl[:, LO], w[:], hl[:, HI].bitcast(F32), ALU.subtract).then_inc(w_lo, 1)
            def step(i):
                for k in range(DC):
                    dve.wait_ge(xT_hi, i * DC + k + 1)
                    nc.vector.tensor_tensor(xT[:, LO, k, :], pt[k][:, 0:TOK], xT[:, HI, k, :].bitcast(F32),
                                            ALU.subtract).then_inc(xT_lo, 1)
                for c in range(DC):
                    dve.wait_ge(q_hi, i * DC + c + 1)
                    nc.vector.tensor_tensor(q_hl[:, LO, c, :], q32[:, c, :], q_hl[:, HI, c, :].bitcast(F32),
                                            ALU.subtract).then_inc(q_lo, 1)

            all_steps(dve, step)


def attention_phase(nc, d, io, keep):
    B, N, M, D, T = d.B, d.N, d.M, d.D, d.T
    TC, DC, DH = T // P, D // P, D // HEADS
    MT = -(-M // P)
    LAST = M - P * (MT - 1)
    TB = MT // 2
    SPLIT = ((0, TB * P), (TB * P, M - TB * P))
    MH = M // 2
    SW = MH + 1
    PAIRS, QUADS = HEADS // 2, HEADS // 4
    assert M % 2 == 0 and SW % 2 == 0 and MT % 2 == 0
    K_STEPS = [("k", c, n) for c in range(DC) for n in range(2)]
    V_STEPS = [("v", t, 0) for t in range(MT)]
    STEPS = [x for pair in zip(K_STEPS, V_STEPS) for x in pair] + K_STEPS[MT:]
    NK, NV, NSTEP = len(K_STEPS), len(V_STEPS), len(STEPS)
    FILLS = TC
    NEED_K = [STEPS.index(("k", c, 1)) for c in range(DC)]
    by_slot = [[n for n in range(NSTEP) if min(FILLS + n, HEADS - 1) == h] for h in range(HEADS)]

    def k_before(n):
        return sum(x[0] == "k" for x in STEPS[:n])

    def rows_of(t):
        return LAST if t == MT - 1 else P

    with ExitStack() as ctx:
        s = Scope(nc, ctx)
        cn = [s.sb(f"a_cn{i}", [P, MT, T]) for i in range(2)]
        cT = s.sb("a_cT", [P, 2, TC, M], F32R)
        kt = [s.sb(f"a_kt{i}", [P, PAIRS, M], F32R) for i in range(2)]
        vn = [s.sb(f"a_vn{i}", [P, MT, D]) for i in range(2)]
        qm = [s.sb(f"a_qm{i}", [P, 2, HEADS, N], F32R) for i in range(2)]
        pr = s.sb("a_pr", [N, 4, M])
        pT = s.sb("a_pT", [P, 2, 4, MT, N])
        nmax, sums = s.sb("a_nmax", [N, 2, HEADS]), s.sb("a_sums", [N, 2, HEADS])
        rexp = s.sb("a_rexp", [N, 2, 4, DH])
        rb = s.sb("a_rb", [P, 2, N])
        at = s.sb("a_at", [P, 2, QUADS, N])
        ps = s.psum("a_ps", [P, 8 * BANK])
        tp = [ps[:, 4 * BANK:5 * BANK], ps[:, 5 * BANK:6 * BANK]]
        pj, av = ps[:, 6 * BANK:7 * BANK], ps[:, 7 * BANK:8 * BANK]

        def scores(buf):
            start = 2 * buf * BANK
            return ps[0:N, start:start + 2 * (BANK + 1)].rearrange("p (c n) -> p c n", c=2)[:, :, 0:MH]

        ctx_loaded, q_loaded = s.sems("a_ctx_loaded", 2), s.sems("a_q_loaded", 2)
        zeroed, stored = s.sem("a_zeroed"), s.sems("a_stored", 2)
        filled, cT_hi, cT_lo = s.sem("a_filled"), s.sem("a_cT_hi"), s.sem("a_cT_lo")
        proj_done, k_hi = s.sem("a_proj_done"), s.sem("a_k_hi")
        k_ready, v_ready = s.sem("a_k_ready"), s.sem("a_v_ready")
        scores_done, max_ready, exp_done = s.sem("a_scores_done"), s.sem("a_max_ready"), s.sem("a_exp_done")
        p_turned, pT_ready = s.sem("a_p_turned"), s.sems("a_pT_ready", 2)
        rexp_ready, av_done = s.sem("a_rexp_ready"), s.sem("a_av_done")
        rb_ready, at_ready = s.sem("a_rb_ready"), s.sem("a_at_ready")
        block = ctx.enter_context(nc.Block())
        Q_LOADS = 8 * 16

        def all_batches(eng, batch):
            batch(Batch(0, 0), first=True)
            batch(Batch(0, 1))
            with eng.Fori(1, B // 2 - 1) as pair:
                batch(Batch(pair, 0))
                batch(Batch(pair, 1))
            batch(Batch(B // 2 - 1, 0))
            batch(Batch(B // 2 - 1, 1), last=True)

        @block.sync
        def _(sp):
            def load_ctx(b):
                wait(sp, filled, (b.n - 1) * 2 * FILLS)
                src = io.ctx[bass.ds(b.n, 1), :, :].rearrange("b m t -> (b m) t")
                whole = P * (MT - 1)
                sp.dma_start(cn[b.par][:, 0:MT - 1, :], src[0:whole, :].rearrange("(t p) d -> p t d", p=P)).then_inc(ctx_loaded[b.par], 16)
                sp.dma_start(cn[b.par][0:LAST, MT - 1, :], src[whole:M, :]).then_inc(ctx_loaded[b.par], 16)

            def load_q(b):
                wait(sp, scores_done, (b.n - 1) * HEADS)
                for hl in range(2):
                    src = keep.q_dram[hl, :, bass.ds(b.n * N, N)].rearrange("(i o d) n -> o d i n", o=2, d=DH)
                    for odd in range(2):
                        dst = qm[b.par][:, hl].bitcast(F32).rearrange("p (i o) n -> p o i n", o=2)[:, odd]
                        for copy in range(2):
                            r = (2 * copy + odd) * DH
                            sp.dma_start(dst[r:r + DH], src[odd]).then_inc(q_loaded[b.par], 16)

            def store(b):
                sp.wait_ge(at_ready, (b.n + 1) * QUADS)
                sp.dma_start(keep.attn_dram[:, bass.ds(b.n * N, N)].rearrange("(c p) n -> p c n", p=P),
                             at[:, b.par]).then_inc(stored[b.par], 16)

            def batch(b, first=False, last=False):
                if not isinstance(b.n, int) or b.n + 2 < B:
                    load_ctx(b.next().next())
                if not last:
                    load_q(b.next())
                if not first:
                    store(b.prev())

            load_ctx(Batch(0, 0))
            load_ctx(Batch(0, 1))
            sp.wait_ge(zeroed, 2)
            load_q(Batch(0, 0))
            all_batches(sp, batch)
            store(Batch(B // 2 - 1, 1))
            for par in range(2):
                sp.wait_ge(stored[par], 16 * (B // 2))

        @block.gpsimd
        def _(pool):
            for i in range(2):
                nc.gpsimd.memset(qm[i][:].bitcast(F32), 0.0).then_inc(zeroed, 1)

        @block.tensor
        def _(pe):
            def bank_free(heads, fills):
                for n in range(2):
                    wait(pe, pT_ready[n], heads)
                wait(pe, cT_lo, fills * 2)

            def fill(b, k, heads):
                if k == 0:
                    pe.wait_ge(ctx_loaded[b.par], (b.pair + 1) * 32)
                bank_free(heads, b.n * FILLS + k)
                for n in range(2):
                    for t in range(TB * n, TB * (n + 1)):
                        at0, rows = P * (t - TB * n), rows_of(t)
                        last = nc.tensor.transpose(tp[n][:, at0:at0 + rows], cn[b.par][0:rows, t, P * k:P * (k + 1)],
                                                   keep.ident[0:rows, 0:rows])
                    last.then_inc(filled, 1)

            def project(b, n):
                kind, i, half = STEPS[n]
                if n == 0:
                    pe.wait_ge(cT_lo, (b.n + 1) * 2 * FILLS)
                wait(pe, k_ready, b.n * NK + k_before(n))
                wait(pe, v_ready, b.n * NV + n - k_before(n))
                for k in range(TC):
                    for x, y in PASSES:
                        flags = dict(start=(k, x, y) == (0, HI, HI), stop=(k, x, y) == (TC - 1, LO, HI))
                        if kind == "k":
                            m0, cols = SPLIT[half]
                            last = nc.tensor.matmul(pj[:, 0:cols], keep.wk_hl[:, x, k, P * i:P * (i + 1)],
                                                    cT[:, y, k, m0:m0 + cols], **flags)
                        else:
                            last = nc.tensor.matmul(pj[0:rows_of(i), :], cT[:, x, k, P * i:P * i + rows_of(i)],
                                                    keep.wv_hl[:, y, k, :], **flags)
                last.then_inc(proj_done, 1)

            def score(b, h):
                if h == 0:
                    pe.wait_ge(q_loaded[b.par], (b.pair + 1) * Q_LOADS)
                if h % 4 == 0:
                    pe.wait_ge(k_ready, b.n * NK + k_before(NEED_K[h // 4]) + 1)
                wait(pe, exp_done, b.n * HEADS + h - 1)
                for n in range(2):
                    at0 = (2 * (h % 2) + n) * BANK
                    m0 = n * (MH - 1)
                    for hl in range(2):
                        last = nc.tensor.matmul(ps[0:N, at0:at0 + SW], qm[b.par][:, hl, h, :],
                                                kt[b.par][:, h // 2, m0:m0 + SW], start=hl == HI, stop=hl == LO)
                last.then_inc(scores_done, 1)

            def turn(b, h, fills):
                g = b.n * HEADS + h
                pe.wait_ge(exp_done, g + 1)
                bank_free(g, fills)
                for n in range(2):
                    for t in range(TB * n, TB * (n + 1)):
                        at0 = N * (t - TB * n)
                        last = nc.tensor.transpose(tp[n][0:rows_of(t), at0:at0 + N], pr[:, h % 4, P * t:P * t + rows_of(t)],
                                                   keep.ident[0:N, 0:N])
                last.then_inc(p_turned, 1)

            def values(b, q):
                quad = b.n * QUADS + q
                for n in range(2):
                    pe.wait_ge(pT_ready[n], (quad + 1) * 4)
                if q == 0:
                    pe.wait_ge(v_ready, (b.n + 1) * NV)
                wait(pe, at_ready, quad)
                for t in range(MT):
                    for j in range(4):
                        h = 4 * q + j
                        nc.tensor.matmul(av[DH * j:DH * (j + 1), 0:N], vn[b.par][0:rows_of(t), t, DH * h:DH * (h + 1)],
                                         pT[0:rows_of(t), q % 2, j, t, :], start=t == 0, stop=t == MT - 1)
                pe.wait_ge(rexp_ready, quad + 1)
                nc.tensor.matmul(av[:, P:P + N], rexp[:, q % 2].rearrange("n j d -> n (j d)"), keep.ident[0:N, 0:N],
                                 start=True, stop=True).then_inc(av_done, 1)

            def batch(b, first=False, last=False):
                fills = (b.n + 1) * FILLS
                for h in range(HEADS):
                    score(b, h)
                    if h > 0:
                        turn(b, h - 1, fills + (0 if last else min(h, FILLS)))
                    elif not first:
                        turn(b.prev(), HEADS - 1, fills)
                    if not last:
                        if h < FILLS:
                            fill(b.next(), h, b.n * HEADS + h)
                        for n in by_slot[h]:
                            project(b.next(), n)
                    if h % 4 == 1 and h > 1:
                        values(b, h // 4 - 1)
                    elif h == 1 and not first:
                        values(b.prev(), QUADS - 1)

            for k in range(FILLS):
                fill(Batch(0, 0), k, 0)
            for n in range(NSTEP):
                project(Batch(0, 0), n)
            all_batches(pe, batch)
            end = Batch(B // 2 - 1, 1)
            turn(end, HEADS - 1, B * FILLS)
            values(end, QUADS - 1)

        @block.scalar
        def _(act):
            def fill_hi(b, k):
                for n, (m0, cols) in enumerate(SPLIT):
                    act.wait_ge(filled, b.n * 2 * FILLS + 2 * k + n + 1)
                    wait(act, proj_done, b.n * NSTEP)
                    nc.scalar.activation(cT[:, HI, k, m0:m0 + cols], tp[n][:, 0:cols], ACT.Copy).then_inc(cT_hi, 1)

            def key_hi(b, n):
                kind, i, half = STEPS[n]
                if kind != "k":
                    return
                m0, cols = SPLIT[half]
                act.wait_ge(proj_done, b.n * NSTEP + n + 1)
                for r in range(2):
                    nc.scalar.activation(kt[b.par][0:64, 2 * i + r, m0:m0 + cols], pj[64 * r:64 * r + 64, 0:cols],
                                         ACT.Identity, bias=keep.bk0[64 * r:64 * r + 64, i:i + 1]).then_inc(k_hi, 1)

            def turned(b, h):
                act.wait_ge(p_turned, b.n * HEADS + h + 1)
                if h % 4 == 0:
                    wait(act, av_done, b.n * QUADS + h // 4 - 1)
                nc.scalar.activation(pT[:, (h // 4) % 2, h % 4, TB:MT, :],
                                     tp[1][:, 0:TB * N].rearrange("p (t n) -> p t n", n=N), ACT.Copy).then_inc(pT_ready[1], 1)

            def exp(b, h):
                g = b.n * HEADS + h
                act.wait_ge(max_ready, g + 1)
                wait(act, p_turned, g - 3)
                nc.scalar.activation(pr[:, h % 4, :].rearrange("n (c m) -> n c m", c=2), scores(h % 2), ACT.Exp,
                                     bias=nmax[:, b.par, h:h + 1], accum_out=sums[:, b.par, h:h + 1]).then_inc(exp_done, 1)

            def spread(b, q):
                quad = b.n * QUADS + q
                act.wait_ge(av_done, quad + 1)
                wait(act, at_ready, quad - 1)
                nc.scalar.activation(rb[:, q % 2, :], av[:, P:P + N], ACT.Copy).then_inc(rb_ready, 1)

            def batch(b, first=False, last=False):
                for h in range(HEADS):
                    if h > 0:
                        turned(b, h - 1)
                    elif not first:
                        turned(b.prev(), HEADS - 1)
                    exp(b, h)
                    if not last:
                        if h < FILLS:
                            fill_hi(b.next(), h)
                        for n in by_slot[h]:
                            key_hi(b.next(), n)
                    if h % 4 == 1 and h > 1:
                        spread(b, h // 4 - 1)
                    elif h == 1 and not first:
                        spread(b.prev(), QUADS - 1)

            for k in range(FILLS):
                fill_hi(Batch(0, 0), k)
            for n in range(NSTEP):
                key_hi(Batch(0, 0), n)
            all_batches(act, batch)
            end = Batch(B // 2 - 1, 1)
            turned(end, HEADS - 1)
            spread(end, QUADS - 1)

        @block.vector
        def _(dve):
            def fill_lo(b, k):
                for n, (m0, cols) in enumerate(SPLIT):
                    dve.wait_ge(cT_hi, b.n * 2 * FILLS + 2 * k + n + 1)
                    nc.vector.tensor_tensor(cT[:, LO, k, m0:m0 + cols], tp[n][:, 0:cols],
                                            cT[:, HI, k, m0:m0 + cols].bitcast(F32), ALU.subtract).then_inc(cT_lo, 1)

            def project_out(b, n):
                kind, i, half = STEPS[n]
                if kind == "v":
                    dve.wait_ge(proj_done, b.n * NSTEP + n + 1)
                    nc.vector.tensor_copy(vn[b.par][0:rows_of(i), i, :], pj[0:rows_of(i), :]).then_inc(v_ready, 1)
                    return
                m0, cols = SPLIT[half]
                for r in range(2):
                    dve.wait_ge(k_hi, (b.n * NK + k_before(n)) * 2 + r + 1)
                    last = nc.vector.scalar_tensor_tensor(
                        out=kt[b.par][64:P, 2 * i + r, m0:m0 + cols], in0=pj[64 * r:64 * r + 64, 0:cols],
                        scalar=keep.bk0[64 * r:64 * r + 64, i:i + 1],
                        in1=kt[b.par][0:64, 2 * i + r, m0:m0 + cols].bitcast(F32), op0=ALU.add, op1=ALU.subtract)
                last.then_inc(k_ready, 1)

            def row_max(b, h):
                dve.wait_ge(scores_done, b.n * HEADS + h + 1)
                nc.vector.tensor_reduce(nmax[:, b.par, h:h + 1], scores(h % 2), AX.XY, ALU.max, negate=True).then_inc(max_ready, 1)

            def turned(b, h):
                dve.wait_ge(p_turned, b.n * HEADS + h + 1)
                if h % 4 == 0:
                    wait(dve, av_done, b.n * QUADS + h // 4 - 1)
                nc.vector.tensor_copy(pT[:, (h // 4) % 2, h % 4, 0:TB, :],
                                      tp[0][:, 0:TB * N].rearrange("p (t n) -> p t n", n=N)).then_inc(pT_ready[0], 1)

            def inverse(b, q):
                quad = b.n * QUADS + q
                dve.wait_ge(exp_done, (quad + 1) * 4)
                wait(dve, av_done, quad - 1)
                nc.vector.reciprocal(rexp[:, q % 2], sums[:, b.par, 4 * q:4 * q + 4].unsqueeze(2).to_broadcast([N, 4, DH])).then_inc(rexp_ready, 1)

            def scale(b, q):
                quad = b.n * QUADS + q
                dve.wait_ge(rb_ready, quad + 1)
                if q == 0:
                    wait(dve, stored[b.par], b.pair * 16)
                nc.vector.tensor_tensor(at[:, b.par, q, :], av[:, 0:N], rb[:, q % 2, :], ALU.mult).then_inc(at_ready, 1)

            def batch(b, first=False, last=False):
                for h in range(HEADS):
                    row_max(b, h)
                    if h > 0:
                        turned(b, h - 1)
                    elif not first:
                        turned(b.prev(), HEADS - 1)
                    if h % 4 == 1 and h > 1:
                        inverse(b, h // 4 - 1)
                    elif h == 1 and not first:
                        inverse(b.prev(), QUADS - 1)
                    if not last:
                        if h < FILLS:
                            fill_lo(b.next(), h)
                        for n in by_slot[h]:
                            project_out(b.next(), n)
                    if h % 4 == 1 and h > 1:
                        scale(b, h // 4 - 1)
                    elif h == 1 and not first:
                        scale(b.prev(), QUADS - 1)

            for k in range(FILLS):
                fill_lo(Batch(0, 0), k)
            for n in range(NSTEP):
                project_out(Batch(0, 0), n)
            all_batches(dve, batch)
            end = Batch(B // 2 - 1, 1)
            turned(end, HEADS - 1)
            inverse(end, QUADS - 1)
            scale(end, QUADS - 1)


def tokens_phase(nc, d, io, keep):
    D, T, F = d.D, d.T, d.F
    DC, TC, FC = D // P, T // P, F // P
    TG = 5
    TOK = TG * P
    GROUPS = d.B * d.N // TOK
    HALF = TOK // 2
    assert GROUPS * TOK == d.B * d.N and HALF <= BANK
    RB = 3
    USES = ([("rows", i) for i in range(TG)] + [("up", n) for n in range(2 * FC)] + [("proj", i) for i in range(TG)]
            + [("qrows", i) for i in range(TG)] + [("query", n) for n in range(2 * TC)])

    def bank_of(use):
        return USES.index(use) % RB

    with ExitStack() as ctx:
        s = Scope(nc, ctx)
        wo, w2 = s.sb("t_wo", [P, 2, DC, D], F32R), s.sb("t_w2", [P, 2, FC, D], F32R)
        aw, w1 = s.sb("t_aw", [P, 2, DC, T], F32R), s.sb("t_w1", [P, 2, 2, DC, P], F32R)
        b2_row = s.sb("t_b2_row", [P, D])
        zn = s.sb("t_zn", [P, TG * D])
        at_in = zn[:].rearrange("p (c n) -> p c n", c=DC)
        z = zn[:].rearrange("p (i n) -> p i n", i=TG)
        wide = s.sb("t_wide", [P, 2, DC, TOK], F32R)
        zT = s.sb("t_zT", [P, 2, DC, TOK], F32R)
        xb, ob = s.sb("t_xb", [P, TG, D]), s.sb("t_ob", [P, TG, D])
        h32, h_hl = s.sb("t_h32", [P, 2, HALF]), s.sb("t_h_hl", [P, 2, 2, TOK], F32R)
        junk = s.sb("t_junk", [P, D])
        st_h, st_q = s.sb("t_st_h", [P, TG, 6]), s.sb("t_st_q", [P, TG, 6])
        mv_h, mv_q = s.sb("t_mv_h", [P, TG, 2]), s.sb("t_mv_q", [P, TG, 2])
        ve_h, ve_q = s.sb("t_ve_h", [P, TG]), s.sb("t_ve_q", [P, TG])
        rs_h, rs_q = s.sb("t_rs_h", [P, TG]), s.sb("t_rs_q", [P, TG])
        cs = s.sb("t_cs", [P, TG])
        acc = [s.psum(f"t_acc{i}", [P, BANK]) for i in range(TG)]
        ring = [s.psum(f"t_ring{i}", [P, BANK]) for i in range(RB)]

        passed = s.sem("t_passed")
        wo_loaded, aw_loaded, w2_loaded = s.sem("t_wo_loaded"), s.sem("t_aw_loaded"), s.sem("t_w2_loaded")
        b2_loaded, w1_loaded, at_loaded, x_loaded = s.sem("t_b2_loaded"), s.sems("t_w1_loaded", 2), s.sem("t_at_loaded"), s.sem("t_x_loaded")
        t_stored, x_stored, c_stored = s.sem("t_t_stored"), s.sem("t_x_stored"), s.sem("t_c_stored")
        rows_done, up_done, proj_done, qrows_done, query_done, down_done = (
            s.sem(f"t_{n}_done") for n in ("rows", "up", "proj", "qrows", "query", "down"))
        at_hi, at_lo, zT_hi, gelu_done, h_hi, h_lo, t_hi = (
            s.sem(f"t_{n}") for n in ("at_hi", "at_lo", "zT_hi", "gelu_done", "h_hi", "h_lo", "t_hi"))
        zT_lo, t_lo = s.sem("t_zT_lo"), s.sem("t_t_lo")
        o_ready, x1_ready, st_h_ready, st_q_ready, mv_h_ready, mv_q_ready = (
            s.sem(f"t_{n}_ready") for n in ("o", "x1", "st_h", "st_q", "mv_h", "mv_q"))
        ve_h_ready, ve_q_ready, rs_h_ready, rs_q_ready = (s.sem(f"t_{n}_ready") for n in ("ve_h", "ve_q", "rs_h", "rs_q"))
        zh_ready, zq_ready, c_ready, xb_ready, xo_ready, x1b_ready = (
            s.sem(f"t_{n}_ready") for n in ("zh", "zq", "c", "xb", "xo", "x1b"))
        block = ctx.enter_context(nc.Block())

        def all_groups(eng, group):
            group(0)
            with eng.Fori(1, GROUPS - 1) as g:
                group(g)
            group(GROUPS - 1, last=True)

        def tile(ap, i):
            return ap[:, P * i:P * (i + 1)]

        @block.sync
        def _(sp):
            def load_at(g):
                wait(sp, rows_done, g * TG)
                sp.dma_start(at_in, keep.attn_dram[:, bass.ds(g * TOK, TOK)].rearrange("(c p) n -> p c n", p=P)).then_inc(at_loaded, 16)

            def load_w1(g, j):
                wait(sp, up_done, g * 2 * FC + 2 * (j - 1))
                sp.dma_start(w1[:, j % 2].bitcast(F32), keep.W1_dram[j]).then_inc(w1_loaded[j % 2], 16)

            def group(g, last=False):
                wait(sp, x_stored, g * 16)
                rows = io.x.rearrange("b n d -> (b n) d")[bass.ds(g * TOK, TOK), :]
                sp.dma_start(xb[:], rows.rearrange("(i p) d -> p i d", p=P)).then_inc(x_loaded, 16)
                if not last:
                    load_at(g + 1)
                for j in range(2, FC):
                    load_w1(g, j)
                if not last:
                    for j in range(2):
                        load_w1(g + 1, j)
                sp.wait_ge(x1b_ready, (g + 1) * TG)
                sp.dma_start(keep.x1_dram[bass.ds(g * TOK, TOK), :].rearrange("(i p) d -> p i d", p=P), xb[:]).then_inc(x_stored, 16)
                wait_alone(sp, c_ready, (g + 1) * TG, passed)
                sp.dma_start(keep.c_dram[bass.ds(g * TOK, TOK), :].rearrange("(i p) o -> p (i o)", p=P), cs[:],
                             allow_slow_non_contiguous=True).then_inc(c_stored, 16)
                sp.wait_ge(t_hi, (g + 1) * 2 * TC)
                sp.wait_ge(t_lo, (g + 1) * 2 * TC)
                for hl in range(2):
                    sp.dma_start(keep.t_dram[hl, :, bass.ds(g * TOK, TOK)].rearrange("(c p) n -> p c n", p=P),
                                 wide[:, hl, 0:TC, :].bitcast(F32)).then_inc(t_stored, 16)

            load_at(0)
            sp.dma_start(wo[:].bitcast(F32), keep.Wo_dram.rearrange("h (c p) n -> p h c n", p=P)).then_inc(wo_loaded, 16)
            for j in range(2):
                load_w1(0, j)
            sp.dma_start(b2_row[:], row(io.b2)).then_inc(b2_loaded, 16)
            sp.dma_start(w2[:].bitcast(F32), keep.W2_dram.rearrange("h (c p) n -> p h c n", p=P)).then_inc(w2_loaded, 16)
            sp.dma_start(aw[:].bitcast(F32), keep.A_dram.rearrange("h (c p) n -> p h c n", p=P)).then_inc(aw_loaded, 16)
            all_groups(sp, group)
            sp.wait_ge(x_stored, 16 * GROUPS)
            sp.wait_ge(c_stored, 16 * GROUPS)
            sp.wait_ge(t_stored, 32 * GROUPS)

        @block.tensor
        def _(pe):
            def bank(g, use, last):
                left = {"rows": (zT_lo, 2 * TG, 1), "up": (gelu_done, 2 * FC, 1), "proj": (o_ready, TG, TG + 1),
                        "qrows": (zT_lo, 2 * TG, TG + 1), "query": (t_lo, 2 * TC, 1)}
                before = [v for v in USES[bank_of(use):USES.index(use):RB] if not (last and v[0] == "proj")]
                if before:
                    kind, n = before[-1]
                    sem, per_group, start = left[kind]
                    pe.wait_ge(sem, g * per_group + start + n)
                else:
                    wait(pe, t_lo, g * 2 * TC)
                return ring[bank_of(use)]

            def project(g, i, first=False):
                if first:
                    wait(pe, o_ready, i - RB + 1)
                out = ring[bank_of(("proj", i))] if first else bank(g, ("proj", i), False)
                for k in range(DC):
                    for x, y in PASSES:
                        last = nc.tensor.matmul(out[:, 0:D], tile(wide[:, x, k, :], i), wo[:, y, k, :],
                                                start=(k, x, y) == (0, HI, HI), stop=(k, x, y) == (DC - 1, LO, HI))
                last.then_inc(proj_done, 1)

            def turn(out, i, done):
                for k in range(DC):
                    last = nc.tensor.transpose(tile(out, k), tile(z[:, i, :], k), keep.ident[:])
                last.then_inc(done, 1)

            def up(g, n, last):
                j, half = n // 2, n % 2
                if half == 0:
                    pe.wait_ge(w1_loaded[j % 2], (g * (FC // 2) + j // 2 + 1) * 16)
                out = bank(g, ("up", n), last)
                for k in range(DC):
                    for x, y in PASSES:
                        ins = nc.tensor.matmul(out[:, 0:HALF], w1[:, j % 2, x, k, :], zT[:, y, k, HALF * half:HALF * (half + 1)],
                                               start=(k, x, y) == (0, HI, HI), stop=(k, x, y) == (DC - 1, LO, HI))
                ins.then_inc(up_done, 1)

            def down(g, j):
                pe.wait_ge(h_lo, g * 2 * FC + 2 * (j + 1))
                pe.wait_ge(h_hi, g * 2 * FC + 2 * (j + 1))
                for i in range(TG):
                    for x, y in PASSES:
                        ins = nc.tensor.matmul(acc[i][:, 0:D], tile(h_hl[:, j % 2, x, :], i), w2[:, y, j, :],
                                               start=(j, x, y) == (0, HI, HI), stop=(j, x, y) == (FC - 1, LO, HI))
                ins.then_inc(down_done, 1)

            def group(g, last=False):
                for i in range(TG):
                    pe.wait_ge(zh_ready, g * TG + i + 1)
                    turn(bank(g, ("rows", i), last), i, rows_done)
                pe.wait_ge(zT_lo, g * 2 * TG + TG)
                wait(pe, x1_ready, g * TG)
                for j in range(FC):
                    for half in range(2):
                        up(g, 2 * j + half, last)
                    if j > 0:
                        down(g, j - 1)
                down(g, FC - 1)
                if not last:
                    pe.wait_ge(at_lo, (g + 2) * DC)
                    for i in range(TG):
                        project(g, i)
                for i in range(TG):
                    pe.wait_ge(zq_ready, g * TG + i + 1)
                    turn(bank(g, ("qrows", i), last), i, qrows_done)
                pe.wait_ge(zT_lo, (g + 1) * 2 * TG)
                for n in range(2 * TC):
                    c, half = n // 2, n % 2
                    out = bank(g, ("query", n), last)
                    for k in range(DC):
                        for x, y in PASSES:
                            ins = nc.tensor.matmul(out[:, 0:HALF], tile(aw[:, x, k, :], c), zT[:, y, k, HALF * half:HALF * (half + 1)],
                                                   start=(k, x, y) == (0, HI, HI), stop=(k, x, y) == (DC - 1, LO, HI))
                    ins.then_inc(query_done, 1)

            pe.wait_ge(wo_loaded, 16)
            pe.wait_ge(at_lo, DC)
            for i in range(TG):
                project(0, i, first=True)
            pe.wait_ge(w2_loaded, 16)
            pe.wait_ge(aw_loaded, 16)
            all_groups(pe, group)

        @block.scalar
        def _(act):
            def attn_hi(g, k):
                act.wait_ge(at_loaded, (g + 1) * 16)
                wait(act, t_stored, (g - 1) * 32)
                nc.scalar.activation(wide[:, HI, k, :], at_in[:, k, :], ACT.Copy).then_inc(at_hi, 1)

            def rows_hi(use, done, count):
                act.wait_ge(done, count)
                nc.scalar.activation(zT[:, HI, :, P * use[1]:P * (use[1] + 1)],
                                     ring[bank_of(use)][:].rearrange("p (c n) -> p c n", c=DC), ACT.Copy).then_inc(zT_hi, 1)

            def gelu(g, n):
                j, half = n // 2, n % 2
                b = bank_of(("up", n))
                act.wait_ge(up_done, g * 2 * FC + n + 1)
                wait(act, h_lo, g * 2 * FC + n - 1)
                nc.scalar.activation(h32[:, half, :], ring[b][:, 0:HALF], ACT.Gelu, bias=keep.b1[:, j:j + 1]).then_inc(gelu_done, 1)
                act.wait_ge(gelu_done, g * 2 * FC + n + 1)
                wait(act, down_done, g * FC + j - 1)
                nc.scalar.activation(h_hl[:, j % 2, HI, HALF * half:HALF * (half + 1)], h32[:, half, :], ACT.Copy).then_inc(h_hi, 1)

            def group(g, last=False):
                for i in range(TG):
                    rows_hi(("rows", i), rows_done, g * TG + i + 1)
                for n in range(2 * FC):
                    gelu(g, n)
                    if not last and n % 4 == 3 and n // 4 >= 4:
                        attn_hi(g + 1, n // 4 - 4)
                for i in range(TG):
                    rows_hi(("qrows", i), qrows_done, g * TG + i + 1)
                for n in range(2 * TC):
                    c, half = n // 2, n % 2
                    act.wait_ge(query_done, g * 2 * TC + n + 1)
                    nc.scalar.activation(wide[:, HI, c, HALF * half:HALF * (half + 1)], ring[bank_of(("query", n))][:, 0:HALF],
                                         ACT.Identity, bias=keep.t_bias[:, c:c + 1]).then_inc(t_hi, 1)

            for k in range(DC):
                attn_hi(0, k)
            all_groups(act, group)

        @block.vector
        def _(dve):
            def attn_lo(g, k):
                dve.wait_ge(at_hi, g * DC + k + 1)
                nc.vector.tensor_tensor(wide[:, LO, k, :], at_in[:, k, :], wide[:, HI, k, :].bitcast(F32), ALU.subtract).then_inc(at_lo, 1)

            def normalise_stats(src, i, st, mv, st_ready, mv_ready, count):
                nc.vector.bn_stats(st[:, i, :], src).then_inc(st_ready, 1)
                wait_alone(dve, st_ready, count, passed)
                nc.vector.bn_aggr(mv[:, i, :], st[:, i, :]).then_inc(mv_ready, 1)

            def rows_out(g, i):
                b = bank_of(("proj", i))
                dve.wait_ge(proj_done, g * TG + i + 1)
                wait(dve, xo_ready, g * TG)
                nc.vector.tensor_tensor(ob[:, i, :], ring[b][:, 0:D], keep.bo_row[:], ALU.add).then_inc(o_ready, 1)
                dve.wait_ge(o_ready, g * TG + i + 1)
                normalise_stats(ob[:, i, :], i, st_h, mv_h, st_h_ready, mv_h_ready, g * TG + i + 1)

            def norm(out, src, i, mv, rs, rs_ready, count, ready):
                dve.wait_ge(rs_ready, count)
                nc.vector.tensor_scalar(out, src, mv[:, i, 0:1], rs[:, i:i + 1], ALU.subtract, ALU.mult).then_inc(ready, 1)

            def rows_lo(use, hi_count):
                dve.wait_ge(zT_hi, hi_count)
                nc.vector.tensor_tensor(zT[:, LO, :, P * use[1]:P * (use[1] + 1)],
                                        ring[bank_of(use)][:].rearrange("p (c n) -> p c n", c=DC),
                                        zT[:, HI, :, P * use[1]:P * (use[1] + 1)].bitcast(F32), ALU.subtract).then_inc(zT_lo, 1)

            def norm_h(g, i):
                norm(z[:, i, :], ob[:, i, :], i, mv_h, rs_h, rs_h_ready, g * TG + i + 1, zh_ready)

            def x1_out(g, i):
                nc.vector.tensor_tensor(xb[:, i, :], acc[i][:, 0:D], xb[:, i, :], ALU.add).then_inc(x1_ready, 1)
                dve.wait_ge(x1_ready, g * TG + i + 1)
                normalise_stats(xb[:, i, :], i, st_q, mv_q, st_q_ready, mv_q_ready, g * TG + i + 1)

            def group(g, last=False):
                for i in range(TG):
                    rows_lo(("rows", i), g * 2 * TG + i + 1)
                for n in range(2 * FC):
                    j, half = n // 2, n % 2
                    dve.wait_ge(h_hi, g * 2 * FC + n + 1)
                    part = slice(HALF * half, HALF * (half + 1))
                    nc.vector.tensor_tensor(h_hl[:, j % 2, LO, part], h32[:, half, :], h_hl[:, j % 2, HI, part].bitcast(F32),
                                            ALU.subtract).then_inc(h_lo, 1)
                    if not last and n % 4 == 3 and n // 4 >= 4:
                        attn_lo(g + 1, n // 4 - 4)
                dve.wait_ge(down_done, (g + 1) * FC)
                dve.wait_ge(xo_ready, (g + 1) * TG)
                for i in range(TG + 1):
                    if i < TG:
                        x1_out(g, i)
                        if not last:
                            rows_out(g + 1, i)
                    if i > 0:
                        norm(z[:, i - 1, :], xb[:, i - 1, :], i - 1, mv_q, rs_q, rs_q_ready, g * TG + i, zq_ready)
                wait(dve, c_stored, g * 16)
                for i in range(TG):
                    if i == 0:
                        dve.wait_ge(zq_ready, (g + 1) * TG)
                    rows_lo(("qrows", i), g * 2 * TG + TG + i + 1)
                    wait(dve, c_ready, g * TG + i)
                    nc.vector.tensor_tensor_reduce(out=junk[:], in0=z[:, i, :], in1=keep.score_row[:], scale=1.0,
                                                   scalar=keep.score_const[:], op0=ALU.mult, op1=ALU.add,
                                                   accum_out=cs[:, i:i + 1]).then_inc(c_ready, 1)
                    if not last:
                        dve.wait_ge(c_ready, g * TG + i + 1)
                        norm_h(g + 1, i)
                for n in range(2 * TC):
                    c, half = n // 2, n % 2
                    part = slice(HALF * half, HALF * (half + 1))
                    dve.wait_ge(t_hi, g * 2 * TC + n + 1)
                    nc.vector.scalar_tensor_tensor(out=wide[:, LO, c, part], in0=ring[bank_of(("query", n))][:, 0:HALF],
                                                   scalar=keep.t_bias[:, c:c + 1], in1=wide[:, HI, c, part].bitcast(F32),
                                                   op0=ALU.add, op1=ALU.subtract).then_inc(t_lo, 1)

            for k in range(DC):
                attn_lo(0, k)
            for i in range(TG):
                rows_out(0, i)
            dve.wait_ge(at_lo, DC)
            for i in range(TG):
                norm_h(0, i)
            all_groups(dve, group)

        @block.gpsimd
        def _(pool):
            def inverse_std(mv, ve, rs, i, mv_ready, ve_ready, rs_ready, count):
                wait_alone(pool, mv_ready, count, passed)
                nc.gpsimd.tensor_scalar(ve[:, i:i + 1], mv[:, i, 1:2], EPS, 1.0, ALU.add, ALU.mult).then_inc(ve_ready, 1)
                pool.wait_ge(ve_ready, count)
                nc.gpsimd.tensor_tensor(rs[:, i:i + 1], ve[:, i:i + 1], keep.minus_half[:, 0:1], ALU.pow).then_inc(rs_ready, 1)

            def group(g, last=False):
                pool.wait_ge(x_loaded, (g + 1) * 16)
                for i in range(TG):
                    nc.gpsimd.tensor_tensor(xb[:, i, :], xb[:, i, :], b2_row[:], ALU.add).then_inc(xb_ready, 1)
                for i in range(TG):
                    pool.wait_ge(xb_ready, g * TG + i + 1)
                    pool.wait_ge(o_ready, g * TG + i + 1)
                    nc.gpsimd.tensor_tensor(xb[:, i, :], xb[:, i, :], ob[:, i, :], ALU.add).then_inc(xo_ready, 1)
                for i in range(TG):
                    inverse_std(mv_q, ve_q, rs_q, i, mv_q_ready, ve_q_ready, rs_q_ready, g * TG + i + 1)
                    if not last:
                        inverse_std(mv_h, ve_h, rs_h, i, mv_h_ready, ve_h_ready, rs_h_ready, (g + 1) * TG + i + 1)
                for i in range(TG):
                    pool.wait_ge(zq_ready, g * TG + i + 1)
                    nc.gpsimd.tensor_tensor(xb[:, i, :], xb[:, i, :], keep.bd_row[:], ALU.add).then_inc(x1b_ready, 1)

            pool.wait_ge(b2_loaded, 16)
            for i in range(TG):
                inverse_std(mv_h, ve_h, rs_h, i, mv_h_ready, ve_h_ready, rs_h_ready, i + 1)
            all_groups(pool, group)


def attention1_phase(nc, d, io, keep):
    B, N, M, T, E = d.B, d.N, d.M, d.T, d.E
    TC = T // P
    MT = -(-M // P)
    LAST = M - P * (MT - 1)
    TB = MT // 2
    SPLIT = ((0, TB * P), (TB * P, M - TB * P))
    MH = M // 2
    SW = MH + 1
    FILLS = 2 * TC

    def rows_of(t):
        return LAST if t == MT - 1 else P

    with ExitStack() as ctx:
        s = Scope(nc, ctx)
        bw = s.sb("b_bw", [P, 2, TC, E], F32R)
        cn = [s.sb(f"b_cn{i}", [P, MT, T]) for i in range(2)]
        xk = [s.sb(f"b_xk{i}", [P, MT, T]) for i in range(2)]
        xT = [s.sb(f"b_xT{i}", [P, 2, TC, M], F32R) for i in range(2)]
        tq = [s.sb(f"b_tq{i}", [P, 2, TC, N], F32R) for i in range(2)]
        cst, x1 = s.sb("b_cst", [N, 2]), s.sb("b_x1", [N, 2, E])
        st, mv = s.sb("b_st", [P, 2, MT, 6]), s.sb("b_mv", [P, 2, MT, 2])
        ve, rs = s.sb("b_ve", [P, 2, MT]), s.sb("b_rs", [P, 2, MT])
        nmax, bias, sums, inv = (s.sb(f"b_{n}", [N, 2]) for n in ("nmax", "bias", "sums", "inv"))
        pr, pT = s.sb("b_pr", [N, 2, M]), s.sb("b_pT", [P, 2, MT, N])
        uT = s.sb("b_uT", [P, 2, 2, TC * N], F32R)
        y, out = s.sb("b_y", [N, 2, E]), s.sb("b_out", [N, 2, E])
        sc = s.psum("b_sc", [P, 3 * BANK])
        tp = [s.psum(f"b_tp{i}", [P, BANK]) for i in range(2)]
        tt = [s.psum(f"b_tt{i}", [P, BANK]) for i in range(2)]
        ff = s.psum("b_ff", [P, BANK])
        uu = sc[:, 2 * BANK:3 * BANK]
        scores = sc[0:N, 0:2 * (BANK + 1)].rearrange("p (c n) -> p c n", c=2)[:, :, 0:MH]

        passed = s.sem("b_passed")
        b_loaded, ctx_loaded, t_loaded = s.sem("b_b_loaded"), s.sems("b_ctx_loaded", 2), s.sems("b_t_loaded", 2)
        x1_loaded, out_stored = s.sems("b_x1_loaded", 2), s.sems("b_out_stored", 2)
        zeroed, tail_zeroed = s.sem("b_zeroed"), s.sem("b_tail_zeroed")
        st_ready, mv_ready, ve_ready, rs_ready, xk_ready = (s.sem(f"b_{n}_ready") for n in ("st", "mv", "ve", "rs", "xk"))
        filled, xT_hi, xT_lo = s.sem("b_filled"), s.sem("b_xT_hi"), s.sem("b_xT_lo")
        scores_done, max_ready, bias_ready, exp_done = (s.sem(f"b_{n}") for n in ("scores_done", "max_ready", "bias_ready", "exp_done"))
        part_ready, inv_ready = s.sem("b_part_ready"), s.sem("b_inv_ready")
        p_turned, pT_ready = s.sem("b_p_turned"), s.sems("b_pT_ready", 2)
        values_done, uT_hi, uT_lo = s.sem("b_values_done"), s.sem("b_uT_hi"), s.sem("b_uT_lo")
        final_done, y_ready, out_ready = s.sem("b_final_done"), s.sem("b_y_ready"), s.sem("b_out_ready")
        block = ctx.enter_context(nc.Block())

        def all_batches(eng, batch):
            batch(Batch(0, 0), first=True)
            batch(Batch(0, 1))
            with eng.Fori(1, B // 2 - 1) as pair:
                batch(Batch(pair, 0))
                batch(Batch(pair, 1))
            batch(Batch(B // 2 - 1, 0))
            batch(Batch(B // 2 - 1, 1), last=True)

        def exists(b):
            return not isinstance(b.n, int) or b.n < B

        @block.sync
        def _(sp):
            def load_ctx(b):
                wait(sp, xk_ready, (b.n - 1) * MT)
                src = io.ctx[bass.ds(b.n, 1), :, :].rearrange("b m t -> (b m) t")
                whole = P * (MT - 1)
                sp.dma_start(cn[b.par][:, 0:MT - 1, :], src[0:whole, :].rearrange("(t p) d -> p t d", p=P)).then_inc(ctx_loaded[b.par], 16)
                sp.dma_start(cn[b.par][0:LAST, MT - 1, :], src[whole:M, :]).then_inc(ctx_loaded[b.par], 16)

            def load_rows(b):
                wait(sp, scores_done, b.n - 1)
                for hl in range(2):
                    sp.dma_start(tq[b.par][:, hl].bitcast(F32),
                                 keep.t_dram[hl, :, bass.ds(b.n * N, N)].rearrange("(c p) n -> p c n", p=P)).then_inc(t_loaded[b.par], 16)
                wait(sp, bias_ready, b.n - 1)
                sp.dma_start(cst[:, b.par:b.par + 1], keep.c_dram[bass.ds(b.n * N, N), :],
                             allow_slow_non_contiguous=True).then_inc(t_loaded[b.par], 16)
                wait(sp, out_ready, b.n - 1)
                sp.dma_start(x1[:, b.par, :], keep.x1_dram[bass.ds(b.n * N, N), :]).then_inc(x1_loaded[b.par], 16)

            def store(b):
                sp.wait_ge(out_ready, b.n + 1)
                sp.dma_start(io.out.rearrange("b n d -> (b n) d")[bass.ds(b.n * N, N), :], out[:, b.par, :]).then_inc(out_stored[b.par], 16)

            def batch(b, first=False, last=False):
                if exists(b.next().next()):
                    load_ctx(b.next().next())
                if not last:
                    load_rows(b.next())
                if not first:
                    store(b.prev())

            load_ctx(Batch(0, 0))
            load_rows(Batch(0, 0))
            load_ctx(Batch(0, 1))
            sp.dma_start(bw[:].bitcast(F32), keep.B_dram.rearrange("h (c p) n -> p h c n", p=P)).then_inc(b_loaded, 16)
            all_batches(sp, batch)
            store(Batch(B // 2 - 1, 1))
            for par in range(2):
                sp.wait_ge(out_stored[par], 16 * (B // 2))

        @block.gpsimd
        def _(pool):
            def inverse_std(b):
                wait_alone(pool, mv_ready, (b.n + 1) * MT, passed)
                nc.gpsimd.tensor_scalar(ve[:, b.par, :], mv[:, b.par, :, 1], EPS, 1.0, ALU.add, ALU.mult).then_inc(ve_ready, 1)
                pool.wait_ge(ve_ready, b.n + 1)
                nc.gpsimd.tensor_tensor(rs[:, b.par, :], ve[:, b.par, :], keep.minus_half[:, 0:MT], ALU.pow).then_inc(rs_ready, 1)

            def add(b):
                pool.wait_ge(y_ready, b.n + 1)
                pool.wait_ge(x1_loaded[b.par], (b.pair + 1) * 16)
                wait(pool, out_stored[b.par], b.pair * 16)
                nc.gpsimd.tensor_tensor(out[:, b.par, :], y[:, b.par, :], x1[:, b.par, :], ALU.add).then_inc(out_ready, 1)

            def batch(b, first=False, last=False):
                if exists(b.next().next()):
                    inverse_std(b.next().next())
                if not first:
                    add(b.prev())

            nc.gpsimd.memset(mv[:], 1.0).then_inc(zeroed, 1)
            inverse_std(Batch(0, 0))
            inverse_std(Batch(0, 1))
            all_batches(pool, batch)
            add(Batch(B // 2 - 1, 1))

        @block.tensor
        def _(pe):
            def fill(b, k):
                if k == 0:
                    pe.wait_ge(xk_ready, (b.n + 1) * MT)
                for n in range(2):
                    wait(pe, xT_lo, b.n * FILLS + 2 * k + n - 1)
                    for t in range(TB * n, TB * (n + 1)):
                        at0, rows = P * (t - TB * n), rows_of(t)
                        last = nc.tensor.transpose(tp[n][:, at0:at0 + rows], xk[b.par][0:rows, t, P * k:P * (k + 1)],
                                                   keep.ident[0:rows, 0:rows])
                    last.then_inc(filled, 1)

            def score(b):
                pe.wait_ge(t_loaded[b.par], (b.pair + 1) * 48)
                pe.wait_ge(xT_lo, (b.n + 1) * FILLS)
                wait(pe, exp_done, b.n)
                for n in range(2):
                    m0 = n * (MH - 1)
                    for k in range(TC):
                        for x, y_ in PASSES:
                            last = nc.tensor.matmul(sc[0:N, n * BANK:n * BANK + SW], tq[b.par][:, x, k, :],
                                                    xT[b.par][:, y_, k, m0:m0 + SW],
                                                    start=(k, x, y_) == (0, HI, HI), stop=(k, x, y_) == (TC - 1, LO, HI))
                last.then_inc(scores_done, 1)

            def turn(b):
                pe.wait_ge(exp_done, b.n + 1)
                pe.wait_ge(tail_zeroed, 1)
                for n in range(2):
                    wait(pe, pT_ready[n], b.n)
                    for t in range(TB * n, TB * (n + 1)):
                        at0 = N * (t - TB * n)
                        last = nc.tensor.transpose(tt[n][0:rows_of(t), at0:at0 + N], pr[:, b.par, P * t:P * t + rows_of(t)],
                                                   keep.ident[0:N, 0:N])
                last.then_inc(p_turned, 1)

            def values(b):
                for n in range(2):
                    pe.wait_ge(pT_ready[n], b.n + 1)
                wait(pe, uT_lo, b.n)
                for k in range(TC):
                    for t in range(MT):
                        last = nc.tensor.matmul(uu[:, N * k:N * (k + 1)], xk[b.par][0:rows_of(t), t, P * k:P * (k + 1)],
                                                pT[0:rows_of(t), b.par, t, :], start=t == 0, stop=t == MT - 1)
                last.then_inc(values_done, 1)

            def final(b):
                pe.wait_ge(uT_lo, b.n + 1)
                wait(pe, y_ready, b.n)
                for k in range(TC):
                    for x, y_ in PASSES:
                        last = nc.tensor.matmul(ff[0:N, 0:E], uT[:, b.par, x, N * k:N * (k + 1)], bw[:, y_, k, :],
                                                start=(k, x, y_) == (0, HI, HI), stop=(k, x, y_) == (TC - 1, LO, HI))
                last.then_inc(final_done, 1)

            def batch(b, first=False, last=False):
                score(b)
                if not first:
                    final(b.prev())
                if not last:
                    for k in range(TC):
                        fill(b.next(), k)
                turn(b)
                values(b)

            pe.wait_ge(b_loaded, 16)
            for k in range(TC):
                fill(Batch(0, 0), k)
            all_batches(pe, batch)
            final(Batch(B // 2 - 1, 1))

        @block.scalar
        def _(act):
            def fill_hi(b, k):
                wait(act, scores_done, b.n - 1)
                for n, (m0, cols) in enumerate(SPLIT):
                    act.wait_ge(filled, b.n * FILLS + 2 * k + n + 1)
                    nc.scalar.activation(xT[b.par][:, HI, k, m0:m0 + cols], tp[n][:, 0:cols], ACT.Copy).then_inc(xT_hi, 1)

            def exp(b):
                act.wait_ge(bias_ready, b.n + 1)
                wait(act, p_turned, b.n - 1)
                nc.scalar.activation(pr[:, b.par, :].rearrange("n (c m) -> n c m", c=2), scores, ACT.Exp,
                                     bias=bias[:, b.par:b.par + 1], accum_out=sums[:, b.par:b.par + 1]).then_inc(exp_done, 1)

            def turned(b):
                act.wait_ge(p_turned, b.n + 1)
                for n in range(2):
                    nc.scalar.activation(pT[:, b.par, TB * n:TB * (n + 1), :],
                                         tt[n][:, 0:TB * N].rearrange("p (t n) -> p t n", n=N), ACT.Copy).then_inc(pT_ready[n], 1)

            def values_hi(b):
                act.wait_ge(values_done, b.n + 1)
                wait(act, final_done, b.n - 1)
                nc.scalar.activation(uT[:, b.par, HI, :], uu[:, 0:TC * N], ACT.Copy).then_inc(uT_hi, 1)

            def normalise(b):
                act.wait_ge(final_done, b.n + 1)
                act.wait_ge(inv_ready, b.n + 1)
                wait(act, out_ready, b.n - 1)
                nc.scalar.activation(y[:, b.par, :], ff[0:N, 0:E], ACT.Copy, scale=inv[:, b.par:b.par + 1]).then_inc(y_ready, 1)

            def batch(b, first=False, last=False):
                if not last:
                    fill_hi(b.next(), 0)
                exp(b)
                if not first:
                    normalise(b.prev())
                if not last:
                    for k in range(1, TC):
                        fill_hi(b.next(), k)
                turned(b)
                values_hi(b)

            for k in range(TC):
                fill_hi(Batch(0, 0), k)
            act.wait_ge(tail_zeroed, 1)
            all_batches(act, batch)
            normalise(Batch(B // 2 - 1, 1))

        @block.vector
        def _(dve):
            def stats(b):
                dve.wait_ge(ctx_loaded[b.par], (b.pair + 1) * 32)
                for t in range(MT):
                    nc.vector.bn_stats(st[0:rows_of(t), b.par, t, :], cn[b.par][0:rows_of(t), t, :]).then_inc(st_ready, 1)
                for t in range(MT):
                    wait_alone(dve, st_ready, b.n * MT + t + 1, passed)
                    nc.vector.bn_aggr(mv[0:rows_of(t), b.par, t, :], st[0:rows_of(t), b.par, t, :]).then_inc(mv_ready, 1)

            def normalise(b):
                dve.wait_ge(rs_ready, b.n + 1)
                for t in range(MT):
                    rows = rows_of(t)
                    nc.vector.tensor_scalar(xk[b.par][0:rows, t, :], cn[b.par][0:rows, t, :], mv[0:rows, b.par, t, 0:1],
                                            rs[0:rows, b.par, t:t + 1], ALU.subtract, ALU.mult).then_inc(xk_ready, 1)

            def fill_lo(b, k):
                for n, (m0, cols) in enumerate(SPLIT):
                    dve.wait_ge(xT_hi, b.n * FILLS + 2 * k + n + 1)
                    nc.vector.tensor_tensor(xT[b.par][:, LO, k, m0:m0 + cols], tp[n][:, 0:cols],
                                            xT[b.par][:, HI, k, m0:m0 + cols].bitcast(F32), ALU.subtract).then_inc(xT_lo, 1)

            def row_bias(b):
                p = slice(b.par, b.par + 1)
                dve.wait_ge(scores_done, b.n + 1)
                nc.vector.tensor_reduce(nmax[:, p], scores, AX.XY, ALU.max, negate=True).then_inc(max_ready, 1)
                dve.wait_ge(max_ready, b.n + 1)
                nc.vector.tensor_scalar(bias[:, p], nmax[:, p], cst[:, p], cst[:, p], ALU.subtract, ALU.add).then_inc(bias_ready, 1)

            def inverse(b):
                dve.wait_ge(exp_done, b.n + 1)
                nc.vector.reciprocal(inv[:, b.par:b.par + 1], sums[:, b.par:b.par + 1]).then_inc(inv_ready, 1)

            def values_lo(b):
                dve.wait_ge(uT_hi, b.n + 1)
                nc.vector.tensor_tensor(uT[:, b.par, LO, :], uu[:, 0:TC * N], uT[:, b.par, HI, :].bitcast(F32), ALU.subtract).then_inc(uT_lo, 1)

            def batch(b, first=False, last=False):
                if not last:
                    fill_lo(b.next(), 0)
                row_bias(b)
                if exists(b.next().next()):
                    stats(b.next().next())
                if not last:
                    for k in range(1, TC):
                        fill_lo(b.next(), k)
                inverse(b)
                values_lo(b)
                if exists(b.next().next()):
                    normalise(b.next().next())

            nc.vector.memset(tt[1][:, 0:TB * N], 0.0).then_inc(tail_zeroed, 1)
            dve.wait_ge(zeroed, 1)
            for par in range(2):
                stats(Batch(0, par))
            for par in range(2):
                normalise(Batch(0, par))
            for k in range(TC):
                fill_lo(Batch(0, 0), k)
            all_batches(dve, batch)




def cross_attention_kernel(nc, io):
    d = Shapes(io)
    B, N, D, M, T = d.B, d.N, d.D, d.M, d.T
    tokens = B * N
    keep = Kept()

    def dram(name, shape):
        return nc.dram_tensor(name, shape, F32, kind="Internal").ap()

    keep.A_dram = dram("folded_A", (2, D, T))
    keep.B_dram = dram("folded_B", (2, T, d.E))
    keep.Wo_dram = dram("Wo_parts", (2, D, D))
    keep.W1_dram = dram("W1_parts", (d.F // P, P, 2, D // P, P))
    keep.W2_dram = dram("W2_parts", (2, d.F, D))
    keep.q_dram = dram("queries", (2, D, tokens))
    keep.attn_dram = dram("attention", (D, tokens))
    keep.x1_dram = dram("x1", (tokens, D))
    keep.t_dram = dram("folded_queries", (2, T, tokens))
    keep.c_dram = dram("score_consts", (tokens, 1))
    with ExitStack() as ctx:
        s = Scope(nc, ctx)
        keep.ident = s.sb("ident", [P, P])
        keep.minus_half = s.sb("minus_half", [P, 8])
        keep.score_row, keep.score_const = s.sb("score_row", [P, D]), s.sb("score_const", [P, 1])
        keep.bd_row, keep.bo_row = s.sb("bd_row", [P, d.E]), s.sb("bo_row", [P, D])
        keep.t_bias = s.sb("t_bias", [P, T // P])
        keep.b1 = s.sb("b1_folded", [P, d.F // P])
        fold_phase(nc, d, io, keep)
        with ExitStack() as inner:
            s = Scope(nc, inner)
            keep.wk_hl = s.sb("wk_hl", [P, 2, T // P, D], F32R)
            keep.wv_hl = s.sb("wv_hl", [P, 2, T // P, D], F32R)
            keep.bk0 = s.sb("bk0", [P, D // P])
            queries_phase(nc, d, io, keep)
            attention_phase(nc, d, io, keep)
        tokens_phase(nc, d, io, keep)
        attention1_phase(nc, d, io, keep)


NAMES = ["x", "ctx_768"] + [f"L0_xattn_{n}" for n in (
    "Wq", "bq", "Wk", "bk", "Wv", "bv", "Wo", "bo", "ln_g", "ln_b", "W1", "b1", "W2", "b2")] + [
    f"L1_xattn_{n}" for n in ("Wq", "bq", "Wk", "bk", "Wv", "bv", "Wd", "bd", "g_q", "be_q", "g_kv", "be_kv")]


def kernel(**inputs):
    import numpy as _np
    import concourse.bacc as _bacc
    from concourse import mybir as _mybir
    from concourse.bass_utils import run_bass_kernel_spmd as _run

    nc = _bacc.Bacc("TRN2", target_bir_lowering=False, num_devices=1)
    arrays, aps = {}, {}
    for name in NAMES:
        a = _np.ascontiguousarray(inputs[name])
        arrays[f"in_{name}_dram"] = a
        aps[name] = nc.dram_tensor(f"in_{name}_dram", a.shape, _mybir.dt.from_np(a.dtype), kind="ExternalInput").ap()
    x = arrays["in_x_dram"]
    aps["out"] = nc.dram_tensor("out_0_dram", x.shape, _mybir.dt.from_np(x.dtype), kind="ExternalOutput").ap()
    cross_attention_kernel(nc, Inputs(aps))
    r = _run(nc, [arrays], core_ids=[0])
    return r.results[0]["out_0_dram"]
```

```python
from contextlib import ExitStack

import concourse.bass as bass
from concourse import mybir

F32 = mybir.dt.float32
F32R = mybir.dt.float32r
ALU = mybir.AluOpType
ACT = mybir.ActivationFunctionType
AX = mybir.AxisListType

P = 128
BANK = 512
EPS = 1e-5
HEADS = 16
HI, LO = 0, 1
PASSES = ((HI, HI), (HI, LO), (LO, HI))


def wait(eng, sem, value):
    if isinstance(value, int) and value <= 0:
        return
    eng.wait_ge(sem, value)


def wait_alone(eng, sem, value, passed):
    wait(eng, sem, value)
    eng.sem_inc(passed, 1)


class Inputs:

    def __init__(self, t):
        self.x, self.ctx = t["x"], t["ctx_768"]
        self.Wq0, self.bq0, self.Wk0, self.bk0 = (t[f"L0_xattn_{n}"] for n in ("Wq", "bq", "Wk", "bk"))
        self.Wv0, self.bv0, self.Wo, self.bo = (t[f"L0_xattn_{n}"] for n in ("Wv", "bv", "Wo", "bo"))
        self.ln_g, self.ln_b, self.W1, self.b1 = (t[f"L0_xattn_{n}"] for n in ("ln_g", "ln_b", "W1", "b1"))
        self.W2, self.b2 = t["L0_xattn_W2"], t["L0_xattn_b2"]
        self.Wq1, self.bq1, self.Wk1, self.bk1 = (t[f"L1_xattn_{n}"] for n in ("Wq", "bq", "Wk", "bk"))
        self.Wv1, self.bv1, self.Wd, self.bd = (t[f"L1_xattn_{n}"] for n in ("Wv", "bv", "Wd", "bd"))
        self.g_q, self.be_q, self.g_kv, self.be_kv = (t[f"L1_xattn_{n}"] for n in ("g_q", "be_q", "g_kv", "be_kv"))
        self.out = t["out"]


class Shapes:
    def __init__(self, io):
        self.B, self.N, self.D = io.x.shape
        _, self.M, self.T = io.ctx.shape
        self.E, self.F = io.Wq1.shape[0], io.W1.shape[1]
        self.SCALE = float(self.D // HEADS) ** -0.5


class Kept:
    pass


class Scope:

    def __init__(self, nc, ctx):
        self.nc, self.ctx = nc, ctx

    def sb(self, name, shape, dt=F32):
        return self.ctx.enter_context(self.nc.sbuf_tensor(name, shape, dt))

    def psum(self, name, shape):
        return self.ctx.enter_context(self.nc.psum_tensor(name, shape, F32))

    def sem(self, name):
        return self.ctx.enter_context(self.nc.semaphore(name))

    def sems(self, name, n):
        return [self.sem(f"{name}{i}") for i in range(n)]


class Batch:

    def __init__(self, pair, par):
        self.pair, self.par = pair, par
        self.n = pair * 2 + par

    def next(self):
        return Batch(self.pair, 1) if self.par == 0 else Batch(self.pair + 1, 0)

    def prev(self):
        return Batch(self.pair, 0) if self.par == 1 else Batch(self.pair - 1, 1)


class QuadBatch:

    def __init__(self, quad, slot):
        self.quad, self.slot, self.par = quad, slot, slot % 2
        self.n = quad * 4 + slot
        self.pair = quad * 2 + slot // 2

    def after(self, steps):
        slot = self.slot + steps
        return QuadBatch(self.quad + slot // 4, slot % 4)


def column(ap):
    return ap.rearrange("(c p) -> p c", p=P)


def row(ap):
    return ap.partition_broadcast(P)


def chunks(ap):
    return ap.rearrange("(c p) n -> p c n", p=P)


def fold_phase(nc, d, io, keep):
    D, T, E = d.D, d.T, d.E
    DC, TC, EC = D // P, T // P, E // P
    with ExitStack() as ctx:
        s = Scope(nc, ctx)
        wq, wk, wv = s.sb("f_wq", [P, EC, D]), s.sb("f_wk", [P, EC, T]), s.sb("f_wv", [P, EC, T])
        wd, wdT = s.sb("f_wd", [P, EC, E]), s.sb("f_wdT", [P, EC, E])
        wo0 = s.sb("f_wo0", [P, DC, D])
        gkv_row, bekv_row = s.sb("f_gkv_row", [P, T]), s.sb("f_bekv_row", [P, T])
        gq_row, beq_row = s.sb("f_gq_row", [P, D]), s.sb("f_beq_row", [P, D])
        bd_row, bo_row = s.sb("f_bd_row", [P, E]), s.sb("f_bo_row", [P, D])
        gq, gkv, beq = s.sb("f_gq", [P, DC]), s.sb("f_gkv", [P, TC]), s.sb("f_beq", [P, DC])
        bq, bk, bv, bv0 = (s.sb(f"f_b{n}", [P, EC]) for n in ("q", "k", "v", "v0"))
        bks, bvs = s.sb("f_bks", [P, EC]), s.sb("f_bvs", [P, EC])
        junk = s.sb("f_junk", [P, D])
        bks_wide, bvs_wide, bv0_wide = (s.sb(f"f_{n}_wide", [P, EC, P]) for n in ("bks", "bvs", "bv0"))
        a_raw, a_s = s.sb("f_a_raw", [P, DC, T]), s.sb("f_a_s", [P, DC, T])
        a_hl, b_hl = s.sb("f_a_hl", [P, 2, DC, T], F32R), s.sb("f_b_hl", [P, 2, TC, E], F32R)
        b_s = s.sb("f_b_s", [P, TC, E])
        u, csum, qbk = s.sb("f_u", [P, D]), s.sb("f_csum", [P, 1]), s.sb("f_qbk", [P, 1])
        ps = [s.psum(f"f_ps{i}", [P, BANK]) for i in range(8)]
        loads, wo_loads, stores = s.sem("f_loads"), s.sem("f_wo_loads"), s.sem("f_stores")
        sums_ready = s.sem("f_sums_ready")
        wide_ready = s.sem("f_wide_ready")
        wdT_in_psum, wdT_ready = s.sem("f_wdT_in_psum"), s.sem("f_wdT_ready")
        a_in_psum, a_copied = s.sem("f_a_in_psum"), s.sem("f_a_copied")
        a_scaled, a_hi_ready, a_lo_ready = s.sem("f_a_scaled"), s.sem("f_a_hi_ready"), s.sem("f_a_lo_ready")
        b_in_psum, b_scaled, b_hi_ready, b_lo_ready = (
            s.sem(f"f_b_{n}") for n in ("in_psum", "scaled", "hi_ready", "lo_ready"))
        rows_in_psum, u_ready, rows_done = s.sem("f_rows_in_psum"), s.sem("f_u_ready"), s.sem("f_rows_done")
        ident_ready = s.sem("f_ident_ready")
        block = ctx.enter_context(nc.Block())
        W2C = d.F // D
        PIECES = [("wo", 0)] + [("w1", k) for k in range(DC)] + [("w2", k) for k in range(W2C)]
        pw, pw_hl = s.sb("f_pw", [P, 2, d.F]), s.sb("f_pw_hl", [P, 2, 2, d.F], F32R)
        ln_g, ln_b, b1, b1_sum = s.sb("f_ln_g", [P, DC]), s.sb("f_ln_b", [P, DC]), s.sb("f_b1", [P, d.F // P]), s.sb("f_b1_sum", [P, DC, d.F // P])
        piece_loaded, piece_stored = s.sems("f_piece_loaded", 2), s.sems("f_piece_stored", 2)
        piece_hi, piece_lo, ln_loaded = s.sem("f_piece_hi"), s.sem("f_piece_lo"), s.sem("f_ln_loaded")
        b1_in_psum, b1_done = s.sem("f_b1_in_psum"), s.sem("f_b1_done")
        VECTORS = ((gkv_row, row(io.g_kv)), (bekv_row, row(io.be_kv)), (gq_row, row(io.g_q)),
                   (beq_row, row(io.be_q)), (bd_row, row(io.bd)), (bo_row, row(io.bo)),
                   (gq, column(io.g_q)), (gkv, column(io.g_kv)), (beq, column(io.be_q)),
                   (bq, column(io.bq1)), (bk, column(io.bk1)), (bv, column(io.bv1)), (bv0, column(io.bv0)))
        ALL_LOADS = 16 * (4 + len(VECTORS))

        @block.sync
        def _(sp):
            for t, w in ((wq, io.Wq1), (wk, io.Wk1), (wv, io.Wv1), (wd, io.Wd)):
                sp.dma_start(t[:], chunks(w)).then_inc(loads, 16)
            for t, v in VECTORS:
                sp.dma_start(t[:], v, allow_slow_non_contiguous=True).then_inc(loads, 16)
            sp.dma_start(wo0[:], chunks(io.Wo)).then_inc(wo_loads, 16)

            def load(n):
                kind, k = PIECES[n]
                src = {"wo": lambda: chunks(io.Wo), "w1": lambda: io.W1[P * k:P * (k + 1), :],
                       "w2": lambda: chunks(io.W2[D * k:D * (k + 1), :])}[kind]()
                dst = pw[:, n % 2, :]
                if kind != "w1":
                    dst = dst.rearrange("p (c n) -> p c n", n=D)
                sp.dma_start(dst, src).then_inc(piece_loaded[n % 2], 16)

            for t, v in ((ln_g, io.ln_g), (ln_b, io.ln_b), (b1, io.b1)):
                sp.dma_start(t[:], column(v), allow_slow_non_contiguous=True).then_inc(ln_loaded, 16)
            load(0)
            load(1)
            for n, (kind, k) in enumerate(PIECES):
                sp.wait_ge(piece_hi, n + 1)
                sp.wait_ge(piece_lo, n + 1)
                for hl in range(2):
                    src = pw_hl[:, n % 2, hl, :].bitcast(F32)
                    if kind == "w1":
                        dst = keep.W1_dram[:, :, hl, k, :].rearrange("j p n -> p j n")
                        src = src.rearrange("p (j n) -> p j n", n=P)
                    else:
                        dst = (keep.Wo_dram[hl] if kind == "wo" else keep.W2_dram[hl, D * k:D * (k + 1), :])
                        dst = dst.rearrange("(c p) n -> p c n", p=P)
                        src = src.rearrange("p (c n) -> p c n", n=D)
                    sp.dma_start(dst, src).then_inc(piece_stored[n % 2], 16)
                if n + 2 < len(PIECES):
                    if kind == "w1":
                        sp.wait_ge(b1_in_psum, k + 1)
                    load(n + 2)
            for par in range(2):
                sp.wait_ge(piece_stored[par], 32 * len(range(par, len(PIECES), 2)))
            sp.wait_ge(a_hi_ready, 1)
            sp.wait_ge(a_lo_ready, 1)
            sp.dma_start(keep.A_dram.rearrange("h (c p) n -> p h c n", p=P), a_hl[:].bitcast(F32)).then_inc(stores, 16)
            sp.wait_ge(b_hi_ready, 1)
            sp.wait_ge(b_lo_ready, 1)
            sp.dma_start(keep.B_dram.rearrange("h (c p) n -> p h c n", p=P), b_hl[:].bitcast(F32)).then_inc(stores, 16)
            sp.wait_ge(stores, 32)

        @block.gpsimd
        def _(pool):
            nc.gpsimd.memset(keep.minus_half[:], -0.5)
            nc.gpsimd.memset(keep.ident[:], 0.0).then_inc(ident_ready, 1)
            pool.wait_ge(ident_ready, 1)
            nc.gpsimd.affine_select(out=keep.ident[:], in_=keep.ident[:], compare_op=ALU.not_equal, fill=1.0,
                                    base=0, pattern=[[-1, P]], channel_multiplier=1).then_inc(ident_ready, 1)

        @block.vector
        def _(dve):
            dve.wait_ge(loads, ALL_LOADS)
            for n, (w, b, out) in enumerate(((wk, bk, bks), (wv, bv, bvs))):
                for c in range(EC):
                    wait(dve, sums_ready, n * EC + c)
                    nc.vector.tensor_tensor_reduce(out=junk[:, 0:T], in0=w[:, c, :], in1=bekv_row[:], scale=1.0,
                                                   scalar=b[:, c:c + 1], op0=ALU.mult, op1=ALU.add,
                                                   accum_out=out[:, c:c + 1]).then_inc(sums_ready, 1)
            dve.wait_ge(sums_ready, 2 * EC)
            for src, dst in ((bks, bks_wide), (bvs, bvs_wide), (bv0, bv0_wide)):
                nc.vector.tensor_copy(dst[:], src[:].unsqueeze(2).to_broadcast([P, EC, P])).then_inc(wide_ready, 1)
            dve.wait_ge(wdT_in_psum, 1)
            for c in range(EC):
                nc.vector.tensor_copy(wdT[:, c, :], ps[c][:, 0:E]).then_inc(wdT_ready, 1)
            dve.wait_ge(a_in_psum, 1)
            for c in range(DC):
                nc.vector.tensor_copy(a_raw[:, c, :], ps[4 + c][:, 0:T]).then_inc(a_copied, 1)
                dve.wait_ge(a_copied, c + 1)
                nc.vector.scalar_tensor_tensor(out=a_s[:, c, :], in0=a_raw[:, c, :], scalar=gq[:, c:c + 1],
                                               in1=gkv_row[:], op0=ALU.mult, op1=ALU.mult).then_inc(a_scaled, 1)
            dve.wait_ge(a_hi_ready, 1)
            nc.vector.tensor_tensor(a_hl[:, LO], a_s[:], a_hl[:, HI].bitcast(F32), ALU.subtract).then_inc(a_lo_ready, 1)
            dve.wait_ge(b_in_psum, 1)
            for c in range(TC):
                nc.vector.tensor_scalar(b_s[:, c, :], ps[c][:, 0:E], gkv[:, c:c + 1], None, ALU.mult).then_inc(b_scaled, 1)
            dve.wait_ge(b_hi_ready, 1)
            nc.vector.tensor_tensor(b_hl[:, LO], b_s[:], b_hl[:, HI].bitcast(F32), ALU.subtract).then_inc(b_lo_ready, 1)
            dve.wait_ge(rows_in_psum, 1)
            nc.vector.tensor_copy(u[:], ps[4][:, 0:D]).then_inc(u_ready, 1)
            dve.wait_ge(u_ready, 1)
            nc.vector.tensor_tensor(keep.score_row[:], u[:], gq_row[:], ALU.mult).then_inc(rows_done, 1)
            nc.vector.tensor_tensor_reduce(out=junk[:], in0=u[:], in1=beq_row[:], scale=1.0, scalar=0.0,
                                           op0=ALU.mult, op1=ALU.add, accum_out=csum[:]).then_inc(rows_done, 1)
            dve.wait_ge(rows_done, 2)
            nc.vector.tensor_tensor(keep.score_const[:], ps[7][:, 0:1], csum[:], ALU.add).then_inc(rows_done, 1)
            nc.vector.tensor_tensor(keep.bd_row[:], ps[5][:, 0:E], bd_row[:], ALU.add).then_inc(rows_done, 1)
            nc.vector.tensor_tensor(keep.bo_row[:], ps[6][:, 0:D], bo_row[:], ALU.add).then_inc(rows_done, 1)
            nc.vector.tensor_tensor(keep.t_bias[:], ps[3][:, 0:TC], gkv[:], ALU.mult).then_inc(rows_done, 1)
            dve.wait_ge(rows_done, 6)
            dve.wait_ge(ln_loaded, 48)
            for n, (kind, k) in enumerate(PIECES):
                dve.wait_ge(piece_hi, n + 1)
                hi = pw_hl[:, n % 2, HI, :].bitcast(F32)
                if kind == "w1":
                    nc.vector.scalar_tensor_tensor(out=pw_hl[:, n % 2, LO, :], in0=pw[:, n % 2, :], scalar=ln_g[:, k:k + 1],
                                                   in1=hi, op0=ALU.mult, op1=ALU.subtract).then_inc(piece_lo, 1)
                else:
                    nc.vector.tensor_tensor(pw_hl[:, n % 2, LO, :], pw[:, n % 2, :], hi, ALU.subtract).then_inc(piece_lo, 1)
            dve.wait_ge(b1_in_psum, DC)
            nc.vector.tensor_copy(b1_sum[:], ps[0][:, 0:DC * (d.F // P)].rearrange("p (k j) -> p k j", k=DC)).then_inc(b1_done, 1)
            for k in range(DC):
                dve.wait_ge(b1_done, k + 1)
                nc.vector.tensor_tensor(keep.b1[:], b1_sum[:, k, :], (b1 if k == 0 else keep.b1)[:], ALU.add).then_inc(b1_done, 1)

        @block.scalar
        def _(act):
            act.wait_ge(a_scaled, DC)
            nc.scalar.activation(a_hl[:, HI], a_s[:], ACT.Copy).then_inc(a_hi_ready, 1)
            act.wait_ge(b_scaled, TC)
            nc.scalar.activation(b_hl[:, HI], b_s[:], ACT.Copy).then_inc(b_hi_ready, 1)
            act.wait_ge(ln_loaded, 48)
            for n, (kind, k) in enumerate(PIECES):
                act.wait_ge(piece_loaded[n % 2], 16 * (n // 2 + 1))
                wait(act, piece_stored[n % 2], 32 * (n // 2))
                act_scale = ln_g[:, k:k + 1] if kind == "w1" else 1.0
                nc.scalar.activation(pw_hl[:, n % 2, HI, :], pw[:, n % 2, :], ACT.Copy, scale=act_scale).then_inc(piece_hi, 1)

        @block.tensor
        def _(pe):
            pe.wait_ge(ident_ready, 2)
            pe.wait_ge(loads, ALL_LOADS)
            for c in range(EC):
                for f in range(EC):
                    last = nc.tensor.transpose(ps[c][:, P * f:P * (f + 1)], wd[:, f, P * c:P * (c + 1)], keep.ident[:])
            last.then_inc(wdT_in_psum, 1)
            for c in range(DC):
                for e in range(EC):
                    last = nc.tensor.matmul(ps[4 + c][:, 0:T], wq[:, e, P * c:P * (c + 1)], wk[:, e, :],
                                            start=e == 0, stop=e == EC - 1)
            last.then_inc(a_in_psum, 1)
            pe.wait_ge(wdT_ready, EC)
            for c in range(TC):
                for e in range(EC):
                    last = nc.tensor.matmul(ps[c][:, 0:E], wv[:, e, P * c:P * (c + 1)], wdT[:, e, :],
                                            start=e == 0, stop=e == EC - 1)
            last.then_inc(b_in_psum, 1)
            pe.wait_ge(wide_ready, 3)
            pe.wait_ge(wo_loads, 16)
            pe.wait_ge(a_copied, DC)
            for bank, lhs, rhs in ((4, bks_wide, wq), (5, bvs_wide, wdT), (6, bv0_wide, wo0), (7, bks_wide, bq)):
                n = 1 if rhs is bq else D
                for e in range(EC):
                    moving = bq[:, e:e + 1] if rhs is bq else rhs[:, e, :]
                    nc.tensor.matmul(ps[bank][:, 0:n], lhs[:, e, :], moving, start=e == 0, stop=e == EC - 1)
            for c in range(TC):
                for e in range(EC):
                    nc.tensor.matmul(ps[3][:, c:c + 1], wk[:, e, P * c:P * (c + 1)], bq[:, e:e + 1],
                                     start=e == 0, stop=False)
                for q in range(DC):
                    last = nc.tensor.matmul(ps[3][:, c:c + 1], a_raw[:, q, P * c:P * (c + 1)], beq[:, q:q + 1],
                                            start=False, stop=q == DC - 1)
            last.then_inc(rows_in_psum, 1)
            pe.wait_ge(ln_loaded, 48)
            pe.wait_ge(b_scaled, TC)
            for k in range(DC):
                n = PIECES.index(("w1", k))
                pe.wait_ge(piece_loaded[n % 2], 16 * (n // 2 + 1))
                for j in range(d.F // P):
                    at0 = k * (d.F // P) + j
                    last = nc.tensor.matmul(ps[0][:, at0:at0 + 1], pw[:, n % 2, P * j:P * (j + 1)], ln_b[:, k:k + 1],
                                            start=True, stop=True)
                last.then_inc(b1_in_psum, 1)


def queries_phase(nc, d, io, keep):
    D, T, N = d.D, d.T, d.N
    DC, TC = D // P, T // P
    PER = 4
    STEPS = d.B // PER
    TOK = PER * N
    with ExitStack() as ctx:
        s = Scope(nc, ctx)
        wq, wk, wv = s.sb("q_wq", [P, DC, D]), s.sb("q_wk", [P, TC, D]), s.sb("q_wv", [P, TC, D])
        wq_hl = s.sb("q_wq_hl", [P, 2, DC, D], F32R)
        bq, bqs = s.sb("q_bq", [P, DC]), s.sb("q_bqs", [P, DC])
        xn = s.sb("q_xn", [N, PER, D])
        xT = s.sb("q_xT", [P, 2, DC, TOK], F32R)
        q32 = s.sb("q_q32", [P, DC, TOK])
        q_hl = s.sb("q_q_hl", [P, 2, DC, TOK], F32R)
        pt = [s.psum(f"q_pt{i}", [P, BANK]) for i in range(4)]
        pq = [s.psum(f"q_pq{i}", [P, BANK]) for i in range(4)]
        passed = s.sem("q_passed")
        w_loads, x_loads, stores = s.sem("q_w_loads"), s.sem("q_x_loads"), s.sem("q_stores")
        w_hi, w_lo, bias_ready = s.sem("q_w_hi"), s.sem("q_w_lo"), s.sem("q_bias_ready")
        xT_in_psum, xT_hi, xT_lo = s.sem("q_xT_in_psum"), s.sem("q_xT_hi"), s.sem("q_xT_lo")
        q_in_psum, q_ready, q_hi, q_lo = (s.sem(f"q_q_{n}") for n in ("in_psum", "ready", "hi", "lo"))
        block = ctx.enter_context(nc.Block())
        WEIGHTS = ((wq, wq_hl), (wk, keep.wk_hl), (wv, keep.wv_hl))
        x_rows = io.x.rearrange("b n d -> (b n) d")

        def all_steps(eng, step):
            step(0)
            with eng.Fori(1, STEPS) as i:
                step(i)

        @block.sync
        def _(sp):
            sp.dma_start(wq[:], chunks(io.Wq0)).then_inc(w_loads, 16)
            sp.dma_start(bq[:], column(io.bq0), allow_slow_non_contiguous=True).then_inc(w_loads, 16)
            sp.dma_start(keep.bk0[:], column(io.bk0), allow_slow_non_contiguous=True).then_inc(w_loads, 16)
            sp.dma_start(wk[:], chunks(io.Wk0)).then_inc(w_loads, 16)
            sp.dma_start(wv[:], chunks(io.Wv0)).then_inc(w_loads, 16)
            def step(i):
                wait(sp, xT_in_psum, i * DC)
                sp.dma_start(xn[:], x_rows[bass.ds(i * TOK, TOK), :].rearrange("(t p) d -> p t d", p=N)).then_inc(x_loads, 16)
                wait_alone(sp, q_lo, (i + 1) * DC, passed)
                sp.dma_start(keep.q_dram[:, :, bass.ds(i * TOK, TOK)].rearrange("h (c p) n -> p h c n", p=P),
                             q_hl[:].bitcast(F32)).then_inc(stores, 16)

            all_steps(sp, step)
            sp.wait_ge(stores, 16 * STEPS)

        @block.tensor
        def _(pe):
            pe.wait_ge(w_lo, 3)
            def step(i):
                pe.wait_ge(x_loads, 16 * (i + 1))
                for k in range(DC):
                    wait(pe, xT_lo, i * DC)
                    for t in range(PER):
                        last = nc.tensor.transpose(pt[k][:, t * N:(t + 1) * N], xn[:, t, P * k:P * (k + 1)],
                                                   keep.ident[0:N, 0:N])
                    last.then_inc(xT_in_psum, 1)
                pe.wait_ge(xT_lo, (i + 1) * DC)
                wait(pe, q_ready, i * DC)
                for c in range(DC):
                    for k in range(DC):
                        for a, b in PASSES:
                            last = nc.tensor.matmul(pq[c][:, 0:TOK], wq_hl[:, a, k, P * c:P * (c + 1)], xT[:, b, k, :],
                                                    start=(k, a, b) == (0, HI, HI), stop=(k, a, b) == (DC - 1, LO, HI))
                    last.then_inc(q_in_psum, 1)

            all_steps(pe, step)

        @block.scalar
        def _(act):
            act.wait_ge(w_loads, 5 * 16)
            nc.scalar.mul(bqs[:], bq[:], d.SCALE).then_inc(bias_ready, 1)
            for w, hl in WEIGHTS:
                nc.scalar.activation(hl[:, HI], w[:], ACT.Copy).then_inc(w_hi, 1)
            act.wait_ge(bias_ready, 1)
            def step(i):
                for k in range(DC):
                    act.wait_ge(xT_in_psum, i * DC + k + 1)
                    wait(act, q_in_psum, i * DC)
                    nc.scalar.activation(xT[:, HI, k, :], pt[k][:, 0:TOK], ACT.Copy).then_inc(xT_hi, 1)
                wait(act, stores, i * 16)
                wait(act, q_lo, i * DC)
                for c in range(DC):
                    act.wait_ge(q_in_psum, i * DC + c + 1)
                    nc.scalar.activation(q32[:, c, :], pq[c][:, 0:TOK], ACT.Identity, bias=bqs[:, c:c + 1],
                                         scale=d.SCALE).then_inc(q_ready, 1)
                    act.wait_ge(q_ready, i * DC + c + 1)
                    nc.scalar.activation(q_hl[:, HI, c, :], q32[:, c, :], ACT.Copy).then_inc(q_hi, 1)

            all_steps(act, step)

        @block.vector
        def _(dve):
            for n, (w, hl) in enumerate(WEIGHTS):
                dve.wait_ge(w_hi, n + 1)
                nc.vector.tensor_tensor(hl[:, LO], w[:], hl[:, HI].bitcast(F32), ALU.subtract).then_inc(w_lo, 1)
            def step(i):
                for k in range(DC):
                    dve.wait_ge(xT_hi, i * DC + k + 1)
                    nc.vector.tensor_tensor(xT[:, LO, k, :], pt[k][:, 0:TOK], xT[:, HI, k, :].bitcast(F32),
                                            ALU.subtract).then_inc(xT_lo, 1)
                for c in range(DC):
                    dve.wait_ge(q_hi, i * DC + c + 1)
                    nc.vector.tensor_tensor(q_hl[:, LO, c, :], q32[:, c, :], q_hl[:, HI, c, :].bitcast(F32),
                                            ALU.subtract).then_inc(q_lo, 1)

            all_steps(dve, step)


def attention_phase(nc, d, io, keep):
    B, N, M, D, T = d.B, d.N, d.M, d.D, d.T
    TC, DC, DH = T // P, D // P, D // HEADS
    MT = -(-M // P)
    LAST = M - P * (MT - 1)
    TB = MT // 2
    SPLIT = ((0, TB * P), (TB * P, M - TB * P))
    MH = M // 2
    SW = MH + 1
    PAIRS, QUADS = HEADS // 2, HEADS // 4
    assert M % 2 == 0 and SW % 2 == 0 and MT % 2 == 0
    K_STEPS = [("k", c, n) for c in range(DC) for n in range(2)]
    V_STEPS = [("v", t, 0) for t in range(MT)]
    STEPS = [x for pair in zip(K_STEPS, V_STEPS) for x in pair] + K_STEPS[MT:]
    NK, NV, NSTEP = len(K_STEPS), len(V_STEPS), len(STEPS)
    FILLS = TC
    NEED_K = [STEPS.index(("k", c, 1)) for c in range(DC)]
    by_slot = [[n for n in range(NSTEP) if min(FILLS + n, HEADS - 1) == h] for h in range(HEADS)]

    lo_of_slot = [[]] + by_slot[0:HEADS - 2] + [by_slot[HEADS - 2] + by_slot[HEADS - 1][:-1]]

    def k_before(n):
        return sum(x[0] == "k" for x in STEPS[:n])

    def rows_of(t):
        return LAST if t == MT - 1 else P

    with ExitStack() as ctx:
        s = Scope(nc, ctx)
        cn = [s.sb(f"a_cn{i}", [P, MT, T]) for i in range(2)]
        cT = s.sb("a_cT", [P, 2, TC, M], F32R)
        kt = [s.sb(f"a_kt{i}", [P, PAIRS, M], F32R) for i in range(2)]
        vn = [s.sb(f"a_vn{i}", [P, MT, D]) for i in range(2)]
        qm = [s.sb(f"a_qm{i}", [P, 2, HEADS, N], F32R) for i in range(2)]
        pr = s.sb("a_pr", [N, 4, M])
        pT = s.sb("a_pT", [P, 2, 4, MT, N])
        nmax, sums = s.sb("a_nmax", [N, 2, HEADS]), s.sb("a_sums", [N, 2, HEADS])
        kw = s.sb("a_kw", [P, 2, SPLIT[0][1]])
        inv, rexp = s.sb("a_inv", [N, 2, 4]), s.sb("a_rexp", [N, 2, 4, DH])
        rb = s.sb("a_rb", [P, 2, N])
        at = s.sb("a_at", [P, 2, QUADS, N])
        ps = s.psum("a_ps", [P, 8 * BANK])
        tp = [ps[:, 4 * BANK:5 * BANK], ps[:, 5 * BANK:6 * BANK]]
        pj, av = ps[:, 6 * BANK:7 * BANK], ps[:, 7 * BANK:8 * BANK]

        def scores(buf):
            start = 2 * buf * BANK
            return ps[0:N, start:start + 2 * (BANK + 1)].rearrange("p (c n) -> p c n", c=2)[:, :, 0:MH]

        ctx_loaded, q_loaded = s.sems("a_ctx_loaded", 2), s.sems("a_q_loaded", 2)
        zeroed, tail_zeroed, stored = s.sem("a_zeroed"), s.sem("a_tail_zeroed"), s.sems("a_stored", 2)
        filled, cT_hi, cT_lo = s.sem("a_filled"), s.sem("a_cT_hi"), s.sem("a_cT_lo")
        proj_done, kw_ready, k_hi = s.sem("a_proj_done"), s.sem("a_kw_ready"), s.sem("a_k_hi")
        k_ready, v_ready = s.sem("a_k_ready"), s.sem("a_v_ready")
        scores_done, max_ready, exp_done = s.sem("a_scores_done"), s.sem("a_max_ready"), s.sem("a_exp_done")
        p_turned, pT_ready = s.sem("a_p_turned"), s.sems("a_pT_ready", 2)
        inv_ready, rexp_ready, av_done = s.sem("a_inv_ready"), s.sem("a_rexp_ready"), s.sem("a_av_done")
        rb_ready, at_ready = s.sem("a_rb_ready"), s.sem("a_at_ready")
        block = ctx.enter_context(nc.Block())
        Q_LOADS = 8 * 16

        def all_batches(eng, batch):
            batch(Batch(0, 0), first=True)
            batch(Batch(0, 1))
            with eng.Fori(1, B // 2 - 1) as pair:
                batch(Batch(pair, 0))
                batch(Batch(pair, 1))
            batch(Batch(B // 2 - 1, 0))
            batch(Batch(B // 2 - 1, 1), last=True)

        @block.sync
        def _(sp):
            def load_ctx(b):
                wait(sp, filled, (b.n - 1) * 2 * FILLS)
                src = io.ctx[bass.ds(b.n, 1), :, :].rearrange("b m t -> (b m) t")
                whole = P * (MT - 1)
                sp.dma_start(cn[b.par][:, 0:MT - 1, :], src[0:whole, :].rearrange("(t p) d -> p t d", p=P)).then_inc(ctx_loaded[b.par], 16)
                sp.dma_start(cn[b.par][0:LAST, MT - 1, :], src[whole:M, :]).then_inc(ctx_loaded[b.par], 16)

            def load_q(b):
                wait(sp, scores_done, (b.n - 1) * HEADS)
                for hl in range(2):
                    src = keep.q_dram[hl, :, bass.ds(b.n * N, N)].rearrange("(i o d) n -> o d i n", o=2, d=DH)
                    for odd in range(2):
                        dst = qm[b.par][:, hl].bitcast(F32).rearrange("p (i o) n -> p o i n", o=2)[:, odd]
                        for copy in range(2):
                            r = (2 * copy + odd) * DH
                            sp.dma_start(dst[r:r + DH], src[odd]).then_inc(q_loaded[b.par], 16)

            def store(b):
                sp.wait_ge(at_ready, (b.n + 1) * QUADS)
                sp.dma_start(keep.attn_dram[:, bass.ds(b.n * N, N)].rearrange("(c p) n -> p c n", p=P),
                             at[:, b.par]).then_inc(stored[b.par], 16)

            def batch(b, first=False, last=False):
                if not isinstance(b.n, int) or b.n + 2 < B:
                    load_ctx(b.next().next())
                if not last:
                    load_q(b.next())
                if not first:
                    store(b.prev())

            load_ctx(Batch(0, 0))
            load_ctx(Batch(0, 1))
            sp.wait_ge(zeroed, 2)
            load_q(Batch(0, 0))
            all_batches(sp, batch)
            store(Batch(B // 2 - 1, 1))
            for par in range(2):
                sp.wait_ge(stored[par], 16 * (B // 2))

        @block.gpsimd
        def _(pool):
            for i in range(2):
                nc.gpsimd.memset(qm[i][:].bitcast(F32), 0.0).then_inc(zeroed, 1)

        @block.tensor
        def _(pe):
            def fill(b, k, n):
                if k == 0 and n == 0:
                    pe.wait_ge(ctx_loaded[b.par], (b.pair + 1) * 32)
                    wait(pe, kw_ready, b.n * NK)
                    wait(pe, v_ready, b.n * NV)
                wait(pe, cT_lo, b.n * 2 * FILLS + 2 * k + n)
                for t in range(TB * n, TB * (n + 1)):
                    at0, rows = P * (t - TB * n), rows_of(t)
                    last = nc.tensor.transpose(pj[:, at0:at0 + rows], cn[b.par][0:rows, t, P * k:P * (k + 1)],
                                               keep.ident[0:rows, 0:rows])
                last.then_inc(filled, 1)

            def project(b, n):
                kind, i, half = STEPS[n]
                if n == 0:
                    pe.wait_ge(cT_lo, (b.n + 1) * 2 * FILLS)
                wait(pe, kw_ready, b.n * NK + k_before(n))
                wait(pe, v_ready, b.n * NV + n - k_before(n))
                for k in range(TC):
                    for x, y in PASSES:
                        flags = dict(start=(k, x, y) == (0, HI, HI), stop=(k, x, y) == (TC - 1, LO, HI))
                        if kind == "k":
                            m0, cols = SPLIT[half]
                            last = nc.tensor.matmul(pj[:, 0:cols], keep.wk_hl[:, x, k, P * i:P * (i + 1)],
                                                    cT[:, y, k, m0:m0 + cols], **flags)
                        else:
                            last = nc.tensor.matmul(pj[0:rows_of(i), :], cT[:, x, k, P * i:P * i + rows_of(i)],
                                                    keep.wv_hl[:, y, k, :], **flags)
                last.then_inc(proj_done, 1)

            def score(b, h):
                if h == 0:
                    pe.wait_ge(q_loaded[b.par], (b.pair + 1) * Q_LOADS)
                if h % 4 == 0:
                    pe.wait_ge(k_ready, b.n * NK + k_before(NEED_K[h // 4]) + 1)
                wait(pe, exp_done, b.n * HEADS + h - 1)
                for n in range(2):
                    at0 = (2 * (h % 2) + n) * BANK
                    m0 = n * (MH - 1)
                    for hl in range(2):
                        last = nc.tensor.matmul(ps[0:N, at0:at0 + SW], qm[b.par][:, hl, h, :],
                                                kt[b.par][:, h // 2, m0:m0 + SW], start=hl == HI, stop=hl == LO)
                last.then_inc(scores_done, 1)

            def turn(b, h):
                g = b.n * HEADS + h
                pe.wait_ge(exp_done, g + 1)
                for n in range(2):
                    wait(pe, pT_ready[n], g)
                    for t in range(TB * n, TB * (n + 1)):
                        at0 = N * (t - TB * n)
                        last = nc.tensor.transpose(tp[n][0:rows_of(t), at0:at0 + N], pr[:, h % 4, P * t:P * t + rows_of(t)],
                                                   keep.ident[0:N, 0:N])
                last.then_inc(p_turned, 1)

            def values(b, q):
                quad = b.n * QUADS + q
                for n in range(2):
                    pe.wait_ge(pT_ready[n], (quad + 1) * 4)
                if q == 0:
                    pe.wait_ge(v_ready, (b.n + 1) * NV)
                wait(pe, at_ready, quad)
                for t in range(MT):
                    for j in range(4):
                        h = 4 * q + j
                        nc.tensor.matmul(av[DH * j:DH * (j + 1), 0:N], vn[b.par][0:rows_of(t), t, DH * h:DH * (h + 1)],
                                         pT[0:rows_of(t), q % 2, j, t, :], start=t == 0, stop=t == MT - 1)
                pe.wait_ge(rexp_ready, quad + 1)
                nc.tensor.matmul(av[:, P:P + N], rexp[:, q % 2].rearrange("n j d -> n (j d)"), keep.ident[0:N, 0:N],
                                 start=True, stop=True).then_inc(av_done, 1)

            def batch(b, first=False, last=False):
                for h in range(HEADS):
                    score(b, h)
                    if not last and h < FILLS:
                        fill(b.next(), h, 0)
                    if not last and h == HEADS - 1:
                        for n in by_slot[h][:-1]:
                            project(b.next(), n)
                    if h > 0:
                        turn(b, h - 1)
                    elif not first:
                        turn(b.prev(), HEADS - 1)
                    if not last and h < FILLS:
                        fill(b.next(), h, 1)
                    if h % 4 == 1 and h > 1:
                        values(b, h // 4 - 1)
                    elif h == 1 and not first:
                        values(b.prev(), QUADS - 1)
                    if not last:
                        for n in by_slot[h][-1:]:
                            project(b.next(), n)

            for k in range(FILLS):
                for n in range(2):
                    fill(Batch(0, 0), k, n)
            for n in range(NSTEP):
                project(Batch(0, 0), n)
            pe.wait_ge(tail_zeroed, 1)
            all_batches(pe, batch)
            end = Batch(B // 2 - 1, 1)
            turn(end, HEADS - 1)
            values(end, QUADS - 1)

        @block.scalar
        def _(act):
            def fill_hi(b, k, n):
                m0, cols = SPLIT[n]
                act.wait_ge(filled, b.n * 2 * FILLS + 2 * k + n + 1)
                wait(act, proj_done, b.n * NSTEP)
                nc.scalar.activation(cT[:, HI, k, m0:m0 + cols], pj[:, 0:cols], ACT.Copy).then_inc(cT_hi, 1)

            def key_hi(b, n):
                kind, i, half = STEPS[n]
                if kind != "k":
                    return
                m0, cols = SPLIT[half]
                step = b.n * NK + k_before(n)
                buf = k_before(n) % 2
                act.wait_ge(proj_done, b.n * NSTEP + n + 1)
                wait(act, k_ready, step - 1)
                nc.scalar.activation(kw[:, buf, 0:cols], pj[:, 0:cols], ACT.Identity, bias=keep.bk0[:, i:i + 1]).then_inc(kw_ready, 1)
                act.wait_ge(kw_ready, step + 1)
                for r in range(2):
                    nc.scalar.activation(kt[b.par][0:64, 2 * i + r, m0:m0 + cols], kw[64 * r:64 * r + 64, buf, 0:cols],
                                         ACT.Copy).then_inc(k_hi, 1)

            def turned(b, h):
                act.wait_ge(p_turned, b.n * HEADS + h + 1)
                if h % 4 == 0:
                    wait(act, av_done, b.n * QUADS + h // 4 - 1)
                nc.scalar.activation(pT[:, (h // 4) % 2, h % 4, TB:MT, :],
                                     tp[1][:, 0:TB * N].rearrange("p (t n) -> p t n", n=N), ACT.Copy).then_inc(pT_ready[1], 1)

            def exp(b, h):
                g = b.n * HEADS + h
                act.wait_ge(max_ready, g + 1)
                wait(act, p_turned, g - 3)
                nc.scalar.activation(pr[:, h % 4, :].rearrange("n (c m) -> n c m", c=2), scores(h % 2), ACT.Exp,
                                     bias=nmax[:, b.par, h:h + 1], accum_out=sums[:, b.par, h:h + 1]).then_inc(exp_done, 1)

            def spread(b, q):
                quad = b.n * QUADS + q
                act.wait_ge(av_done, quad + 1)
                wait(act, at_ready, quad - 1)
                nc.scalar.activation(rb[:, q % 2, :], av[:, P:P + N], ACT.Copy).then_inc(rb_ready, 1)

            def batch(b, first=False, last=False):
                for h in range(HEADS):
                    if not last and h < FILLS:
                        fill_hi(b.next(), h, 0)
                    if not last and h == HEADS - 1:
                        for n in by_slot[h][:-1]:
                            key_hi(b.next(), n)
                    if h > 0:
                        turned(b, h - 1)
                    elif not first:
                        turned(b.prev(), HEADS - 1)
                    exp(b, h)
                    if not last and h < FILLS:
                        fill_hi(b.next(), h, 1)
                    if h % 4 == 1 and h > 1:
                        spread(b, h // 4 - 1)
                    elif h == 1 and not first:
                        spread(b.prev(), QUADS - 1)
                    if not last:
                        for n in by_slot[h][-1:]:
                            key_hi(b.next(), n)

            for k in range(FILLS):
                for n in range(2):
                    fill_hi(Batch(0, 0), k, n)
            for n in range(NSTEP):
                key_hi(Batch(0, 0), n)
            act.wait_ge(tail_zeroed, 1)
            all_batches(act, batch)
            end = Batch(B // 2 - 1, 1)
            turned(end, HEADS - 1)
            spread(end, QUADS - 1)

        @block.vector
        def _(dve):
            def fill_lo(b, k, n):
                m0, cols = SPLIT[n]
                dve.wait_ge(cT_hi, b.n * 2 * FILLS + 2 * k + n + 1)
                nc.vector.tensor_tensor(cT[:, LO, k, m0:m0 + cols], pj[:, 0:cols],
                                        cT[:, HI, k, m0:m0 + cols].bitcast(F32), ALU.subtract).then_inc(cT_lo, 1)

            def key_lo(b, n):
                kind, i, half = STEPS[n]
                if kind != "k":
                    return
                m0, cols = SPLIT[half]
                for r in range(2):
                    dve.wait_ge(k_hi, (b.n * NK + k_before(n)) * 2 + r + 1)
                    last = nc.vector.tensor_tensor(
                        kt[b.par][64:P, 2 * i + r, m0:m0 + cols], kw[64 * r:64 * r + 64, k_before(n) % 2, 0:cols],
                        kt[b.par][0:64, 2 * i + r, m0:m0 + cols].bitcast(F32), ALU.subtract)
                last.then_inc(k_ready, 1)

            def value_out(b, n):
                kind, i, half = STEPS[n]
                if kind != "v":
                    return
                dve.wait_ge(proj_done, b.n * NSTEP + n + 1)
                nc.vector.tensor_copy(vn[b.par][0:rows_of(i), i, :], pj[0:rows_of(i), :]).then_inc(v_ready, 1)

            def row_max(b, h):
                dve.wait_ge(scores_done, b.n * HEADS + h + 1)
                nc.vector.tensor_reduce(nmax[:, b.par, h:h + 1], scores(h % 2), AX.XY, ALU.max, negate=True).then_inc(max_ready, 1)

            def turned(b, h):
                dve.wait_ge(p_turned, b.n * HEADS + h + 1)
                if h % 4 == 0:
                    wait(dve, av_done, b.n * QUADS + h // 4 - 1)
                nc.vector.tensor_copy(pT[:, (h // 4) % 2, h % 4, 0:TB, :],
                                      tp[0][:, 0:TB * N].rearrange("p (t n) -> p t n", n=N)).then_inc(pT_ready[0], 1)

            def inverse(b, q):
                quad = b.n * QUADS + q
                dve.wait_ge(exp_done, (quad + 1) * 4)
                wait(dve, av_done, quad - 1)
                nc.vector.reciprocal(inv[:, q % 2], sums[:, b.par, 4 * q:4 * q + 4]).then_inc(inv_ready, 1)
                dve.wait_ge(inv_ready, quad + 1)
                nc.vector.tensor_copy(rexp[:, q % 2], inv[:, q % 2].unsqueeze(2).to_broadcast([N, 4, DH])).then_inc(rexp_ready, 1)

            def scale(b, q):
                quad = b.n * QUADS + q
                dve.wait_ge(rb_ready, quad + 1)
                if q == 0:
                    wait(dve, stored[b.par], b.pair * 16)
                nc.vector.tensor_tensor(at[:, b.par, q, :], av[:, 0:N], rb[:, q % 2, :], ALU.mult).then_inc(at_ready, 1)

            def batch(b, first=False, last=False):
                for h in range(HEADS):
                    row_max(b, h)
                    if not last and h < FILLS:
                        fill_lo(b.next(), h, 0)
                    if h > 0:
                        turned(b, h - 1)
                    elif not first:
                        turned(b.prev(), HEADS - 1)
                    if h % 4 == 0 and h > 0:
                        inverse(b, h // 4 - 1)
                    elif h == 0 and not first:
                        inverse(b.prev(), QUADS - 1)
                    if not last:
                        for n in lo_of_slot[h]:
                            key_lo(b.next(), n)
                        if h < FILLS:
                            fill_lo(b.next(), h, 1)
                    if h == FILLS and not first:
                        key_lo(b, NSTEP - 1)
                    if h % 4 == 1 and h > 1:
                        scale(b, h // 4 - 1)
                    elif h == 1 and not first:
                        scale(b.prev(), QUADS - 1)
                    if not last:
                        for n in by_slot[h]:
                            value_out(b.next(), n)

            nc.vector.memset(tp[1][:, 0:TB * N], 0.0).then_inc(tail_zeroed, 1)
            for k in range(FILLS):
                for n in range(2):
                    fill_lo(Batch(0, 0), k, n)
            for n in range(NSTEP):
                key_lo(Batch(0, 0), n)
                value_out(Batch(0, 0), n)
            all_batches(dve, batch)
            end = Batch(B // 2 - 1, 1)
            turned(end, HEADS - 1)
            inverse(end, QUADS - 1)
            scale(end, QUADS - 1)


def tokens_phase(nc, d, io, keep):
    D, T, F = d.D, d.T, d.F
    DC, TC, FC = D // P, T // P, F // P
    TG = 5
    TOK = TG * P
    GROUPS = d.B * d.N // TOK
    HALF = TOK // 2
    assert GROUPS * TOK == d.B * d.N and HALF <= BANK
    RB = 3
    USES = ([("rows", i) for i in range(TG)] + [("up", n) for n in range(2 * FC)] + [("proj", i) for i in range(TG)]
            + [("qrows", i) for i in range(TG)] + [("query", n) for n in range(2 * TC)])

    def bank_of(use):
        return USES.index(use) % RB

    with ExitStack() as ctx:
        s = Scope(nc, ctx)
        wo, w2 = s.sb("t_wo", [P, 2, DC, D], F32R), s.sb("t_w2", [P, 2, FC, D], F32R)
        aw, w1 = s.sb("t_aw", [P, 2, DC, T], F32R), s.sb("t_w1", [P, 2, 2, DC, P], F32R)
        b2_row = s.sb("t_b2_row", [P, D])
        zn = s.sb("t_zn", [P, TG * D])
        at_in = zn[:].rearrange("p (c n) -> p c n", c=DC)
        z = zn[:].rearrange("p (i n) -> p i n", i=TG)
        wide = s.sb("t_wide", [P, 2, DC, TOK], F32R)
        zT = s.sb("t_zT", [P, 2, DC, TOK], F32R)
        xb, ob = s.sb("t_xb", [P, TG, D]), s.sb("t_ob", [P, TG, D])
        h32, h_hl = s.sb("t_h32", [P, 2, HALF]), s.sb("t_h_hl", [P, 2, 2, TOK], F32R)
        junk = s.sb("t_junk", [P, D])
        st_h, st_q = s.sb("t_st_h", [P, TG, 6]), s.sb("t_st_q", [P, TG, 6])
        mv_h, mv_q = s.sb("t_mv_h", [P, TG, 2]), s.sb("t_mv_q", [P, TG, 2])
        ve_h, ve_q = s.sb("t_ve_h", [P, TG]), s.sb("t_ve_q", [P, TG])
        rs_h, rs_q = s.sb("t_rs_h", [P, TG]), s.sb("t_rs_q", [P, TG])
        cs = s.sb("t_cs", [P, TG])
        acc = [s.psum(f"t_acc{i}", [P, BANK]) for i in range(TG)]
        ring = [s.psum(f"t_ring{i}", [P, BANK]) for i in range(RB)]

        passed = s.sem("t_passed")
        wo_loaded, aw_loaded, w2_loaded = s.sem("t_wo_loaded"), s.sem("t_aw_loaded"), s.sem("t_w2_loaded")
        b2_loaded, w1_loaded, at_loaded, x_loaded = s.sem("t_b2_loaded"), s.sems("t_w1_loaded", 2), s.sem("t_at_loaded"), s.sem("t_x_loaded")
        t_stored, x_stored, c_stored = s.sem("t_t_stored"), s.sem("t_x_stored"), s.sem("t_c_stored")
        rows_done, up_done, proj_done, qrows_done, query_done, down_done = (
            s.sem(f"t_{n}_done") for n in ("rows", "up", "proj", "qrows", "query", "down"))
        at_hi, at_lo, zT_hi, gelu_done, h_hi, h_lo, t_hi = (
            s.sem(f"t_{n}") for n in ("at_hi", "at_lo", "zT_hi", "gelu_done", "h_hi", "h_lo", "t_hi"))
        zT_lo, t_lo = s.sem("t_zT_lo"), s.sem("t_t_lo")
        o_ready, x1_ready, st_h_ready, st_q_ready, mv_h_ready, mv_q_ready = (
            s.sem(f"t_{n}_ready") for n in ("o", "x1", "st_h", "st_q", "mv_h", "mv_q"))
        ve_h_ready, ve_q_ready, rs_h_ready, rs_q_ready = (s.sem(f"t_{n}_ready") for n in ("ve_h", "ve_q", "rs_h", "rs_q"))
        zh_ready, zq_ready, c_ready, xb_ready, xo_ready, x1b_ready = (
            s.sem(f"t_{n}_ready") for n in ("zh", "zq", "c", "xb", "xo", "x1b"))
        block = ctx.enter_context(nc.Block())

        def all_groups(eng, group):
            group(0)
            with eng.Fori(1, GROUPS - 1) as g:
                group(g)
            group(GROUPS - 1, last=True)

        def tile(ap, i):
            return ap[:, P * i:P * (i + 1)]

        @block.sync
        def _(sp):
            def load_at(g):
                wait(sp, rows_done, g * TG)
                sp.dma_start(at_in, keep.attn_dram[:, bass.ds(g * TOK, TOK)].rearrange("(c p) n -> p c n", p=P)).then_inc(at_loaded, 16)

            def load_w1(g, j):
                wait(sp, up_done, g * 2 * FC + 2 * (j - 1))
                sp.dma_start(w1[:, j % 2].bitcast(F32), keep.W1_dram[j]).then_inc(w1_loaded[j % 2], 16)

            def group(g, last=False):
                wait(sp, x_stored, g * 16)
                rows = io.x.rearrange("b n d -> (b n) d")[bass.ds(g * TOK, TOK), :]
                sp.dma_start(xb[:], rows.rearrange("(i p) d -> p i d", p=P)).then_inc(x_loaded, 16)
                if not last:
                    load_at(g + 1)
                for j in range(2, FC):
                    load_w1(g, j)
                if not last:
                    for j in range(2):
                        load_w1(g + 1, j)
                sp.wait_ge(x1b_ready, (g + 1) * TG)
                sp.dma_start(keep.x1_dram[bass.ds(g * TOK, TOK), :].rearrange("(i p) d -> p i d", p=P), xb[:]).then_inc(x_stored, 16)
                wait_alone(sp, c_ready, (g + 1) * TG, passed)
                sp.dma_start(keep.c_dram[bass.ds(g * TOK, TOK), :].rearrange("(i p) o -> p (i o)", p=P), cs[:],
                             allow_slow_non_contiguous=True).then_inc(c_stored, 16)
                sp.wait_ge(t_hi, (g + 1) * 2 * TC)
                sp.wait_ge(t_lo, (g + 1) * 2 * TC)
                for hl in range(2):
                    sp.dma_start(keep.t_dram[hl, :, bass.ds(g * TOK, TOK)].rearrange("(c p) n -> p c n", p=P),
                                 wide[:, hl, 0:TC, :].bitcast(F32)).then_inc(t_stored, 16)

            load_at(0)
            sp.dma_start(wo[:].bitcast(F32), keep.Wo_dram.rearrange("h (c p) n -> p h c n", p=P)).then_inc(wo_loaded, 16)
            for j in range(2):
                load_w1(0, j)
            sp.dma_start(b2_row[:], row(io.b2)).then_inc(b2_loaded, 16)
            sp.dma_start(w2[:].bitcast(F32), keep.W2_dram.rearrange("h (c p) n -> p h c n", p=P)).then_inc(w2_loaded, 16)
            sp.dma_start(aw[:].bitcast(F32), keep.A_dram.rearrange("h (c p) n -> p h c n", p=P)).then_inc(aw_loaded, 16)
            all_groups(sp, group)
            sp.wait_ge(x_stored, 16 * GROUPS)
            sp.wait_ge(c_stored, 16 * GROUPS)
            sp.wait_ge(t_stored, 32 * GROUPS)

        @block.tensor
        def _(pe):
            def bank(g, use, last):
                left = {"rows": (zT_lo, 2 * TG, 1), "up": (gelu_done, 2 * FC, 1), "proj": (o_ready, TG, TG + 1),
                        "qrows": (zT_lo, 2 * TG, TG + 1), "query": (t_lo, 2 * TC, 1)}
                before = [v for v in USES[bank_of(use):USES.index(use):RB] if not (last and v[0] == "proj")]
                if before:
                    kind, n = before[-1]
                    sem, per_group, start = left[kind]
                    pe.wait_ge(sem, g * per_group + start + n)
                else:
                    wait(pe, t_lo, g * 2 * TC)
                return ring[bank_of(use)]

            def project(g, i, first=False):
                if first:
                    wait(pe, o_ready, i - RB + 1)
                out = ring[bank_of(("proj", i))] if first else bank(g, ("proj", i), False)
                for k in range(DC):
                    for x, y in PASSES:
                        last = nc.tensor.matmul(out[:, 0:D], tile(wide[:, x, k, :], i), wo[:, y, k, :],
                                                start=(k, x, y) == (0, HI, HI), stop=(k, x, y) == (DC - 1, LO, HI))
                last.then_inc(proj_done, 1)

            def turn(out, i, done):
                for k in range(DC):
                    last = nc.tensor.transpose(tile(out, k), tile(z[:, i, :], k), keep.ident[:])
                last.then_inc(done, 1)

            def up(g, n, last):
                j, half = n // 2, n % 2
                if half == 0:
                    pe.wait_ge(w1_loaded[j % 2], (g * (FC // 2) + j // 2 + 1) * 16)
                out = bank(g, ("up", n), last)
                for k in range(DC):
                    for x, y in PASSES:
                        ins = nc.tensor.matmul(out[:, 0:HALF], w1[:, j % 2, x, k, :], zT[:, y, k, HALF * half:HALF * (half + 1)],
                                               start=(k, x, y) == (0, HI, HI), stop=(k, x, y) == (DC - 1, LO, HI))
                ins.then_inc(up_done, 1)

            def down(g, j):
                pe.wait_ge(h_lo, g * 2 * FC + 2 * (j + 1))
                pe.wait_ge(h_hi, g * 2 * FC + 2 * (j + 1))
                for i in range(TG):
                    for x, y in PASSES:
                        ins = nc.tensor.matmul(acc[i][:, 0:D], tile(h_hl[:, j % 2, x, :], i), w2[:, y, j, :],
                                               start=(j, x, y) == (0, HI, HI), stop=(j, x, y) == (FC - 1, LO, HI))
                ins.then_inc(down_done, 1)

            def group(g, last=False):
                for i in range(TG):
                    pe.wait_ge(zh_ready, g * TG + i + 1)
                    turn(bank(g, ("rows", i), last), i, rows_done)
                pe.wait_ge(zT_lo, g * 2 * TG + TG)
                wait(pe, x1_ready, g * TG)
                for j in range(FC):
                    for half in range(2):
                        up(g, 2 * j + half, last)
                    if j > 0:
                        down(g, j - 1)
                down(g, FC - 1)
                if not last:
                    pe.wait_ge(at_lo, (g + 2) * DC)
                    for i in range(TG):
                        project(g, i)
                for i in range(TG):
                    pe.wait_ge(zq_ready, g * TG + i + 1)
                    turn(bank(g, ("qrows", i), last), i, qrows_done)
                pe.wait_ge(zT_lo, (g + 1) * 2 * TG)
                for n in range(2 * TC):
                    c, half = n // 2, n % 2
                    out = bank(g, ("query", n), last)
                    for k in range(DC):
                        for x, y in PASSES:
                            ins = nc.tensor.matmul(out[:, 0:HALF], tile(aw[:, x, k, :], c), zT[:, y, k, HALF * half:HALF * (half + 1)],
                                                   start=(k, x, y) == (0, HI, HI), stop=(k, x, y) == (DC - 1, LO, HI))
                    ins.then_inc(query_done, 1)

            pe.wait_ge(wo_loaded, 16)
            pe.wait_ge(at_lo, DC)
            for i in range(TG):
                project(0, i, first=True)
            pe.wait_ge(w2_loaded, 16)
            pe.wait_ge(aw_loaded, 16)
            all_groups(pe, group)

        @block.scalar
        def _(act):
            def attn_hi(g, k):
                act.wait_ge(at_loaded, (g + 1) * 16)
                wait(act, t_stored, (g - 1) * 32)
                nc.scalar.activation(wide[:, HI, k, :], at_in[:, k, :], ACT.Copy).then_inc(at_hi, 1)

            def rows_hi(use, done, count):
                act.wait_ge(done, count)
                nc.scalar.activation(zT[:, HI, :, P * use[1]:P * (use[1] + 1)],
                                     ring[bank_of(use)][:].rearrange("p (c n) -> p c n", c=DC), ACT.Copy).then_inc(zT_hi, 1)

            def gelu(g, n):
                j, half = n // 2, n % 2
                b = bank_of(("up", n))
                act.wait_ge(up_done, g * 2 * FC + n + 1)
                wait(act, h_lo, g * 2 * FC + n - 1)
                nc.scalar.activation(h32[:, half, :], ring[b][:, 0:HALF], ACT.Gelu, bias=keep.b1[:, j:j + 1]).then_inc(gelu_done, 1)
                act.wait_ge(gelu_done, g * 2 * FC + n + 1)
                wait(act, down_done, g * FC + j - 1)
                nc.scalar.activation(h_hl[:, j % 2, HI, HALF * half:HALF * (half + 1)], h32[:, half, :], ACT.Copy).then_inc(h_hi, 1)

            def group(g, last=False):
                for i in range(TG):
                    rows_hi(("rows", i), rows_done, g * TG + i + 1)
                for n in range(2 * FC):
                    gelu(g, n)
                    if not last and n % 4 == 3 and n // 4 >= 4:
                        attn_hi(g + 1, n // 4 - 4)
                for i in range(TG):
                    rows_hi(("qrows", i), qrows_done, g * TG + i + 1)
                for n in range(2 * TC):
                    c, half = n // 2, n % 2
                    act.wait_ge(query_done, g * 2 * TC + n + 1)
                    nc.scalar.activation(wide[:, HI, c, HALF * half:HALF * (half + 1)], ring[bank_of(("query", n))][:, 0:HALF],
                                         ACT.Identity, bias=keep.t_bias[:, c:c + 1]).then_inc(t_hi, 1)

            for k in range(DC):
                attn_hi(0, k)
            all_groups(act, group)

        @block.vector
        def _(dve):
            def attn_lo(g, k):
                dve.wait_ge(at_hi, g * DC + k + 1)
                nc.vector.tensor_tensor(wide[:, LO, k, :], at_in[:, k, :], wide[:, HI, k, :].bitcast(F32), ALU.subtract).then_inc(at_lo, 1)

            def normalise_stats(src, i, st, mv, st_ready, mv_ready, count):
                nc.vector.bn_stats(st[:, i, :], src).then_inc(st_ready, 1)
                wait_alone(dve, st_ready, count, passed)
                nc.vector.bn_aggr(mv[:, i, :], st[:, i, :]).then_inc(mv_ready, 1)

            def rows_out(g, i):
                b = bank_of(("proj", i))
                dve.wait_ge(proj_done, g * TG + i + 1)
                wait(dve, xo_ready, g * TG)
                nc.vector.tensor_tensor(ob[:, i, :], ring[b][:, 0:D], keep.bo_row[:], ALU.add).then_inc(o_ready, 1)
                dve.wait_ge(o_ready, g * TG + i + 1)
                normalise_stats(ob[:, i, :], i, st_h, mv_h, st_h_ready, mv_h_ready, g * TG + i + 1)

            def norm(out, src, i, mv, rs, rs_ready, count, ready):
                dve.wait_ge(rs_ready, count)
                nc.vector.tensor_scalar(out, src, mv[:, i, 0:1], rs[:, i:i + 1], ALU.subtract, ALU.mult).then_inc(ready, 1)

            def rows_lo(use, hi_count):
                dve.wait_ge(zT_hi, hi_count)
                nc.vector.tensor_tensor(zT[:, LO, :, P * use[1]:P * (use[1] + 1)],
                                        ring[bank_of(use)][:].rearrange("p (c n) -> p c n", c=DC),
                                        zT[:, HI, :, P * use[1]:P * (use[1] + 1)].bitcast(F32), ALU.subtract).then_inc(zT_lo, 1)

            def norm_h(g, i):
                norm(z[:, i, :], ob[:, i, :], i, mv_h, rs_h, rs_h_ready, g * TG + i + 1, zh_ready)

            def x1_out(g, i):
                nc.vector.tensor_tensor(xb[:, i, :], acc[i][:, 0:D], xb[:, i, :], ALU.add).then_inc(x1_ready, 1)
                dve.wait_ge(x1_ready, g * TG + i + 1)
                normalise_stats(xb[:, i, :], i, st_q, mv_q, st_q_ready, mv_q_ready, g * TG + i + 1)

            def group(g, last=False):
                for i in range(TG):
                    rows_lo(("rows", i), g * 2 * TG + i + 1)
                for n in range(2 * FC):
                    j, half = n // 2, n % 2
                    dve.wait_ge(h_hi, g * 2 * FC + n + 1)
                    part = slice(HALF * half, HALF * (half + 1))
                    nc.vector.tensor_tensor(h_hl[:, j % 2, LO, part], h32[:, half, :], h_hl[:, j % 2, HI, part].bitcast(F32),
                                            ALU.subtract).then_inc(h_lo, 1)
                    if not last and n % 4 == 3 and n // 4 >= 4:
                        attn_lo(g + 1, n // 4 - 4)
                dve.wait_ge(down_done, (g + 1) * FC)
                dve.wait_ge(xo_ready, (g + 1) * TG)
                for i in range(TG + 1):
                    if i < TG:
                        x1_out(g, i)
                        if not last:
                            rows_out(g + 1, i)
                    if i > 0:
                        norm(z[:, i - 1, :], xb[:, i - 1, :], i - 1, mv_q, rs_q, rs_q_ready, g * TG + i, zq_ready)
                wait(dve, c_stored, g * 16)
                for i in range(TG):
                    if i == 0:
                        dve.wait_ge(zq_ready, (g + 1) * TG)
                    rows_lo(("qrows", i), g * 2 * TG + TG + i + 1)
                    wait(dve, c_ready, g * TG + i)
                    nc.vector.tensor_tensor_reduce(out=junk[:], in0=z[:, i, :], in1=keep.score_row[:], scale=1.0,
                                                   scalar=keep.score_const[:], op0=ALU.mult, op1=ALU.add,
                                                   accum_out=cs[:, i:i + 1]).then_inc(c_ready, 1)
                    if not last:
                        dve.wait_ge(c_ready, g * TG + i + 1)
                        norm_h(g + 1, i)
                for n in range(2 * TC):
                    c, half = n // 2, n % 2
                    part = slice(HALF * half, HALF * (half + 1))
                    dve.wait_ge(t_hi, g * 2 * TC + n + 1)
                    nc.vector.scalar_tensor_tensor(out=wide[:, LO, c, part], in0=ring[bank_of(("query", n))][:, 0:HALF],
                                                   scalar=keep.t_bias[:, c:c + 1], in1=wide[:, HI, c, part].bitcast(F32),
                                                   op0=ALU.add, op1=ALU.subtract).then_inc(t_lo, 1)

            for k in range(DC):
                attn_lo(0, k)
            for i in range(TG):
                rows_out(0, i)
            dve.wait_ge(at_lo, DC)
            for i in range(TG):
                norm_h(0, i)
            all_groups(dve, group)

        @block.gpsimd
        def _(pool):
            def inverse_std(mv, ve, rs, i, mv_ready, ve_ready, rs_ready, count):
                wait_alone(pool, mv_ready, count, passed)
                nc.gpsimd.tensor_scalar(ve[:, i:i + 1], mv[:, i, 1:2], EPS, 1.0, ALU.add, ALU.mult).then_inc(ve_ready, 1)
                pool.wait_ge(ve_ready, count)
                nc.gpsimd.tensor_tensor(rs[:, i:i + 1], ve[:, i:i + 1], keep.minus_half[:, 0:1], ALU.pow).then_inc(rs_ready, 1)

            def group(g, last=False):
                pool.wait_ge(x_loaded, (g + 1) * 16)
                for i in range(TG):
                    nc.gpsimd.tensor_tensor(xb[:, i, :], xb[:, i, :], b2_row[:], ALU.add).then_inc(xb_ready, 1)
                for i in range(TG):
                    pool.wait_ge(xb_ready, g * TG + i + 1)
                    pool.wait_ge(o_ready, g * TG + i + 1)
                    nc.gpsimd.tensor_tensor(xb[:, i, :], xb[:, i, :], ob[:, i, :], ALU.add).then_inc(xo_ready, 1)
                for i in range(TG):
                    inverse_std(mv_q, ve_q, rs_q, i, mv_q_ready, ve_q_ready, rs_q_ready, g * TG + i + 1)
                    if not last:
                        inverse_std(mv_h, ve_h, rs_h, i, mv_h_ready, ve_h_ready, rs_h_ready, (g + 1) * TG + i + 1)
                for i in range(TG):
                    pool.wait_ge(zq_ready, g * TG + i + 1)
                    nc.gpsimd.tensor_tensor(xb[:, i, :], xb[:, i, :], keep.bd_row[:], ALU.add).then_inc(x1b_ready, 1)

            pool.wait_ge(b2_loaded, 16)
            for i in range(TG):
                inverse_std(mv_h, ve_h, rs_h, i, mv_h_ready, ve_h_ready, rs_h_ready, i + 1)
            all_groups(pool, group)


def attention1_phase(nc, d, io, keep):
    B, N, M, T, E = d.B, d.N, d.M, d.T, d.E
    TC = T // P
    MT = -(-M // P)
    LAST = M - P * (MT - 1)
    TB = MT // 2
    SPLIT = ((0, TB * P), (TB * P, M - TB * P))
    MH = M // 2
    SW = MH + 1
    FILLS = 2 * TC

    def rows_of(t):
        return LAST if t == MT - 1 else P

    with ExitStack() as ctx:
        s = Scope(nc, ctx)
        bw = s.sb("b_bw", [P, 2, TC, E], F32R)
        cn = [s.sb(f"b_cn{i}", [P, MT, T]) for i in range(4)]
        xk = [s.sb(f"b_xk{i}", [P, MT, T]) for i in range(4)]
        xT = [s.sb(f"b_xT{i}", [P, 2, TC, M], F32R) for i in range(2)]
        tq = [s.sb(f"b_tq{i}", [P, 2, TC, N], F32R) for i in range(2)]
        cst, x1 = s.sb("b_cst", [N, 2]), s.sb("b_x1", [N, 2, E])
        st, mv = s.sb("b_st", [P, 2, MT, 6]), s.sb("b_mv", [P, 2, MT, 2])
        ve, neg, rs, shift = (s.sb(f"b_{n}", [P, 2, MT]) for n in ("ve", "neg", "rs", "shift"))
        nmax, bias, sums, inv = (s.sb(f"b_{n}", [N, 2]) for n in ("nmax", "bias", "sums", "inv"))
        pr, pT = s.sb("b_pr", [N, 2, M]), s.sb("b_pT", [P, 2, MT, N])
        uT = s.sb("b_uT", [P, 2, 2, TC * N], F32R)
        y, out = s.sb("b_y", [N, 2, E]), s.sb("b_out", [N, 2, E])
        sc = s.psum("b_sc", [P, 3 * BANK])
        tp = [s.psum(f"b_tp{i}", [P, BANK]) for i in range(2)]
        tt = [s.psum(f"b_tt{i}", [P, BANK]) for i in range(2)]
        ff = s.psum("b_ff", [P, BANK])
        uu = sc[:, 2 * BANK:3 * BANK]
        scores = sc[0:N, 0:2 * (BANK + 1)].rearrange("p (c n) -> p c n", c=2)[:, :, 0:MH]

        passed = s.sem("b_passed")
        b_loaded, ctx_loaded, t_loaded = s.sem("b_b_loaded"), s.sems("b_ctx_loaded", 4), s.sems("b_t_loaded", 2)
        x1_loaded, out_stored = s.sems("b_x1_loaded", 2), s.sems("b_out_stored", 2)
        zeroed, tail_zeroed = s.sem("b_zeroed"), s.sem("b_tail_zeroed")
        st_ready, mv_ready, ve_ready, neg_ready, rs_ready, shift_ready, xk_ready = (
            s.sem(f"b_{n}_ready") for n in ("st", "mv", "ve", "neg", "rs", "shift", "xk"))
        filled, xT_hi, xT_lo = s.sem("b_filled"), s.sem("b_xT_hi"), s.sem("b_xT_lo")
        scores_done, max_ready, bias_ready, exp_done = (s.sem(f"b_{n}") for n in ("scores_done", "max_ready", "bias_ready", "exp_done"))
        part_ready, inv_ready = s.sem("b_part_ready"), s.sem("b_inv_ready")
        p_turned, pT_ready = s.sem("b_p_turned"), s.sems("b_pT_ready", 2)
        values_done, uT_hi, uT_lo = s.sem("b_values_done"), s.sem("b_uT_hi"), s.sem("b_uT_lo")
        final_done, y_ready, out_ready = s.sem("b_final_done"), s.sem("b_y_ready"), s.sem("b_out_ready")
        block = ctx.enter_context(nc.Block())

        def all_batches(eng, batch):
            for slot in range(4):
                batch(QuadBatch(0, slot), first=slot == 0)
            with eng.Fori(1, B // 4 - 1) as quad:
                for slot in range(4):
                    batch(QuadBatch(quad, slot))
            for slot in range(4):
                batch(QuadBatch(B // 4 - 1, slot), last=slot == 3)

        def exists(b):
            return not isinstance(b.n, int) or b.n < B

        end = QuadBatch(B // 4 - 1, 3)

        @block.sync
        def _(sp):
            def load_ctx(b):
                wait(sp, xk_ready, (b.n - 3) * MT)
                src = io.ctx[bass.ds(b.n, 1), :, :].rearrange("b m t -> (b m) t")
                whole = P * (MT - 1)
                sp.dma_start(cn[b.slot][:, 0:MT - 1, :], src[0:whole, :].rearrange("(t p) d -> p t d", p=P)).then_inc(ctx_loaded[b.slot], 16)
                sp.dma_start(cn[b.slot][0:LAST, MT - 1, :], src[whole:M, :]).then_inc(ctx_loaded[b.slot], 16)

            def load_rows(b):
                wait(sp, scores_done, b.n - 1)
                for hl in range(2):
                    sp.dma_start(tq[b.par][:, hl].bitcast(F32),
                                 keep.t_dram[hl, :, bass.ds(b.n * N, N)].rearrange("(c p) n -> p c n", p=P)).then_inc(t_loaded[b.par], 16)
                wait(sp, bias_ready, b.n - 1)
                sp.dma_start(cst[:, b.par:b.par + 1], keep.c_dram[bass.ds(b.n * N, N), :],
                             allow_slow_non_contiguous=True).then_inc(t_loaded[b.par], 16)
                wait(sp, out_ready, b.n - 1)
                sp.dma_start(x1[:, b.par, :], keep.x1_dram[bass.ds(b.n * N, N), :]).then_inc(x1_loaded[b.par], 16)

            def store(b):
                sp.wait_ge(out_ready, b.n + 1)
                sp.dma_start(io.out.rearrange("b n d -> (b n) d")[bass.ds(b.n * N, N), :], out[:, b.par, :]).then_inc(out_stored[b.par], 16)

            def batch(b, first=False, last=False):
                if exists(b.after(4)):
                    load_ctx(b.after(4))
                if not last:
                    load_rows(b.after(1))
                if not first:
                    store(b.after(-1))

            load_ctx(QuadBatch(0, 0))
            load_rows(QuadBatch(0, 0))
            load_ctx(QuadBatch(0, 1))
            sp.dma_start(bw[:].bitcast(F32), keep.B_dram.rearrange("h (c p) n -> p h c n", p=P)).then_inc(b_loaded, 16)
            for slot in range(2, 4):
                load_ctx(QuadBatch(0, slot))
            all_batches(sp, batch)
            store(end)
            for par in range(2):
                sp.wait_ge(out_stored[par], 16 * (B // 2))

        @block.gpsimd
        def _(pool):
            def inverse_std(b):
                wait_alone(pool, mv_ready, (b.n + 1) * MT, passed)
                nc.gpsimd.tensor_scalar(ve[:, b.par, :], mv[:, b.par, :, 1], EPS, 1.0, ALU.add, ALU.mult).then_inc(ve_ready, 1)
                nc.gpsimd.tensor_scalar(neg[:, b.par, :], mv[:, b.par, :, 0], -1.0, 0.0, ALU.mult, ALU.add).then_inc(neg_ready, 1)
                pool.wait_ge(ve_ready, b.n + 1)
                wait(pool, xk_ready, (b.n - 1) * MT)
                nc.gpsimd.tensor_tensor(rs[:, b.par, :], ve[:, b.par, :], keep.minus_half[:, 0:MT], ALU.pow).then_inc(rs_ready, 1)
                pool.wait_ge(rs_ready, b.n + 1)
                pool.wait_ge(neg_ready, b.n + 1)
                nc.gpsimd.tensor_tensor(shift[:, b.par, :], neg[:, b.par, :], rs[:, b.par, :], ALU.mult).then_inc(shift_ready, 1)

            def add(b):
                pool.wait_ge(y_ready, b.n + 1)
                pool.wait_ge(x1_loaded[b.par], (b.pair + 1) * 16)
                wait(pool, out_stored[b.par], b.pair * 16)
                nc.gpsimd.tensor_tensor(out[:, b.par, :], y[:, b.par, :], x1[:, b.par, :], ALU.add).then_inc(out_ready, 1)

            def batch(b, first=False, last=False):
                if exists(b.after(3)):
                    inverse_std(b.after(3))
                if not first:
                    add(b.after(-1))

            nc.gpsimd.memset(mv[:], 1.0).then_inc(zeroed, 1)
            for slot in range(3):
                inverse_std(QuadBatch(0, slot))
            all_batches(pool, batch)
            add(end)

        @block.tensor
        def _(pe):
            def fill(b, k):
                if k == 0:
                    pe.wait_ge(xk_ready, (b.n + 1) * MT)
                for n in range(2):
                    wait(pe, xT_lo, b.n * FILLS + 2 * k + n - 1)
                    for t in range(TB * n, TB * (n + 1)):
                        at0, rows = P * (t - TB * n), rows_of(t)
                        last = nc.tensor.transpose(tp[n][:, at0:at0 + rows], xk[b.slot][0:rows, t, P * k:P * (k + 1)],
                                                   keep.ident[0:rows, 0:rows])
                    last.then_inc(filled, 1)

            def score(b):
                pe.wait_ge(t_loaded[b.par], (b.pair + 1) * 48)
                wait(pe, exp_done, b.n)
                for k in range(TC):
                    pe.wait_ge(xT_lo, b.n * FILLS + 2 * (k + 1))
                    for n in range(2):
                        m0 = n * (MH - 1)
                        for x, y_ in PASSES:
                            last = nc.tensor.matmul(sc[0:N, n * BANK:n * BANK + SW], tq[b.par][:, x, k, :],
                                                    xT[b.par][:, y_, k, m0:m0 + SW],
                                                    start=(k, x, y_) == (0, HI, HI), stop=(k, x, y_) == (TC - 1, LO, HI))
                last.then_inc(scores_done, 1)

            def turn(b):
                pe.wait_ge(exp_done, b.n + 1)
                pe.wait_ge(tail_zeroed, 1)
                for n in range(2):
                    wait(pe, pT_ready[n], b.n)
                    for t in range(TB * n, TB * (n + 1)):
                        at0 = N * (t - TB * n)
                        last = nc.tensor.transpose(tt[n][0:rows_of(t), at0:at0 + N], pr[:, b.par, P * t:P * t + rows_of(t)],
                                                   keep.ident[0:N, 0:N])
                last.then_inc(p_turned, 1)

            def values(b):
                for n in range(2):
                    pe.wait_ge(pT_ready[n], b.n + 1)
                wait(pe, uT_lo, b.n)
                for k in range(TC):
                    for t in range(MT):
                        last = nc.tensor.matmul(uu[:, N * k:N * (k + 1)], xk[b.slot][0:rows_of(t), t, P * k:P * (k + 1)],
                                                pT[0:rows_of(t), b.par, t, :], start=t == 0, stop=t == MT - 1)
                last.then_inc(values_done, 1)

            def final(b):
                pe.wait_ge(uT_lo, b.n + 1)
                wait(pe, y_ready, b.n)
                for k in range(TC):
                    for x, y_ in PASSES:
                        last = nc.tensor.matmul(ff[0:N, 0:E], uT[:, b.par, x, N * k:N * (k + 1)], bw[:, y_, k, :],
                                                start=(k, x, y_) == (0, HI, HI), stop=(k, x, y_) == (TC - 1, LO, HI))
                last.then_inc(final_done, 1)

            def batch(b, first=False, last=False):
                score(b)
                if not last:
                    fill(b.after(1), 0)
                if not first:
                    values(b.after(-1))
                if not last:
                    fill(b.after(1), 1)
                turn(b)
                if not first:
                    final(b.after(-1))
                if not last:
                    for k in range(2, TC):
                        fill(b.after(1), k)

            pe.wait_ge(b_loaded, 16)
            for k in range(TC):
                fill(QuadBatch(0, 0), k)
            all_batches(pe, batch)
            values(end)
            final(end)

        @block.scalar
        def _(act):
            def fill_hi(b, k):
                wait(act, scores_done, b.n - 1)
                for n, (m0, cols) in enumerate(SPLIT):
                    act.wait_ge(filled, b.n * FILLS + 2 * k + n + 1)
                    nc.scalar.activation(xT[b.par][:, HI, k, m0:m0 + cols], tp[n][:, 0:cols], ACT.Copy).then_inc(xT_hi, 1)

            def exp(b):
                act.wait_ge(bias_ready, b.n + 1)
                wait(act, p_turned, b.n - 1)
                nc.scalar.activation(pr[:, b.par, :].rearrange("n (c m) -> n c m", c=2), scores, ACT.Exp,
                                     bias=bias[:, b.par:b.par + 1], accum_out=sums[:, b.par:b.par + 1]).then_inc(exp_done, 1)

            def turned(b):
                act.wait_ge(p_turned, b.n + 1)
                for n in range(2):
                    nc.scalar.activation(pT[:, b.par, TB * n:TB * (n + 1), :],
                                         tt[n][:, 0:TB * N].rearrange("p (t n) -> p t n", n=N), ACT.Copy).then_inc(pT_ready[n], 1)

            def values_hi(b):
                act.wait_ge(values_done, b.n + 1)
                wait(act, final_done, b.n - 1)
                nc.scalar.activation(uT[:, b.par, HI, :], uu[:, 0:TC * N], ACT.Copy).then_inc(uT_hi, 1)

            def normalise(b):
                act.wait_ge(final_done, b.n + 1)
                act.wait_ge(inv_ready, b.n + 1)
                wait(act, out_ready, b.n - 1)
                nc.scalar.activation(y[:, b.par, :], ff[0:N, 0:E], ACT.Copy, scale=inv[:, b.par:b.par + 1]).then_inc(y_ready, 1)

            def layer_norm(b, tiles):
                act.wait_ge(shift_ready, b.n + 1)
                for t in tiles:
                    rows = rows_of(t)
                    wait(act, values_done, b.n - 3)
                    nc.scalar.activation(xk[b.slot][0:rows, t, :], cn[b.slot][0:rows, t, :], ACT.Identity,
                                         bias=shift[0:rows, b.par, t:t + 1], scale=rs[0:rows, b.par, t:t + 1]).then_inc(xk_ready, 1)

            def batch(b, first=False, last=False):
                if not last:
                    fill_hi(b.after(1), 0)
                exp(b)
                if exists(b.after(2)):
                    layer_norm(b.after(2), range(0, TB))
                if not first:
                    values_hi(b.after(-1))
                if not last:
                    fill_hi(b.after(1), 1)
                turned(b)
                if exists(b.after(2)):
                    layer_norm(b.after(2), range(TB, MT))
                if not first:
                    normalise(b.after(-1))
                if not last:
                    for k in range(2, TC):
                        fill_hi(b.after(1), k)

            layer_norm(QuadBatch(0, 0), range(MT))
            for k in range(TC):
                fill_hi(QuadBatch(0, 0), k)
            layer_norm(QuadBatch(0, 1), range(MT))
            act.wait_ge(tail_zeroed, 1)
            all_batches(act, batch)
            values_hi(end)
            normalise(end)

        @block.vector
        def _(dve):
            def stats(b, tiles):
                dve.wait_ge(ctx_loaded[b.slot], (b.quad + 1) * 32)
                for t in tiles:
                    nc.vector.bn_stats(st[0:rows_of(t), b.par, t, :], cn[b.slot][0:rows_of(t), t, :]).then_inc(st_ready, 1)

            def combine(b):
                wait(dve, shift_ready, b.n - 1)
                for t in range(MT):
                    wait_alone(dve, st_ready, b.n * MT + t + 1, passed)
                    nc.vector.bn_aggr(mv[0:rows_of(t), b.par, t, :], st[0:rows_of(t), b.par, t, :]).then_inc(mv_ready, 1)

            def fill_lo(b, k):
                for n, (m0, cols) in enumerate(SPLIT):
                    dve.wait_ge(xT_hi, b.n * FILLS + 2 * k + n + 1)
                    nc.vector.tensor_tensor(xT[b.par][:, LO, k, m0:m0 + cols], tp[n][:, 0:cols],
                                            xT[b.par][:, HI, k, m0:m0 + cols].bitcast(F32), ALU.subtract).then_inc(xT_lo, 1)

            def row_bias(b):
                p = slice(b.par, b.par + 1)
                dve.wait_ge(scores_done, b.n + 1)
                nc.vector.tensor_reduce(nmax[:, p], scores, AX.XY, ALU.max, negate=True).then_inc(max_ready, 1)
                dve.wait_ge(max_ready, b.n + 1)
                nc.vector.tensor_scalar(bias[:, p], nmax[:, p], cst[:, p], cst[:, p], ALU.subtract, ALU.add).then_inc(bias_ready, 1)

            def inverse(b):
                dve.wait_ge(exp_done, b.n + 1)
                nc.vector.reciprocal(inv[:, b.par:b.par + 1], sums[:, b.par:b.par + 1]).then_inc(inv_ready, 1)

            def values_lo(b):
                dve.wait_ge(uT_hi, b.n + 1)
                nc.vector.tensor_tensor(uT[:, b.par, LO, :], uu[:, 0:TC * N], uT[:, b.par, HI, :].bitcast(F32), ALU.subtract).then_inc(uT_lo, 1)

            def batch(b, first=False, last=False):
                row_bias(b)
                if not last:
                    fill_lo(b.after(1), 0)
                if exists(b.after(3)):
                    stats(b.after(3), range(0, TB))
                if not first:
                    values_lo(b.after(-1))
                if not last:
                    fill_lo(b.after(1), 1)
                if exists(b.after(3)):
                    stats(b.after(3), range(TB, MT))
                    combine(b.after(3))
                inverse(b)
                if not last:
                    for k in range(2, TC):
                        fill_lo(b.after(1), k)

            nc.vector.memset(tt[1][:, 0:TB * N], 0.0).then_inc(tail_zeroed, 1)
            dve.wait_ge(zeroed, 1)
            for slot in range(2):
                stats(QuadBatch(0, slot), range(MT))
                combine(QuadBatch(0, slot))
            for k in range(TC):
                fill_lo(QuadBatch(0, 0), k)
            stats(QuadBatch(0, 2), range(MT))
            combine(QuadBatch(0, 2))
            all_batches(dve, batch)
            values_lo(end)


def cross_attention_kernel(nc, io):
    d = Shapes(io)
    B, N, D, M, T = d.B, d.N, d.D, d.M, d.T
    tokens = B * N
    keep = Kept()

    def dram(name, shape):
        return nc.dram_tensor(name, shape, F32, kind="Internal").ap()

    keep.A_dram = dram("folded_A", (2, D, T))
    keep.B_dram = dram("folded_B", (2, T, d.E))
    keep.Wo_dram = dram("Wo_parts", (2, D, D))
    keep.W1_dram = dram("W1_parts", (d.F // P, P, 2, D // P, P))
    keep.W2_dram = dram("W2_parts", (2, d.F, D))
    keep.q_dram = dram("queries", (2, D, tokens))
    keep.attn_dram = dram("attention", (D, tokens))
    keep.x1_dram = dram("x1", (tokens, D))
    keep.t_dram = dram("folded_queries", (2, T, tokens))
    keep.c_dram = dram("score_consts", (tokens, 1))
    with ExitStack() as ctx:
        s = Scope(nc, ctx)
        keep.ident = s.sb("ident", [P, P])
        keep.minus_half = s.sb("minus_half", [P, 8])
        keep.score_row, keep.score_const = s.sb("score_row", [P, D]), s.sb("score_const", [P, 1])
        keep.bd_row, keep.bo_row = s.sb("bd_row", [P, d.E]), s.sb("bo_row", [P, D])
        keep.t_bias = s.sb("t_bias", [P, T // P])
        keep.b1 = s.sb("b1_folded", [P, d.F // P])
        fold_phase(nc, d, io, keep)
        with ExitStack() as inner:
            s = Scope(nc, inner)
            keep.wk_hl = s.sb("wk_hl", [P, 2, T // P, D], F32R)
            keep.wv_hl = s.sb("wv_hl", [P, 2, T // P, D], F32R)
            keep.bk0 = s.sb("bk0", [P, D // P])
            queries_phase(nc, d, io, keep)
            attention_phase(nc, d, io, keep)
        tokens_phase(nc, d, io, keep)
        attention1_phase(nc, d, io, keep)


NAMES = ["x", "ctx_768"] + [f"L0_xattn_{n}" for n in (
    "Wq", "bq", "Wk", "bk", "Wv", "bv", "Wo", "bo", "ln_g", "ln_b", "W1", "b1", "W2", "b2")] + [
    f"L1_xattn_{n}" for n in ("Wq", "bq", "Wk", "bk", "Wv", "bv", "Wd", "bd", "g_q", "be_q", "g_kv", "be_kv")]


def kernel(**inputs):
    import numpy as _np
    import concourse.bacc as _bacc
    from concourse import mybir as _mybir
    from concourse.bass_utils import run_bass_kernel_spmd as _run

    nc = _bacc.Bacc("TRN2", target_bir_lowering=False, num_devices=1)
    arrays, aps = {}, {}
    for name in NAMES:
        a = _np.ascontiguousarray(inputs[name])
        arrays[f"in_{name}_dram"] = a
        aps[name] = nc.dram_tensor(f"in_{name}_dram", a.shape, _mybir.dt.from_np(a.dtype), kind="ExternalInput").ap()
    x = arrays["in_x_dram"]
    aps["out"] = nc.dram_tensor("out_0_dram", x.shape, _mybir.dt.from_np(x.dtype), kind="ExternalOutput").ap()
    cross_attention_kernel(nc, Inputs(aps))
    r = _run(nc, [arrays], core_ids=[0])
    return r.results[0]["out_0_dram"]
```

```python
from contextlib import ExitStack

import concourse.bass as bass
from concourse import mybir

F32 = mybir.dt.float32
F32R = mybir.dt.float32r
ALU = mybir.AluOpType
ACT = mybir.ActivationFunctionType
AX = mybir.AxisListType

P = 128
BANK = 512
EPS = 1e-5
HEADS = 16
HI, LO = 0, 1
PER_STEP = 4
PASSES = ((HI, HI), (HI, LO), (LO, HI))


def wait(eng, sem, value):
    if isinstance(value, int) and value <= 0:
        return
    eng.wait_ge(sem, value)


def wait_alone(eng, sem, value, passed):
    wait(eng, sem, value)
    eng.sem_inc(passed, 1)


class Inputs:

    def __init__(self, t):
        self.x, self.ctx = t["x"], t["ctx_768"]
        self.Wq0, self.bq0, self.Wk0, self.bk0 = (t[f"L0_xattn_{n}"] for n in ("Wq", "bq", "Wk", "bk"))
        self.Wv0, self.bv0, self.Wo, self.bo = (t[f"L0_xattn_{n}"] for n in ("Wv", "bv", "Wo", "bo"))
        self.ln_g, self.ln_b, self.W1, self.b1 = (t[f"L0_xattn_{n}"] for n in ("ln_g", "ln_b", "W1", "b1"))
        self.W2, self.b2 = t["L0_xattn_W2"], t["L0_xattn_b2"]
        self.Wq1, self.bq1, self.Wk1, self.bk1 = (t[f"L1_xattn_{n}"] for n in ("Wq", "bq", "Wk", "bk"))
        self.Wv1, self.bv1, self.Wd, self.bd = (t[f"L1_xattn_{n}"] for n in ("Wv", "bv", "Wd", "bd"))
        self.g_q, self.be_q, self.g_kv, self.be_kv = (t[f"L1_xattn_{n}"] for n in ("g_q", "be_q", "g_kv", "be_kv"))
        self.out = t["out"]


class Shapes:
    def __init__(self, io):
        self.B, self.N, self.D = io.x.shape
        _, self.M, self.T = io.ctx.shape
        self.E, self.F = io.Wq1.shape[0], io.W1.shape[1]
        self.SCALE = float(self.D // HEADS) ** -0.5


class Kept:
    pass


class Scope:

    def __init__(self, nc, ctx):
        self.nc, self.ctx = nc, ctx

    def sb(self, name, shape, dt=F32):
        return self.ctx.enter_context(self.nc.sbuf_tensor(name, shape, dt))

    def psum(self, name, shape):
        return self.ctx.enter_context(self.nc.psum_tensor(name, shape, F32))

    def sem(self, name):
        return self.ctx.enter_context(self.nc.semaphore(name))

    def sems(self, name, n):
        return [self.sem(f"{name}{i}") for i in range(n)]


class Batch:

    def __init__(self, pair, par):
        self.pair, self.par = pair, par
        self.n = pair * 2 + par

    def next(self):
        return Batch(self.pair, 1) if self.par == 0 else Batch(self.pair + 1, 0)

    def prev(self):
        return Batch(self.pair, 0) if self.par == 1 else Batch(self.pair - 1, 1)


class QuadBatch:

    def __init__(self, quad, slot):
        self.quad, self.slot, self.par = quad, slot, slot % 2
        self.n = quad * 4 + slot
        self.pair = quad * 2 + slot // 2

    def after(self, steps):
        slot = self.slot + steps
        return QuadBatch(self.quad + slot // 4, slot % 4)


def column(ap):
    return ap.rearrange("(c p) -> p c", p=P)


def row(ap):
    return ap.partition_broadcast(P)


def chunks(ap):
    return ap.rearrange("(c p) n -> p c n", p=P)


def load_x_rows(sp, io, keep, i):
    N = io.x.shape[1]
    rows = io.x.rearrange("b n d -> (b n) d")[bass.ds(i.n * PER_STEP * N, PER_STEP * N), :]
    sp.dma_start(keep.xn[:, i.par], rows.rearrange("(t p) d -> p t d", p=N)).then_inc(keep.x_loads[i.par], 16)


def fold_phase(nc, d, io, keep):
    D, T, E = d.D, d.T, d.E
    DC, TC, EC = D // P, T // P, E // P
    with ExitStack() as ctx:
        s = Scope(nc, ctx)
        wq, wk, wv = s.sb("f_wq", [P, EC, D]), s.sb("f_wk", [P, EC, T]), s.sb("f_wv", [P, EC, T])
        wd, wdT = s.sb("f_wd", [P, EC, E]), s.sb("f_wdT", [P, EC, E])
        wo0 = s.sb("f_wo0", [P, DC, D])
        gkv_row, bekv_row = s.sb("f_gkv_row", [P, T]), s.sb("f_bekv_row", [P, T])
        gq_row, beq_row = s.sb("f_gq_row", [P, D]), s.sb("f_beq_row", [P, D])
        bd_row, bo_row = s.sb("f_bd_row", [P, E]), s.sb("f_bo_row", [P, D])
        gq, gkv, beq = s.sb("f_gq", [P, DC]), s.sb("f_gkv", [P, TC]), s.sb("f_beq", [P, DC])
        bq, bk, bv, bv0 = (s.sb(f"f_b{n}", [P, EC]) for n in ("q", "k", "v", "v0"))
        bks, bvs = s.sb("f_bks", [P, EC]), s.sb("f_bvs", [P, EC])
        junk = s.sb("f_junk", [P, D])
        bks_wide, bvs_wide, bv0_wide = (s.sb(f"f_{n}_wide", [P, EC, P]) for n in ("bks", "bvs", "bv0"))
        a_raw, a_s = s.sb("f_a_raw", [P, DC, T]), s.sb("f_a_s", [P, DC, T])
        a_hl, b_hl = s.sb("f_a_hl", [P, 2, DC, T], F32R), s.sb("f_b_hl", [P, 2, TC, E], F32R)
        b_s = s.sb("f_b_s", [P, TC, E])
        u, csum = s.sb("f_u", [P, D]), s.sb("f_csum", [P, 1])
        ps = [s.psum(f"f_ps{i}", [P, BANK]) for i in range(8)]
        wd_load, wqk_load, wv_load, wo_load = (s.sem(f"f_{n}_load") for n in ("wd", "wqk", "wv", "wo"))
        loads, stores = s.sem("f_loads"), s.sem("f_stores")
        sums_ready = s.sem("f_sums_ready")
        wide_ready = s.sem("f_wide_ready")
        wdT_in_psum, wdT_ready = s.sem("f_wdT_in_psum"), s.sem("f_wdT_ready")
        a_in_psum, a_copied = s.sem("f_a_in_psum"), s.sem("f_a_copied")
        a_scaled, ab_hi, ab_lo = s.sem("f_a_scaled"), s.sem("f_ab_hi"), s.sem("f_ab_lo")
        b_in_psum, b_scaled = s.sem("f_b_in_psum"), s.sem("f_b_scaled")
        rows_in_psum, u_ready, rows_done = s.sem("f_rows_in_psum"), s.sem("f_u_ready"), s.sem("f_rows_done")
        ident_ready = s.sem("f_ident_ready")
        block = ctx.enter_context(nc.Block())
        raw0 = s.sb("f_raw0", [P, 2, DC * D])
        LAYER0 = ((io.Wq0, keep.wq_hl), (io.Wk0, keep.wk_hl), (io.Wv0, keep.wv_hl))
        raw0_loaded, hl0_hi, hl0_lo = s.sems("f_raw0_loaded", 2), s.sem("f_hl0_hi"), s.sem("f_hl0_lo")
        VECTORS = ((gkv_row, row(io.g_kv)), (bekv_row, row(io.be_kv)), (gq_row, row(io.g_q)),
                   (beq_row, row(io.be_q)), (bd_row, row(io.bd)), (bo_row, row(io.bo)),
                   (gq, column(io.g_q)), (gkv, column(io.g_kv)), (beq, column(io.be_q)),
                   (bq, column(io.bq1)), (bk, column(io.bk1)), (bv, column(io.bv1)), (bv0, column(io.bv0)), (keep.bq0, column(io.bq0)),
                   (keep.bk0, column(io.bk0)))
        ALL_LOADS = 16 * len(VECTORS)

        @block.sync
        def _(sp):
            def load_layer0(n):
                w, hl = LAYER0[n]
                wait(sp, hl0_lo, n - 1)
                sp.dma_start(raw0[:, n % 2, 0:(w.shape[0] // P) * D].rearrange("p (c n) -> p c n", n=D), chunks(w)).then_inc(raw0_loaded[n % 2], 16)

            for t, w, loaded in ((wd, io.Wd, wd_load), (wq, io.Wq1, wqk_load), (wk, io.Wk1, wqk_load), (wv, io.Wv1, wv_load)):
                sp.dma_start(t[:], chunks(w)).then_inc(loaded, 16)
            for t, v in VECTORS:
                sp.dma_start(t[:], v, allow_slow_non_contiguous=True).then_inc(loads, 16)
            sp.dma_start(wo0[:], chunks(io.Wo)).then_inc(wo_load, 16)
            for n in range(len(LAYER0) - 1):
                load_layer0(n)
            for par in range(2):
                load_x_rows(sp, io, keep, Batch(0, par))
            load_layer0(len(LAYER0) - 1)
            sp.wait_ge(ab_lo, 1)
            sp.dma_start(keep.A_dram.rearrange("h (c p) n -> p h c n", p=P), a_hl[:].bitcast(F32)).then_inc(stores, 16)
            sp.wait_ge(ab_lo, 2)
            sp.dma_start(keep.B_dram.rearrange("h (c p) n -> p h c n", p=P), b_hl[:].bitcast(F32)).then_inc(stores, 16)
            sp.wait_ge(stores, 32)

        @block.gpsimd
        def _(pool):
            nc.gpsimd.memset(keep.minus_half[:], -0.5)
            nc.gpsimd.memset(keep.ident[:], 0.0).then_inc(ident_ready, 1)
            pool.wait_ge(ident_ready, 1)
            nc.gpsimd.affine_select(out=keep.ident[:], in_=keep.ident[:], compare_op=ALU.not_equal, fill=1.0,
                                    base=0, pattern=[[-1, P]], channel_multiplier=1).then_inc(ident_ready, 1)

        @block.vector
        def _(dve):
            def layer0_lo(n):
                w, hl = LAYER0[n]
                dve.wait_ge(hl0_hi, n + 1)
                cols = (w.shape[0] // P) * D
                nc.vector.tensor_tensor(hl[:, LO], raw0[:, n % 2, 0:cols].rearrange("p (c n) -> p c n", n=D),
                                        hl[:, HI].bitcast(F32), ALU.subtract).then_inc(hl0_lo, 1)

            dve.wait_ge(wdT_in_psum, 1)
            for c in range(EC):
                nc.vector.tensor_copy(wdT[:, c, :], ps[c][:, 0:E]).then_inc(wdT_ready, 1)
            dve.wait_ge(wqk_load, 32)
            dve.wait_ge(wv_load, 16)
            dve.wait_ge(loads, ALL_LOADS)
            for n, (w, b, out) in enumerate(((wk, bk, bks), (wv, bv, bvs))):
                for c in range(EC):
                    wait(dve, sums_ready, n * EC + c)
                    nc.vector.tensor_tensor_reduce(out=junk[:, 0:T], in0=w[:, c, :], in1=bekv_row[:], scale=1.0,
                                                   scalar=b[:, c:c + 1], op0=ALU.mult, op1=ALU.add,
                                                   accum_out=out[:, c:c + 1]).then_inc(sums_ready, 1)
            dve.wait_ge(sums_ready, 2 * EC)
            for src, dst in ((bks, bks_wide), (bvs, bvs_wide), (bv0, bv0_wide)):
                nc.vector.tensor_copy(dst[:], src[:].unsqueeze(2).to_broadcast([P, EC, P])).then_inc(wide_ready, 1)
            dve.wait_ge(a_in_psum, 1)
            for c in range(DC):
                nc.vector.tensor_copy(a_raw[:, c, :], ps[4 + c][:, 0:T]).then_inc(a_copied, 1)
                dve.wait_ge(a_copied, c + 1)
                nc.vector.scalar_tensor_tensor(out=a_s[:, c, :], in0=a_raw[:, c, :], scalar=gq[:, c:c + 1],
                                               in1=gkv_row[:], op0=ALU.mult, op1=ALU.mult).then_inc(a_scaled, 1)
            dve.wait_ge(ab_hi, 1)
            nc.vector.tensor_tensor(a_hl[:, LO], a_s[:], a_hl[:, HI].bitcast(F32), ALU.subtract).then_inc(ab_lo, 1)
            dve.wait_ge(b_in_psum, 1)
            for c in range(TC):
                nc.vector.tensor_scalar(b_s[:, c, :], ps[c][:, 0:E], gkv[:, c:c + 1], None, ALU.mult).then_inc(b_scaled, 1)
            dve.wait_ge(ab_hi, 2)
            nc.vector.tensor_tensor(b_hl[:, LO], b_s[:], b_hl[:, HI].bitcast(F32), ALU.subtract).then_inc(ab_lo, 1)
            layer0_lo(0)
            layer0_lo(1)
            dve.wait_ge(rows_in_psum, 1)
            nc.vector.tensor_copy(u[:], ps[4][:, 0:D]).then_inc(u_ready, 1)
            dve.wait_ge(u_ready, 1)
            nc.vector.tensor_tensor(keep.score_row[:], u[:], gq_row[:], ALU.mult).then_inc(rows_done, 1)
            nc.vector.tensor_tensor_reduce(out=junk[:], in0=u[:], in1=beq_row[:], scale=1.0, scalar=0.0,
                                           op0=ALU.mult, op1=ALU.add, accum_out=csum[:]).then_inc(rows_done, 1)
            dve.wait_ge(rows_done, 2)
            nc.vector.tensor_tensor(keep.score_const[:], ps[7][:, 0:1], csum[:], ALU.add).then_inc(rows_done, 1)
            nc.vector.tensor_tensor(keep.bd_row[:], ps[5][:, 0:E], bd_row[:], ALU.add).then_inc(rows_done, 1)
            nc.vector.tensor_tensor(keep.bo_row[:], ps[6][:, 0:D], bo_row[:], ALU.add).then_inc(rows_done, 1)
            nc.vector.tensor_tensor(keep.t_bias[:], ps[3][:, 0:TC], gkv[:], ALU.mult).then_inc(rows_done, 1)
            dve.wait_ge(rows_done, 6)
            layer0_lo(2)

        @block.scalar
        def _(act):
            act.wait_ge(a_scaled, DC)
            nc.scalar.activation(a_hl[:, HI], a_s[:], ACT.Copy).then_inc(ab_hi, 1)
            act.wait_ge(b_scaled, TC)
            nc.scalar.activation(b_hl[:, HI], b_s[:], ACT.Copy).then_inc(ab_hi, 1)
            def layer0_hi(n):
                w, hl = LAYER0[n]
                act.wait_ge(raw0_loaded[n % 2], 16 * (n // 2 + 1))
                cols = (w.shape[0] // P) * D
                nc.scalar.activation(hl[:, HI], raw0[:, n % 2, 0:cols].rearrange("p (c n) -> p c n", n=D), ACT.Copy).then_inc(hl0_hi, 1)

            for n in range(len(LAYER0)):
                layer0_hi(n)
            act.wait_ge(loads, ALL_LOADS)
            nc.scalar.mul(keep.bqs0[:], keep.bq0[:], d.SCALE)

        @block.tensor
        def _(pe):
            pe.wait_ge(ident_ready, 2)
            pe.wait_ge(wd_load, 16)
            for c in range(EC):
                for f in range(EC):
                    last = nc.tensor.transpose(ps[c][:, P * f:P * (f + 1)], wd[:, f, P * c:P * (c + 1)], keep.ident[:])
            last.then_inc(wdT_in_psum, 1)
            pe.wait_ge(wqk_load, 32)
            for c in range(DC):
                for e in range(EC):
                    last = nc.tensor.matmul(ps[4 + c][:, 0:T], wq[:, e, P * c:P * (c + 1)], wk[:, e, :],
                                            start=e == 0, stop=e == EC - 1)
            last.then_inc(a_in_psum, 1)
            pe.wait_ge(wdT_ready, EC)
            pe.wait_ge(wv_load, 16)
            for c in range(TC):
                for e in range(EC):
                    last = nc.tensor.matmul(ps[c][:, 0:E], wv[:, e, P * c:P * (c + 1)], wdT[:, e, :],
                                            start=e == 0, stop=e == EC - 1)
            last.then_inc(b_in_psum, 1)
            pe.wait_ge(wide_ready, 3)
            pe.wait_ge(wo_load, 16)
            pe.wait_ge(loads, ALL_LOADS)
            pe.wait_ge(a_copied, DC)
            for bank, lhs, rhs in ((4, bks_wide, wq), (5, bvs_wide, wdT), (6, bv0_wide, wo0), (7, bks_wide, bq)):
                n = 1 if rhs is bq else D
                for e in range(EC):
                    moving = bq[:, e:e + 1] if rhs is bq else rhs[:, e, :]
                    nc.tensor.matmul(ps[bank][:, 0:n], lhs[:, e, :], moving, start=e == 0, stop=e == EC - 1)
            for c in range(TC):
                for e in range(EC):
                    nc.tensor.matmul(ps[3][:, c:c + 1], wk[:, e, P * c:P * (c + 1)], bq[:, e:e + 1],
                                     start=e == 0, stop=False)
                for q in range(DC):
                    last = nc.tensor.matmul(ps[3][:, c:c + 1], a_raw[:, q, P * c:P * (c + 1)], beq[:, q:q + 1],
                                            start=False, stop=q == DC - 1)
            last.then_inc(rows_in_psum, 1)


def queries_phase(nc, d, io, keep):
    D, N = d.D, d.N
    DC = D // P
    PER = PER_STEP
    STEPS = d.B // PER
    TOK = PER * N
    with ExitStack() as ctx:
        s = Scope(nc, ctx)
        xn, x_loads = keep.xn, keep.x_loads
        xT = s.sb("q_xT", [P, 2, 2, DC, TOK], F32R)
        q32 = s.sb("q_q32", [P, DC, TOK])
        q_hl = s.sb("q_q_hl", [P, 2, 2, DC, TOK], F32R)
        pt = [s.psum(f"q_pt{i}", [P, BANK]) for i in range(4)]
        pq = [s.psum(f"q_pq{i}", [P, BANK]) for i in range(4)]
        w1 = s.sb("q_w1", [P, DC, d.F])
        ln_g, ln_b, ln_b_wide = s.sb("q_ln_g", [P, DC]), s.sb("q_ln_b", [P, DC]), s.sb("q_ln_b_wide", [P, DC, P])
        b1 = s.sb("q_b1", [1, d.F])
        ln_loaded, w1_loaded, w1_scaled, w1_stored = (s.sem(f"q_{n}") for n in ("ln_loaded", "w1_loaded", "w1_scaled", "w1_stored"))
        ln_b_ready, b1_in_psum, b1_done = s.sem("q_ln_b_ready"), s.sem("q_b1_in_psum"), s.sem("q_b1_done")
        stores = s.sems("q_stores", 2)
        xT_in_psum, xT_hi, xT_lo = s.sem("q_xT_in_psum"), s.sem("q_xT_hi"), s.sem("q_xT_lo")
        q_in_psum, q_ready, q_hi, q_lo = (s.sem(f"q_q_{n}") for n in ("in_psum", "ready", "hi", "lo"))
        assert DC * BANK == d.F
        block = ctx.enter_context(nc.Block())

        def all_steps(eng, step, feed_forward):
            step(Batch(0, 0))
            step(Batch(0, 1))
            feed_forward()
            with eng.Fori(1, STEPS // 2 - 1) as pair:
                step(Batch(pair, 0))
                step(Batch(pair, 1))
            step(Batch(STEPS // 2 - 1, 0))
            step(Batch(STEPS // 2 - 1, 1), last=True)

        @block.sync
        def _(sp):
            def load(i):
                wait(sp, xT_in_psum, (i.n - 1) * DC)
                load_x_rows(sp, io, keep, i)

            def store_w1():
                for par in range(2):
                    load_context(sp, io, keep, Batch(0, par))
                for k in range(DC):
                    sp.wait_ge(w1_scaled, k + 1)
                    sp.dma_start(keep.W1_dram[:, :, k, :].rearrange("j p n -> p j n"),
                                 w1[:, k, :].rearrange("p (j n) -> p j n", n=P)).then_inc(w1_stored, 16)

            def store(i):
                sp.wait_ge(q_lo, (i.n + 1) * DC)
                for hl in range(2):
                    sp.dma_start(keep.q_dram[hl, :, bass.ds(i.n * TOK, TOK)].rearrange("(c p) n -> p c n", p=P),
                                 q_hl[:, i.par, hl].bitcast(F32)).then_inc(stores[i.par], 16)

            def step(i, last=False):
                if not isinstance(i.n, int) or i.n + 2 < STEPS:
                    load(i.next().next())
                if not isinstance(i.n, int) or i.n > 0:
                    store(i.prev())

            for t, v in ((ln_g, column(io.ln_g)), (ln_b, column(io.ln_b)), (b1, io.b1.rearrange("(o n) -> o n", o=1))):
                sp.dma_start(t[:], v, allow_slow_non_contiguous=True).then_inc(ln_loaded, 16)
            for k in range(DC):
                sp.dma_start(w1[:, k, :], io.W1[P * k:P * (k + 1), :]).then_inc(w1_loaded, 16)
            all_steps(sp, step, store_w1)
            store(Batch(STEPS // 2 - 1, 1))
            sp.wait_ge(b1_done, DC)
            sp.dma_start(keep.b1_dram[:], b1[:]).then_inc(w1_stored, 16)
            sp.wait_ge(w1_stored, 16 * (DC + 1))
            for par in range(2):
                sp.wait_ge(stores[par], 32 * (STEPS // 2))

        @block.tensor
        def _(pe):
            def turn(i):
                pe.wait_ge(x_loads[i.par], 16 * (i.pair + 1))
                for k in range(DC):
                    wait(pe, xT_lo, (i.n - 1) * DC + k + 1)
                    for t in range(PER):
                        last = nc.tensor.transpose(pt[k][:, t * N:(t + 1) * N], xn[:, i.par, t, P * k:P * (k + 1)],
                                                   keep.ident[0:N, 0:N])
                    last.then_inc(xT_in_psum, 1)

            def step(i, last=False):
                if not last:
                    turn(i.next())
                pe.wait_ge(xT_lo, (i.n + 1) * DC)
                for c in range(DC):
                    wait(pe, q_ready, (i.n - 1) * DC + c + 1)
                    for k in range(DC):
                        for a, b in PASSES:
                            ins = nc.tensor.matmul(pq[c][:, 0:TOK], keep.wq_hl[:, a, k, P * c:P * (c + 1)], xT[:, i.par, b, k, :],
                                                   start=(k, a, b) == (0, HI, HI), stop=(k, a, b) == (DC - 1, LO, HI))
                    ins.then_inc(q_in_psum, 1)

            def bias_products():
                pe.wait_ge(ln_b_ready, 1)
                pe.wait_ge(w1_loaded, 16 * DC)
                pe.wait_ge(q_ready, 2 * DC)
                for k in range(DC):
                    for c in range(DC):
                        last = nc.tensor.matmul(pq[c][:], ln_b_wide[:, k, :], w1[:, k, BANK * c:BANK * (c + 1)],
                                                start=k == 0, stop=k == DC - 1)
                    last.then_inc(b1_in_psum, 1)
                pe.wait_ge(b1_done, DC)

            turn(Batch(0, 0))
            all_steps(pe, step, bias_products)

        @block.scalar
        def _(act):
            def rows_hi(i):
                for k in range(DC):
                    act.wait_ge(xT_in_psum, i.n * DC + k + 1)
                    wait(act, q_in_psum, (i.n - 1) * DC)
                    nc.scalar.activation(xT[:, i.par, HI, k, :], pt[k][:, 0:TOK], ACT.Copy).then_inc(xT_hi, 1)

            def step(i, last=False):
                if not last:
                    rows_hi(i.next())
                wait(act, stores[i.par], i.pair * 32)
                for c in range(DC):
                    act.wait_ge(q_in_psum, i.n * DC + c + 1)
                    wait(act, q_lo, (i.n - 1) * DC + c + 1)
                    nc.scalar.activation(q32[:, c, :], pq[c][:, 0:TOK], ACT.Identity, bias=keep.bqs0[:, c:c + 1],
                                         scale=d.SCALE).then_inc(q_ready, 1)
                    act.wait_ge(q_ready, i.n * DC + c + 1)
                    nc.scalar.activation(q_hl[:, i.par, HI, c, :], q32[:, c, :], ACT.Copy).then_inc(q_hi, 1)

            def scale_w1():
                for k in range(DC):
                    act.wait_ge(b1_in_psum, k + 1)
                    nc.scalar.activation(w1[:, k, :], w1[:, k, :], ACT.Copy, scale=ln_g[:, k:k + 1]).then_inc(w1_scaled, 1)

            rows_hi(Batch(0, 0))
            all_steps(act, step, scale_w1)

        @block.vector
        def _(dve):
            def rows_lo(i):
                for k in range(DC):
                    dve.wait_ge(xT_hi, i.n * DC + k + 1)
                    nc.vector.tensor_tensor(xT[:, i.par, LO, k, :], pt[k][:, 0:TOK], xT[:, i.par, HI, k, :].bitcast(F32),
                                            ALU.subtract).then_inc(xT_lo, 1)

            def step(i, last=False):
                if not last:
                    rows_lo(i.next())
                for c in range(DC):
                    dve.wait_ge(q_hi, i.n * DC + c + 1)
                    nc.vector.tensor_tensor(q_hl[:, i.par, LO, c, :], q32[:, c, :], q_hl[:, i.par, HI, c, :].bitcast(F32),
                                            ALU.subtract).then_inc(q_lo, 1)

            def b1_out():
                dve.wait_ge(b1_in_psum, DC)
                for c in range(DC):
                    part = slice(BANK * c, BANK * (c + 1))
                    nc.vector.tensor_tensor(b1[:, part], pq[c][0:1, :], b1[:, part], ALU.add).then_inc(b1_done, 1)

            dve.wait_ge(ln_loaded, 3 * 16)
            nc.vector.tensor_copy(ln_b_wide[:], ln_b[:].unsqueeze(2).to_broadcast([P, DC, P])).then_inc(ln_b_ready, 1)
            rows_lo(Batch(0, 0))
            all_steps(dve, step, b1_out)


def load_context(sp, io, keep, b):
    M = io.ctx.shape[1]
    tiles = -(-M // P)
    whole = P * (tiles - 1)
    src = io.ctx[bass.ds(b.n, 1), :, :].rearrange("b m t -> (b m) t")
    sp.dma_start(keep.cn[b.par][:, 0:tiles - 1, :], src[0:whole, :].rearrange("(t p) d -> p t d", p=P)).then_inc(keep.ctx_loaded[b.par], 16)
    sp.dma_start(keep.cn[b.par][0:M - whole, tiles - 1, :], src[whole:M, :]).then_inc(keep.ctx_loaded[b.par], 16)


def attention_phase(nc, d, io, keep):
    B, N, M, D, T = d.B, d.N, d.M, d.D, d.T
    TC, DC, DH = T // P, D // P, D // HEADS
    MT = -(-M // P)
    LAST = M - P * (MT - 1)
    TB = MT // 2
    SPLIT = ((0, TB * P), (TB * P, M - TB * P))
    MH = M // 2
    SW = MH + 1
    PAIRS, QUADS = HEADS // 2, HEADS // 4
    assert M % 2 == 0 and SW % 2 == 0 and MT % 2 == 0
    K_STEPS = [("k", c, n) for c in range(DC) for n in range(2)]
    V_STEPS = [("v", t, 0) for t in range(MT)]
    STEPS = [x for pair in zip(K_STEPS, V_STEPS) for x in pair] + K_STEPS[MT:]
    NK, NV, NSTEP = len(K_STEPS), len(V_STEPS), len(STEPS)
    FILLS = TC
    NEED_K = [STEPS.index(("k", c, 1)) for c in range(DC)]
    DOUBLE = 5
    slot_of = [FILLS + n - (FILLS + n > DOUBLE) for n in range(NSTEP)]
    by_slot = [[n for n in range(NSTEP) if slot_of[n] == h] for h in range(HEADS)]
    assert slot_of[-1] == HEADS - 1

    VALUES_AT = {5: 0, 9: 1, 0: 2, 2: 3}
    lo_of_slot = [[]] + by_slot[0:HEADS - 1]

    def k_before(n):
        return sum(x[0] == "k" for x in STEPS[:n])

    def rows_of(t):
        return LAST if t == MT - 1 else P

    with ExitStack() as ctx:
        s = Scope(nc, ctx)
        cn = keep.cn
        qm0 = keep.wq_hl[:].rearrange("p h c n -> p (h c n)")[:, 0:2 * HEADS * N]
        qm = [qm0.rearrange("p (h i n) -> p h i n", h=2, i=HEADS), s.sb("a_qm1", [P, 2, HEADS, N], F32R)[:]]
        cT = s.sb("a_cT", [P, 2, TC, M], F32R)
        kt = [s.sb(f"a_kt{i}", [P, PAIRS, M], F32R) for i in range(2)]
        vn = [s.sb(f"a_vn{i}", [P, MT, D]) for i in range(2)]
        pr = s.sb("a_pr", [N, 4, M])
        kw = s.sb("a_kw", [P, 2, SPLIT[0][1]])
        pT = s.sb("a_pT", [P, 2, 4, MT, N])
        nmax, sums = s.sb("a_nmax", [N, 2, HEADS]), s.sb("a_sums", [N, 2, HEADS])
        inv, rexp = s.sb("a_inv", [N, 2, 4]), s.sb("a_rexp", [N, 2, 4, DH])
        rb = s.sb("a_rb", [P, 2, N])
        at = s.sb("a_at", [P, 2, QUADS, N])
        ps = s.psum("a_ps", [P, 8 * BANK])
        tp = [ps[:, 4 * BANK:5 * BANK], ps[:, 5 * BANK:6 * BANK]]
        pj, av = ps[:, 6 * BANK:7 * BANK], ps[:, 7 * BANK:8 * BANK]

        FIRST_BANKS = 6

        def bank(n, first):
            return ps[:, (n % FIRST_BANKS) * BANK:(n % FIRST_BANKS + 1) * BANK] if first else pj

        def scores(buf):
            start = 2 * buf * BANK
            return ps[0:N, start:start + 2 * (BANK + 1)].rearrange("p (c n) -> p c n", c=2)[:, :, 0:MH]

        ctx_loaded, q_loaded = keep.ctx_loaded, s.sems("a_q_loaded", 2)
        zeroed, tail_zeroed, stored = s.sem("a_zeroed"), s.sem("a_tail_zeroed"), s.sems("a_stored", 2)
        filled, cT_hi, cT_lo = s.sem("a_filled"), s.sem("a_cT_hi"), s.sem("a_cT_lo")
        proj_done, kw_ready, k_hi = s.sem("a_proj_done"), s.sem("a_kw_ready"), s.sem("a_k_hi")
        k_ready, v_ready = s.sem("a_k_ready"), s.sem("a_v_ready")
        scores_done, max_ready, exp_done = s.sem("a_scores_done"), s.sem("a_max_ready"), s.sem("a_exp_done")
        p_turned, pT_ready = s.sem("a_p_turned"), s.sems("a_pT_ready", 2)
        inv_ready, rexp_ready, av_done = s.sem("a_inv_ready"), s.sem("a_rexp_ready"), s.sem("a_av_done")
        rb_ready, at_ready = s.sem("a_rb_ready"), s.sem("a_at_ready")
        block = ctx.enter_context(nc.Block())

        def quad_at(b, h, first):
            if h not in VALUES_AT or (first and h < FILLS):
                return ()
            return ((b if h >= FILLS else b.prev(), VALUES_AT[h]),)

        Q_LOADS = 8 * 16

        def all_batches(eng, batch):
            batch(Batch(0, 0), first=True)
            batch(Batch(0, 1))
            with eng.Fori(1, B // 2 - 1) as pair:
                batch(Batch(pair, 0))
                batch(Batch(pair, 1))
            batch(Batch(B // 2 - 1, 0))
            batch(Batch(B // 2 - 1, 1), last=True)

        @block.sync
        def _(sp):
            def load_ctx(b):
                wait(sp, filled, (b.n - 1) * 2 * FILLS)
                load_context(sp, io, keep, b)

            def load_q(b):
                wait(sp, scores_done, (b.n - 1) * HEADS)
                for hl in range(2):
                    src = keep.q_dram[hl, :, bass.ds(b.n * N, N)].rearrange("(i o d) n -> o d i n", o=2, d=DH)
                    for odd in range(2):
                        dst = qm[b.par][:, hl].bitcast(F32).rearrange("p (i o) n -> p o i n", o=2)[:, odd]
                        for copy in range(2):
                            r = (2 * copy + odd) * DH
                            sp.dma_start(dst[r:r + DH], src[odd]).then_inc(q_loaded[b.par], 16)

            def store(b):
                sp.wait_ge(at_ready, (b.n + 1) * QUADS)
                sp.dma_start(keep.attn_dram[:, bass.ds(b.n * N, N)].rearrange("(c p) n -> p c n", p=P),
                             at[:, b.par]).then_inc(stored[b.par], 16)

            def batch(b, first=False, last=False):
                if not isinstance(b.n, int) or b.n + 2 < B:
                    load_ctx(b.next().next())
                if not last:
                    load_q(b.next())
                if not first:
                    store(b.prev())

            sp.wait_ge(zeroed, 2)
            load_q(Batch(0, 0))
            all_batches(sp, batch)
            store(Batch(B // 2 - 1, 1))
            for par in range(2):
                sp.wait_ge(stored[par], 16 * (B // 2))

        @block.gpsimd
        def _(pool):
            for i in range(2):
                nc.gpsimd.memset(qm[i].bitcast(F32), 0.0).then_inc(zeroed, 1)

        @block.tensor
        def _(pe):
            def fill(b, k, n, first=False):
                out = bank(2 * k + n, first)
                if k == 0 and n == 0:
                    pe.wait_ge(ctx_loaded[b.par], (b.pair + 1) * 32)
                    wait(pe, kw_ready, b.n * NK)
                    wait(pe, v_ready, b.n * NV)
                if not first:
                    pe.wait_ge(cT_lo, b.n * 2 * FILLS + 2 * k + n)
                for t in range(TB * n, TB * (n + 1)):
                    at0, rows = P * (t - TB * n), rows_of(t)
                    last = nc.tensor.transpose(out[:, at0:at0 + rows], cn[b.par][0:rows, t, P * k:P * (k + 1)],
                                               keep.ident[0:rows, 0:rows])
                last.then_inc(filled, 1)

            def project(b, n, first=False):
                out = bank(n, first)
                left = n - FIRST_BANKS + 1 if first else n
                kind, i, half = STEPS[n]
                if n == 0:
                    pe.wait_ge(cT_lo, (b.n + 1) * 2 * FILLS)
                if left > 0 or not first:
                    wait(pe, kw_ready, b.n * NK + k_before(left))
                    wait(pe, v_ready, b.n * NV + left - k_before(left))
                for k in range(TC):
                    for x, y in PASSES:
                        flags = dict(start=(k, x, y) == (0, HI, HI), stop=(k, x, y) == (TC - 1, LO, HI))
                        if kind == "k":
                            m0, cols = SPLIT[half]
                            last = nc.tensor.matmul(out[:, 0:cols], keep.wk_hl[:, x, k, P * i:P * (i + 1)],
                                                    cT[:, y, k, m0:m0 + cols], **flags)
                        else:
                            last = nc.tensor.matmul(out[0:rows_of(i), :], cT[:, x, k, P * i:P * i + rows_of(i)],
                                                    keep.wv_hl[:, y, k, :], **flags)
                last.then_inc(proj_done, 1)

            def score(b, h):
                if h == 0:
                    pe.wait_ge(q_loaded[b.par], (b.pair + 1) * Q_LOADS)
                if h % 4 == 0:
                    pe.wait_ge(k_ready, b.n * NK + k_before(NEED_K[h // 4]) + 1)
                wait(pe, exp_done, b.n * HEADS + h - 1)
                for n in range(2):
                    at0 = (2 * (h % 2) + n) * BANK
                    m0 = n * (MH - 1)
                    for hl in range(2):
                        last = nc.tensor.matmul(ps[0:N, at0:at0 + SW], qm[b.par][:, hl, h, :],
                                                kt[b.par][:, h // 2, m0:m0 + SW], start=hl == HI, stop=hl == LO)
                last.then_inc(scores_done, 1)

            def turn(b, h):
                g = b.n * HEADS + h
                pe.wait_ge(exp_done, g + 1)
                for n in range(2):
                    wait(pe, pT_ready[n], g)
                    for t in range(TB * n, TB * (n + 1)):
                        at0 = N * (t - TB * n)
                        last = nc.tensor.transpose(tp[n][0:rows_of(t), at0:at0 + N], pr[:, h % 4, P * t:P * t + rows_of(t)],
                                                   keep.ident[0:N, 0:N])
                last.then_inc(p_turned, 1)

            def values(b, q, part=None):
                quad = b.n * QUADS + q
                if part != 1:
                    for n in range(2):
                        pe.wait_ge(pT_ready[n], (quad + 1) * 4)
                    if q == 0:
                        pe.wait_ge(v_ready, (b.n + 1) * NV)
                    wait(pe, at_ready, quad)
                for t in (range(MT) if part is None else range(TB * part, TB * (part + 1))):
                    for j in range(4):
                        h = 4 * q + j
                        nc.tensor.matmul(av[DH * j:DH * (j + 1), 0:N], vn[b.par][0:rows_of(t), t, DH * h:DH * (h + 1)],
                                         pT[0:rows_of(t), q % 2, j, t, :], start=t == 0, stop=t == MT - 1)
                if part != 0:
                    pe.wait_ge(rexp_ready, quad + 1)
                    nc.tensor.transpose(av[:, P:P + N], rexp[:, q % 2].rearrange("n j d -> n (j d)"),
                                        keep.ident[0:N, 0:N]).then_inc(av_done, 1)

            def batch(b, first=False, last=False):
                for h in range(HEADS):
                    score(b, h)
                    if h == 0 and not first:
                        values(b.prev(), QUADS - 2, part=0)
                    if h < FILLS and not last:
                        fill(b.next(), h, 0)
                    if h > 0:
                        turn(b, h - 1)
                    elif not first:
                        turn(b.prev(), HEADS - 1)
                    if h < FILLS and not first:
                        if h == 0:
                            values(b.prev(), QUADS - 2, part=1)
                        else:
                            values(b.prev(), QUADS - 1, part=h - 1)
                    if h < FILLS and not last:
                        fill(b.next(), h, 1)
                    if not last:
                        for n in by_slot[h][:1]:
                            project(b.next(), n)
                    if h >= FILLS:
                        for at in quad_at(b, h, first):
                            values(*at)
                    if not last:
                        for n in by_slot[h][1:]:
                            project(b.next(), n)

            for k in range(FILLS):
                for n in range(2):
                    fill(Batch(0, 0), k, n, first=True)
            for n in range(NSTEP):
                project(Batch(0, 0), n, first=True)
            pe.wait_ge(kw_ready, NK)
            pe.wait_ge(v_ready, NV)
            pe.wait_ge(tail_zeroed, 1)
            all_batches(pe, batch)
            end = Batch(B // 2 - 1, 1)
            values(end, QUADS - 2)
            turn(end, HEADS - 1)
            values(end, QUADS - 1)

        @block.scalar
        def _(act):
            def fill_hi(b, k, n, first=False):
                m0, cols = SPLIT[n]
                act.wait_ge(filled, b.n * 2 * FILLS + 2 * k + n + 1)
                wait(act, proj_done, b.n * NSTEP)
                nc.scalar.activation(cT[:, HI, k, m0:m0 + cols], bank(2 * k + n, first)[:, 0:cols], ACT.Copy).then_inc(cT_hi, 1)

            def key_hi(b, n, first=False):
                kind, i, half = STEPS[n]
                if kind != "k":
                    return
                m0, cols = SPLIT[half]
                step = b.n * NK + k_before(n)
                buf = k_before(n) % 2
                act.wait_ge(proj_done, b.n * NSTEP + n + 1)
                wait(act, k_ready, step - 1)
                nc.scalar.activation(kw[:, buf, 0:cols], bank(n, first)[:, 0:cols], ACT.Identity, bias=keep.bk0[:, i:i + 1]).then_inc(kw_ready, 1)
                act.wait_ge(kw_ready, step + 1)
                for r in range(2):
                    nc.scalar.activation(kt[b.par][0:64, 2 * i + r, m0:m0 + cols], kw[64 * r:64 * r + 64, buf, 0:cols],
                                         ACT.Copy).then_inc(k_hi, 1)

            def turned(b, h):
                act.wait_ge(p_turned, b.n * HEADS + h + 1)
                if h % 4 == 0:
                    wait(act, av_done, b.n * QUADS + h // 4 - 1)
                nc.scalar.activation(pT[:, (h // 4) % 2, h % 4, TB:MT, :],
                                     tp[1][:, 0:TB * N].rearrange("p (t n) -> p t n", n=N), ACT.Copy).then_inc(pT_ready[1], 1)

            def exp(b, h):
                g = b.n * HEADS + h
                act.wait_ge(max_ready, g + 1)
                wait(act, p_turned, g - 3)
                nc.scalar.activation(pr[:, h % 4, :].rearrange("n (c m) -> n c m", c=2), scores(h % 2), ACT.Exp,
                                     bias=nmax[:, b.par, h:h + 1], accum_out=sums[:, b.par, h:h + 1]).then_inc(exp_done, 1)

            def spread(b, q):
                quad = b.n * QUADS + q
                act.wait_ge(av_done, quad + 1)
                wait(act, at_ready, quad - 1)
                nc.scalar.activation(rb[:, q % 2, :], av[:, P:P + N], ACT.Copy).then_inc(rb_ready, 1)

            def batch(b, first=False, last=False):
                for h in range(HEADS):
                    if h < FILLS and not last:
                        fill_hi(b.next(), h, 0)
                    if last and h > 0:
                        exp(b, h)
                    if h > 0:
                        turned(b, h - 1)
                    elif not first:
                        turned(b.prev(), HEADS - 1)
                    if not last or h == 0:
                        exp(b, h)
                    if h < FILLS and not last:
                        fill_hi(b.next(), h, 1)
                    if not last:
                        for n in by_slot[h][:1]:
                            key_hi(b.next(), n)
                    for at in quad_at(b, h, first):
                        spread(*at)
                    if not last:
                        for n in by_slot[h][1:]:
                            key_hi(b.next(), n)

            for k in range(FILLS):
                for n in range(2):
                    fill_hi(Batch(0, 0), k, n, first=True)
            for n in range(NSTEP):
                key_hi(Batch(0, 0), n, first=True)
            act.wait_ge(tail_zeroed, 1)
            all_batches(act, batch)
            end = Batch(B // 2 - 1, 1)
            spread(end, QUADS - 2)
            turned(end, HEADS - 1)
            spread(end, QUADS - 1)

        @block.vector
        def _(dve):
            def fill_lo(b, k, n, first=False):
                m0, cols = SPLIT[n]
                dve.wait_ge(cT_hi, b.n * 2 * FILLS + 2 * k + n + 1)
                nc.vector.tensor_tensor(cT[:, LO, k, m0:m0 + cols], bank(2 * k + n, first)[:, 0:cols],
                                        cT[:, HI, k, m0:m0 + cols].bitcast(F32), ALU.subtract).then_inc(cT_lo, 1)

            def key_lo(b, n):
                kind, i, half = STEPS[n]
                if kind != "k":
                    return
                m0, cols = SPLIT[half]
                for r in range(2):
                    dve.wait_ge(k_hi, (b.n * NK + k_before(n)) * 2 + r + 1)
                    last = nc.vector.tensor_tensor(
                        kt[b.par][64:P, 2 * i + r, m0:m0 + cols], kw[64 * r:64 * r + 64, k_before(n) % 2, 0:cols],
                        kt[b.par][0:64, 2 * i + r, m0:m0 + cols].bitcast(F32), ALU.subtract)
                last.then_inc(k_ready, 1)

            def value_out(b, n, first=False):
                kind, i, half = STEPS[n]
                if kind != "v":
                    return
                dve.wait_ge(proj_done, b.n * NSTEP + n + 1)
                nc.vector.tensor_copy(vn[b.par][0:rows_of(i), i, :], bank(n, first)[0:rows_of(i), :]).then_inc(v_ready, 1)

            def row_max(b, h):
                dve.wait_ge(scores_done, b.n * HEADS + h + 1)
                nc.vector.tensor_reduce(nmax[:, b.par, h:h + 1], scores(h % 2), AX.XY, ALU.max, negate=True).then_inc(max_ready, 1)

            def turned(b, h):
                dve.wait_ge(p_turned, b.n * HEADS + h + 1)
                if h % 4 == 0:
                    wait(dve, av_done, b.n * QUADS + h // 4 - 1)
                nc.vector.tensor_copy(pT[:, (h // 4) % 2, h % 4, 0:TB, :],
                                      tp[0][:, 0:TB * N].rearrange("p (t n) -> p t n", n=N)).then_inc(pT_ready[0], 1)

            def inverse(b, q):
                quad = b.n * QUADS + q
                dve.wait_ge(exp_done, (quad + 1) * 4)
                wait(dve, av_done, quad - 1)
                nc.vector.reciprocal(inv[:, q % 2], sums[:, b.par, 4 * q:4 * q + 4]).then_inc(inv_ready, 1)
                dve.wait_ge(inv_ready, quad + 1)
                nc.vector.tensor_copy(rexp[:, q % 2], inv[:, q % 2].unsqueeze(2).to_broadcast([N, 4, DH])).then_inc(rexp_ready, 1)

            def scale(b, q):
                quad = b.n * QUADS + q
                dve.wait_ge(rb_ready, quad + 1)
                if q == 0:
                    wait(dve, stored[b.par], b.pair * 16)
                nc.vector.tensor_tensor(at[:, b.par, q, :], av[:, 0:N], rb[:, q % 2, :], ALU.mult).then_inc(at_ready, 1)

            def batch(b, first=False, last=False):
                for h in range(HEADS):
                    row_max(b, h)
                    for at in quad_at(b, h, first):
                        inverse(*at)
                    if h < FILLS and not last:
                        fill_lo(b.next(), h, 0)
                    if h > 0:
                        turned(b, h - 1)
                    elif not first:
                        turned(b.prev(), HEADS - 1)
                    if h < FILLS and not last:
                        fill_lo(b.next(), h, 1)
                    if not last:
                        for n in lo_of_slot[h]:
                            key_lo(b.next(), n)
                        for n in by_slot[h][:1]:
                            value_out(b.next(), n)
                    for at in quad_at(b, h, first):
                        scale(*at)
                    if not last:
                        for n in by_slot[h][1:]:
                            value_out(b.next(), n)
                    if h == FILLS and not first:
                        key_lo(b, NSTEP - 1)

            for k in range(FILLS):
                for n in range(2):
                    fill_lo(Batch(0, 0), k, n, first=True)
            for n in range(NSTEP):
                value_out(Batch(0, 0), n, first=True)
                key_lo(Batch(0, 0), n)
            dve.wait_ge(kw_ready, NK)
            dve.wait_ge(v_ready, NV)
            nc.vector.memset(tp[1][:, 0:TB * N], 0.0).then_inc(tail_zeroed, 1)
            all_batches(dve, batch)
            end = Batch(B // 2 - 1, 1)
            inverse(end, QUADS - 2)
            scale(end, QUADS - 2)
            turned(end, HEADS - 1)
            inverse(end, QUADS - 1)
            scale(end, QUADS - 1)


def tokens_phase(nc, d, io, keep):
    D, T, F = d.D, d.T, d.F
    DC, TC, FC = D // P, T // P, F // P
    TG = 5
    TOK = TG * P
    GROUPS = d.B * d.N // TOK
    HALF = TOK // 2
    assert GROUPS * TOK == d.B * d.N and HALF <= BANK
    RB = 3
    USES = ([("rows", i) for i in range(TG)] + [("up", n) for n in range(2 * FC)] + [("proj", i) for i in range(RB)]
            + [("qrows", i) for i in range(TG)] + [("proj", i) for i in range(RB, TG)] + [("query", n) for n in range(2 * TC)])
    LAST_DOWNS = [(0, 0), (0, 1), (0, 2), (1, 0), (0, 3), (1, 1), (0, 4), (1, 2), (1, 3), (1, 4)]
    DOWNS = FC - 2 + TG
    assert TG == 5

    def bank_of(use):
        return USES.index(use) % RB

    with ExitStack() as ctx:
        s = Scope(nc, ctx)
        wo, w2 = s.sb("t_wo", [P, 2, DC, D], F32R), s.sb("t_w2", [P, 2, FC, D], F32R)
        aw, w1 = s.sb("t_aw", [P, 2, DC, T], F32R), s.sb("t_w1", [P, 2, 2, DC, P], F32R)
        w1_raw, w2_raw = s.sb("t_w1_raw", [P, 2, DC, P]), s.sb("t_w2_raw", [P, 2, D])
        b1, b2_row = s.sb("t_b1", [P, FC]), s.sb("t_b2_row", [P, D])
        zn = s.sb("t_zn", [P, TG * D])
        at_in = zn[:].rearrange("p (c n) -> p c n", c=DC)
        z = zn[:].rearrange("p (i n) -> p i n", i=TG)
        wide = s.sb("t_wide", [P, 2, DC, TOK], F32R)
        zT = s.sb("t_zT", [P, 2, DC, TOK], F32R)
        xb, ob = s.sb("t_xb", [P, TG, D]), s.sb("t_ob", [P, TG, D])
        wo_raw = ob[:, 0:DC, :]
        h32, h_hl = s.sb("t_h32", [P, 2, HALF]), s.sb("t_h_hl", [P, 2, 2, TOK], F32R)
        junk = s.sb("t_junk", [P, D])
        st_h, st_q = s.sb("t_st_h", [P, TG, 6]), s.sb("t_st_q", [P, TG, 6])
        mv_h, mv_q = s.sb("t_mv_h", [P, TG, 2]), s.sb("t_mv_q", [P, TG, 2])
        ve_h, ve_q = s.sb("t_ve_h", [P, TG]), s.sb("t_ve_q", [P, TG])
        rs_h, rs_q = s.sb("t_rs_h", [P, TG]), s.sb("t_rs_q", [P, TG])
        cs = s.sb("t_cs", [P, TG])
        acc = [s.psum(f"t_acc{i}", [P, BANK]) for i in range(TG)]
        ring = [s.psum(f"t_ring{i}", [P, BANK]) for i in range(RB)]

        passed = keep.passed
        wo_loaded, aw_loaded, w2_loaded = s.sem("t_wo_loaded"), s.sem("t_aw_loaded"), s.sems("t_w2_loaded", 2)
        wo_hi, wo_lo, w1_hi, w1_lo, w2_hi, w2_lo = (s.sem(f"t_{n}") for n in ("wo_hi", "wo_lo", "w1_hi", "w1_lo", "w2_hi", "w2_lo"))
        bias_loaded, w1_loaded, at_loaded, x_loaded = s.sem("t_bias_loaded"), s.sems("t_w1_loaded", 2), s.sem("t_at_loaded"), s.sem("t_x_loaded")
        t_stored, x_stored, c_stored = s.sem("t_t_stored"), s.sem("t_x_stored"), s.sem("t_c_stored")
        rows_done, up_done, proj_done, qrows_done, query_done, down_done = (
            s.sem(f"t_{n}_done") for n in ("rows", "up", "proj", "qrows", "query", "down"))
        at_hi, at_lo, zT_hi, gelu_done, h_hi, h_lo, t_hi = (
            s.sem(f"t_{n}") for n in ("at_hi", "at_lo", "zT_hi", "gelu_done", "h_hi", "h_lo", "t_hi"))
        zT_lo, t_lo = s.sem("t_zT_lo"), s.sem("t_t_lo")
        o_ready, x1_ready, st_h_ready, st_q_ready, mv_h_ready, mv_q_ready = (
            s.sem(f"t_{n}_ready") for n in ("o", "x1", "st_h", "st_q", "mv_h", "mv_q"))
        ve_h_ready, ve_q_ready, rs_h_ready, rs_q_ready = (s.sem(f"t_{n}_ready") for n in ("ve_h", "ve_q", "rs_h", "rs_q"))
        zh_ready, zq_ready, c_ready, xb_ready, xo_ready, x1b_ready = (
            s.sem(f"t_{n}_ready") for n in ("zh", "zq", "c", "xb", "xo", "x1b"))
        block = ctx.enter_context(nc.Block())

        def all_groups(eng, group):
            group(0, first=True)
            with eng.Fori(1, GROUPS - 1) as g:
                group(g)
            group(GROUPS - 1, last=True)

        def tile(ap, i):
            return ap[:, P * i:P * (i + 1)]

        @block.sync
        def _(sp):
            def load_at(g):
                wait(sp, rows_done, g * TG)
                sp.dma_start(at_in, keep.attn_dram[:, bass.ds(g * TOK, TOK)].rearrange("(c p) n -> p c n", p=P)).then_inc(at_loaded, 16)

            def load_w1(g, j):
                wait(sp, w1_lo, g * FC + j - 1)
                sp.dma_start(w1_raw[:, j % 2], keep.W1_dram[j]).then_inc(w1_loaded[j % 2], 16)

            def load_w2(j):
                wait(sp, w2_lo, j - 1)
                sp.dma_start(w2_raw[:, j % 2], io.W2[P * j:P * (j + 1), :]).then_inc(w2_loaded[j % 2], 16)

            def group(g, first=False, last=False):
                wait(sp, x_stored, g * 16)
                rows = io.x.rearrange("b n d -> (b n) d")[bass.ds(g * TOK, TOK), :]
                sp.dma_start(xb[:], rows.rearrange("(i p) d -> p i d", p=P)).then_inc(x_loaded, 16)
                if not last:
                    load_at(g + 1)
                for j in range(2, FC):
                    load_w1(g, j)
                    if first:
                        load_w2(j)
                if not last:
                    for j in range(2):
                        load_w1(g + 1, j)
                sp.wait_ge(x1b_ready, (g + 1) * TG)
                sp.dma_start(keep.x1_dram[bass.ds(g * TOK, TOK), :].rearrange("(i p) d -> p i d", p=P), xb[:]).then_inc(x_stored, 16)
                wait_alone(sp, c_ready, (g + 1) * TG, passed)
                sp.dma_start(keep.c_dram[bass.ds(g * TOK, TOK), :].rearrange("(i p) o -> p (i o)", p=P), cs[:],
                             allow_slow_non_contiguous=True).then_inc(c_stored, 16)
                sp.wait_ge(t_hi, (g + 1) * 2 * TC)
                sp.wait_ge(t_lo, (g + 1) * 2 * TC)
                for hl in range(2):
                    sp.dma_start(keep.t_dram[hl, :, bass.ds(g * TOK, TOK)].rearrange("(c p) n -> p c n", p=P),
                                 wide[:, hl, 0:TC, :].bitcast(F32)).then_inc(t_stored, 16)

            sp.dma_start(wo_raw, chunks(io.Wo)).then_inc(wo_loaded, 16)
            load_at(0)
            for j in range(2):
                load_w1(0, j)
            sp.dma_start(b2_row[:], row(io.b2)).then_inc(bias_loaded, 16)
            sp.dma_start(b1[:], column(keep.b1_dram[0]), allow_slow_non_contiguous=True).then_inc(bias_loaded, 16)
            for j in range(2):
                load_w2(j)
            sp.dma_start(aw[:].bitcast(F32), keep.A_dram.rearrange("h (c p) n -> p h c n", p=P)).then_inc(aw_loaded, 16)
            all_groups(sp, group)
            sp.wait_ge(x_stored, 16 * GROUPS)
            sp.wait_ge(c_stored, 16 * GROUPS)
            sp.wait_ge(t_stored, 32 * GROUPS)

        @block.tensor
        def _(pe):
            def bank(g, use, last):
                left = {"rows": (zT_lo, 2 * TG, 1), "up": (gelu_done, 2 * FC, 1), "proj": (o_ready, TG, TG + 1),
                        "qrows": (zT_lo, 2 * TG, TG + 1), "query": (t_lo, 2 * TC, 1)}
                before = [v for v in USES[bank_of(use):USES.index(use):RB] if not (last and v[0] == "proj")]
                if before:
                    kind, n = before[-1]
                    sem, per_group, start = left[kind]
                    pe.wait_ge(sem, g * per_group + start + n)
                else:
                    wait(pe, t_lo, g * 2 * TC)
                return ring[bank_of(use)]

            def project(g, i, first=False):
                if first:
                    wait(pe, o_ready, max([u + 1 for u in range(i) if bank_of(("proj", u)) == bank_of(("proj", i))], default=0))
                out = ring[bank_of(("proj", i))] if first else bank(g, ("proj", i), False)
                for k in range(DC):
                    for x, y in PASSES:
                        last = nc.tensor.matmul(out[:, 0:D], tile(wide[:, x, k, :], i), wo[:, y, k, :],
                                                start=(k, x, y) == (0, HI, HI), stop=(k, x, y) == (DC - 1, LO, HI))
                last.then_inc(proj_done, 1)

            def turn(out, i, done):
                for k in range(DC):
                    last = nc.tensor.transpose(tile(out, k), tile(z[:, i, :], k), keep.ident[:])
                last.then_inc(done, 1)

            def up(g, n, last):
                j, half = n // 2, n % 2
                if half == 0:
                    pe.wait_ge(w1_lo, g * FC + j + 1)
                if j == 0:
                    pe.wait_ge(zT_lo, g * 2 * TG + (TG // 2 + 1 if half == 0 else TG))
                out = bank(g, ("up", n), last)
                for k in range(DC):
                    for x, y in PASSES:
                        ins = nc.tensor.matmul(out[:, 0:HALF], w1[:, j % 2, x, k, :], zT[:, y, k, HALF * half:HALF * (half + 1)],
                                               start=(k, x, y) == (0, HI, HI), stop=(k, x, y) == (DC - 1, LO, HI))
                ins.then_inc(up_done, 1)

            def down(g, j, i):
                for x, y in PASSES:
                    ins = nc.tensor.matmul(acc[i][:, 0:D], tile(h_hl[:, j % 2, x, :], i), w2[:, y, j, :],
                                           start=(j, x, y) == (0, HI, HI), stop=(j, x, y) == (FC - 1, LO, HI))
                return ins

            def down_inputs(g, j, first):
                if first:
                    pe.wait_ge(w2_lo, j + 1)
                pe.wait_ge(h_lo, g * 2 * FC + 2 * (j + 1))
                pe.wait_ge(h_hi, g * 2 * FC + 2 * (j + 1))

            def group(g, first=False, last=False):
                for i in range(TG):
                    pe.wait_ge(zh_ready, g * TG + i + 1)
                    turn(bank(g, ("rows", i), last), i, rows_done)
                wait(pe, x1_ready, g * TG)
                for j in range(FC):
                    for half in range(2):
                        up(g, 2 * j + half, last)
                    if 0 < j < FC - 1:
                        down_inputs(g, j - 1, first)
                        for i in range(TG):
                            ins = down(g, j - 1, i)
                        ins.then_inc(down_done, 1)
                down_inputs(g, FC - 2, first)
                for step, i in LAST_DOWNS:
                    if (step, i) == (1, 0):
                        down_inputs(g, FC - 1, first)
                    ins = down(g, FC - 2 + step, i)
                    if step == 1:
                        ins.then_inc(down_done, 1)
                if not last:
                    pe.wait_ge(at_lo, (g + 2) * DC)
                    for i in range(RB):
                        project(g, i)
                for i in range(TG):
                    pe.wait_ge(zq_ready, g * TG + i + 1)
                    turn(bank(g, ("qrows", i), last), i, qrows_done)
                if not last:
                    for i in range(RB, TG):
                        project(g, i)
                pe.wait_ge(zT_lo, (g + 1) * 2 * TG)
                for n in range(2 * TC):
                    c, half = n // 2, n % 2
                    out = bank(g, ("query", n), last)
                    for k in range(DC):
                        for x, y in PASSES:
                            ins = nc.tensor.matmul(out[:, 0:HALF], tile(aw[:, x, k, :], c), zT[:, y, k, HALF * half:HALF * (half + 1)],
                                                   start=(k, x, y) == (0, HI, HI), stop=(k, x, y) == (DC - 1, LO, HI))
                    ins.then_inc(query_done, 1)

            pe.wait_ge(wo_lo, 1)
            pe.wait_ge(at_lo, DC)
            for i in range(TG):
                project(0, i, first=True)
            pe.wait_ge(o_ready, TG)
            pe.wait_ge(aw_loaded, 16)
            all_groups(pe, group)

        @block.scalar
        def _(act):
            def attn_hi(g, k):
                act.wait_ge(at_loaded, (g + 1) * 16)
                wait(act, t_stored, (g - 1) * 32)
                nc.scalar.activation(wide[:, HI, k, :], at_in[:, k, :], ACT.Copy).then_inc(at_hi, 1)

            def up_weights_hi(g, j):
                act.wait_ge(w1_loaded[j % 2], (g * (FC // 2) + j // 2 + 1) * 16)
                wait(act, up_done, (g * FC + j - 1) * 2)
                nc.scalar.activation(w1[:, j % 2, HI], w1_raw[:, j % 2], ACT.Copy).then_inc(w1_hi, 1)

            def down_weights_hi(j):
                act.wait_ge(w2_loaded[j % 2], (j // 2 + 1) * 16)
                nc.scalar.activation(w2[:, HI, j, :], w2_raw[:, j % 2], ACT.Copy).then_inc(w2_hi, 1)

            def rows_hi(use, done, count):
                act.wait_ge(done, count)
                nc.scalar.activation(zT[:, HI, :, P * use[1]:P * (use[1] + 1)],
                                     ring[bank_of(use)][:].rearrange("p (c n) -> p c n", c=DC), ACT.Copy).then_inc(zT_hi, 1)

            def gelu(g, n):
                j, half = n // 2, n % 2
                b = bank_of(("up", n))
                act.wait_ge(up_done, g * 2 * FC + n + 1)
                wait(act, h_lo, g * 2 * FC + n - 1)
                nc.scalar.activation(h32[:, half, :], ring[b][:, 0:HALF], ACT.Gelu, bias=b1[:, j:j + 1]).then_inc(gelu_done, 1)
                act.wait_ge(gelu_done, g * 2 * FC + n + 1)
                wait(act, down_done, g * DOWNS + (j - 1 if j > 1 else 0))
                nc.scalar.activation(h_hl[:, j % 2, HI, HALF * half:HALF * (half + 1)], h32[:, half, :], ACT.Copy).then_inc(h_hi, 1)

            def group(g, first=False, last=False):
                for i in range(TG):
                    rows_hi(("rows", i), rows_done, g * TG + i + 1)
                for n in range(2 * FC):
                    gelu(g, n)
                    if first and n % 2 == 0:
                        down_weights_hi(n // 2)
                    if n % 2 == 1 and n // 2 + 2 < FC:
                        up_weights_hi(g, n // 2 + 2)
                    elif n % 2 == 1 and not last:
                        up_weights_hi(g + 1, n // 2 + 2 - FC)
                    if not last and n % 4 == 3 and n // 4 >= 4:
                        attn_hi(g + 1, n // 4 - 4)
                for i in range(TG):
                    rows_hi(("qrows", i), qrows_done, g * TG + i + 1)
                for n in range(2 * TC):
                    c, half = n // 2, n % 2
                    act.wait_ge(query_done, g * 2 * TC + n + 1)
                    nc.scalar.activation(wide[:, HI, c, HALF * half:HALF * (half + 1)], ring[bank_of(("query", n))][:, 0:HALF],
                                         ACT.Identity, bias=keep.t_bias[:, c:c + 1]).then_inc(t_hi, 1)

            act.wait_ge(wo_loaded, 16)
            nc.scalar.activation(wo[:, HI], wo_raw, ACT.Copy).then_inc(wo_hi, 1)
            for k in range(DC):
                attn_hi(0, k)
            for j in range(2):
                up_weights_hi(0, j)
            act.wait_ge(bias_loaded, 32)
            all_groups(act, group)

        @block.vector
        def _(dve):
            def attn_lo(g, k):
                dve.wait_ge(at_hi, g * DC + k + 1)
                nc.vector.tensor_tensor(wide[:, LO, k, :], at_in[:, k, :], wide[:, HI, k, :].bitcast(F32), ALU.subtract).then_inc(at_lo, 1)

            def up_weights_lo(g, j):
                dve.wait_ge(w1_hi, g * FC + j + 1)
                nc.vector.tensor_tensor(w1[:, j % 2, LO], w1_raw[:, j % 2], w1[:, j % 2, HI].bitcast(F32), ALU.subtract).then_inc(w1_lo, 1)

            def down_weights_lo(j):
                dve.wait_ge(w2_hi, j + 1)
                nc.vector.tensor_tensor(w2[:, LO, j, :], w2_raw[:, j % 2], w2[:, HI, j, :].bitcast(F32), ALU.subtract).then_inc(w2_lo, 1)

            def normalise_stats(src, i, st, mv, st_ready, mv_ready, count):
                nc.vector.bn_stats(st[:, i, :], src).then_inc(st_ready, 1)
                wait_alone(dve, st_ready, count, passed)
                nc.vector.bn_aggr(mv[:, i, :], st[:, i, :]).then_inc(mv_ready, 1)

            def rows_out(g, i):
                b = bank_of(("proj", i))
                dve.wait_ge(proj_done, g * TG + i + 1)
                wait(dve, xo_ready, g * TG)
                nc.vector.tensor_tensor(ob[:, i, :], ring[b][:, 0:D], keep.bo_row[:], ALU.add).then_inc(o_ready, 1)

            def rows_stats(g, i):
                dve.wait_ge(o_ready, g * TG + i + 1)
                normalise_stats(ob[:, i, :], i, st_h, mv_h, st_h_ready, mv_h_ready, g * TG + i + 1)

            def norm(out, src, i, mv, rs, rs_ready, count, ready):
                dve.wait_ge(rs_ready, count)
                nc.vector.tensor_scalar(out, src, mv[:, i, 0:1], rs[:, i:i + 1], ALU.subtract, ALU.mult).then_inc(ready, 1)

            def rows_lo(use, hi_count):
                dve.wait_ge(zT_hi, hi_count)
                nc.vector.tensor_tensor(zT[:, LO, :, P * use[1]:P * (use[1] + 1)],
                                        ring[bank_of(use)][:].rearrange("p (c n) -> p c n", c=DC),
                                        zT[:, HI, :, P * use[1]:P * (use[1] + 1)].bitcast(F32), ALU.subtract).then_inc(zT_lo, 1)

            def norm_h(g, i):
                norm(z[:, i, :], ob[:, i, :], i, mv_h, rs_h, rs_h_ready, g * TG + i + 1, zh_ready)

            def x1_out(g, i):
                nc.vector.tensor_tensor(xb[:, i, :], acc[i][:, 0:D], xb[:, i, :], ALU.add).then_inc(x1_ready, 1)
                dve.wait_ge(x1_ready, g * TG + i + 1)
                normalise_stats(xb[:, i, :], i, st_q, mv_q, st_q_ready, mv_q_ready, g * TG + i + 1)

            def group(g, first=False, last=False):
                for i in range(TG):
                    rows_lo(("rows", i), g * 2 * TG + i + 1)
                for n in range(2 * FC):
                    j, half = n // 2, n % 2
                    dve.wait_ge(h_hi, g * 2 * FC + n + 1)
                    part = slice(HALF * half, HALF * (half + 1))
                    nc.vector.tensor_tensor(h_hl[:, j % 2, LO, part], h32[:, half, :], h_hl[:, j % 2, HI, part].bitcast(F32),
                                            ALU.subtract).then_inc(h_lo, 1)
                    if first and n % 2 == 0:
                        down_weights_lo(j)
                    if n % 2 == 1 and j + 2 < FC:
                        up_weights_lo(g, j + 2)
                    elif n % 2 == 1 and not last:
                        up_weights_lo(g + 1, j + 2 - FC)
                    if not last and n % 4 == 3 and n // 4 >= 4:
                        attn_lo(g + 1, n // 4 - 4)
                dve.wait_ge(xo_ready, (g + 1) * TG)
                for i in range(TG + 1):
                    if i < TG:
                        dve.wait_ge(down_done, g * DOWNS + FC - 2 + i + 1)
                        x1_out(g, i)
                    if i == TG - 1 and not last:
                        rows_out(g + 1, 0)
                    if i > 0:
                        norm(z[:, i - 1, :], xb[:, i - 1, :], i - 1, mv_q, rs_q, rs_q_ready, g * TG + i, zq_ready)
                if not last:
                    for i in range(1, RB):
                        rows_out(g + 1, i)
                    rows_stats(g + 1, 0)
                for i in range(TG):
                    rows_lo(("qrows", i), g * 2 * TG + TG + i + 1)
                if not last:
                    for i in range(1, RB):
                        rows_stats(g + 1, i)
                    for i in range(RB, TG):
                        rows_out(g + 1, i)
                        rows_stats(g + 1, i)
                wait(dve, c_stored, g * 16)
                dve.wait_ge(zq_ready, (g + 1) * TG)

                def const_out(i):
                    wait(dve, c_ready, g * TG + i)
                    nc.vector.tensor_tensor_reduce(out=junk[:], in0=z[:, i, :], in1=keep.score_row[:], scale=1.0,
                                                   scalar=keep.score_const[:], op0=ALU.mult, op1=ALU.add,
                                                   accum_out=cs[:, i:i + 1]).then_inc(c_ready, 1)
                    if not last:
                        dve.wait_ge(c_ready, g * TG + i + 1)
                        norm_h(g + 1, i)

                for n in range(2 * TC):
                    c, half = n // 2, n % 2
                    part = slice(HALF * half, HALF * (half + 1))
                    dve.wait_ge(t_hi, g * 2 * TC + n + 1)
                    nc.vector.scalar_tensor_tensor(out=wide[:, LO, c, part], in0=ring[bank_of(("query", n))][:, 0:HALF],
                                                   scalar=keep.t_bias[:, c:c + 1], in1=wide[:, HI, c, part].bitcast(F32),
                                                   op0=ALU.add, op1=ALU.subtract).then_inc(t_lo, 1)
                    if n < TG:
                        const_out(n)

            dve.wait_ge(wo_hi, 1)
            nc.vector.tensor_tensor(wo[:, LO], wo_raw, wo[:, HI].bitcast(F32), ALU.subtract).then_inc(wo_lo, 1)
            for k in range(DC):
                attn_lo(0, k)
            for j in range(2):
                up_weights_lo(0, j)
            dve.wait_ge(wo_lo, 1)
            dve.wait_ge(at_lo, DC)
            for i in range(TG + 1):
                if i < TG:
                    rows_out(0, i)
                    rows_stats(0, i)
                if i > 0:
                    norm_h(0, i - 1)
            all_groups(dve, group)

        @block.gpsimd
        def _(pool):
            def inverse_std(mv, ve, rs, i, mv_ready, ve_ready, rs_ready, count):
                wait_alone(pool, mv_ready, count, passed)
                nc.gpsimd.tensor_scalar(ve[:, i:i + 1], mv[:, i, 1:2], EPS, 1.0, ALU.add, ALU.mult).then_inc(ve_ready, 1)
                pool.wait_ge(ve_ready, count)
                nc.gpsimd.tensor_tensor(rs[:, i:i + 1], ve[:, i:i + 1], keep.minus_half[:, 0:1], ALU.pow).then_inc(rs_ready, 1)

            def group(g, first=False, last=False):
                pool.wait_ge(x_loaded, (g + 1) * 16)
                for i in range(TG):
                    nc.gpsimd.tensor_tensor(xb[:, i, :], xb[:, i, :], b2_row[:], ALU.add).then_inc(xb_ready, 1)
                for i in range(TG):
                    pool.wait_ge(xb_ready, g * TG + i + 1)
                    pool.wait_ge(o_ready, g * TG + i + 1)
                    nc.gpsimd.tensor_tensor(xb[:, i, :], xb[:, i, :], ob[:, i, :], ALU.add).then_inc(xo_ready, 1)
                for i in range(TG):
                    inverse_std(mv_q, ve_q, rs_q, i, mv_q_ready, ve_q_ready, rs_q_ready, g * TG + i + 1)
                if not last:
                    for i in range(TG):
                        inverse_std(mv_h, ve_h, rs_h, i, mv_h_ready, ve_h_ready, rs_h_ready, (g + 1) * TG + i + 1)
                for i in range(TG):
                    pool.wait_ge(zq_ready, g * TG + i + 1)
                    nc.gpsimd.tensor_tensor(xb[:, i, :], xb[:, i, :], keep.bd_row[:], ALU.add).then_inc(x1b_ready, 1)

            pool.wait_ge(bias_loaded, 32)
            for i in range(TG):
                inverse_std(mv_h, ve_h, rs_h, i, mv_h_ready, ve_h_ready, rs_h_ready, i + 1)
            all_groups(pool, group)


def attention1_phase(nc, d, io, keep):
    B, N, M, T, E = d.B, d.N, d.M, d.T, d.E
    TC = T // P
    MT = -(-M // P)
    LAST = M - P * (MT - 1)
    TB = MT // 2
    SPLIT = ((0, TB * P), (TB * P, M - TB * P))
    MH = M // 2
    SW = MH + 1
    FILLS = 2 * TC

    def rows_of(t):
        return LAST if t == MT - 1 else P

    with ExitStack() as ctx:
        s = Scope(nc, ctx)
        bw = s.sb("b_bw", [P, 2, TC, E], F32R)
        cn = [s.sb(f"b_cn{i}", [P, MT, T]) for i in range(4)]
        xk = [s.sb(f"b_xk{i}", [P, MT, T]) for i in range(4)]
        xT = [s.sb(f"b_xT{i}", [P, 2, TC, M], F32R) for i in range(2)]
        tq = [s.sb(f"b_tq{i}", [P, 2, TC, N], F32R) for i in range(2)]
        cst, x1 = s.sb("b_cst", [N, 2]), s.sb("b_x1", [N, 2, E])
        st, mv = s.sb("b_st", [P, 2, MT, 6]), s.sb("b_mv", [P, 2, MT, 2])
        ve, neg, rs, shift = (s.sb(f"b_{n}", [P, 2, MT]) for n in ("ve", "neg", "rs", "shift"))
        nmax, bias, sums, inv = (s.sb(f"b_{n}", [N, 2]) for n in ("nmax", "bias", "sums", "inv"))
        pr, pT = s.sb("b_pr", [N, 2, M]), s.sb("b_pT", [P, 2, MT, N])
        uT = s.sb("b_uT", [P, 2, 2, TC * N], F32R)
        y, out = s.sb("b_y", [N, 2, E]), s.sb("b_out", [N, 2, E])
        sc = s.psum("b_sc", [P, 3 * BANK])
        tp = [s.psum(f"b_tp{i}", [P, BANK]) for i in range(2)]
        tt = [s.psum(f"b_tt{i}", [P, BANK]) for i in range(2)]
        ff = s.psum("b_ff", [P, BANK])
        uu = sc[:, 2 * BANK:3 * BANK]
        scores = sc[0:N, 0:2 * (BANK + 1)].rearrange("p (c n) -> p c n", c=2)[:, :, 0:MH]

        passed = keep.passed
        b_loaded, ctx_loaded, t_loaded = s.sem("b_b_loaded"), s.sems("b_ctx_loaded", 4), s.sems("b_t_loaded", 2)
        x1_loaded, out_stored = s.sems("b_x1_loaded", 2), s.sems("b_out_stored", 2)
        zeroed, tail_zeroed = s.sem("b_zeroed"), s.sem("b_tail_zeroed")
        st_ready, mv_ready, ve_ready, neg_ready, rs_ready, shift_ready, xk_ready = (
            s.sem(f"b_{n}_ready") for n in ("st", "mv", "ve", "neg", "rs", "shift", "xk"))
        filled, xT_hi, xT_lo = s.sem("b_filled"), s.sem("b_xT_hi"), s.sem("b_xT_lo")
        scores_done, max_ready, bias_ready, exp_done = (s.sem(f"b_{n}") for n in ("scores_done", "max_ready", "bias_ready", "exp_done"))
        inv_ready = s.sem("b_inv_ready")
        p_turned, pT_ready = s.sem("b_p_turned"), s.sems("b_pT_ready", 2)
        values_done, uT_hi, uT_lo = s.sem("b_values_done"), s.sem("b_uT_hi"), s.sem("b_uT_lo")
        final_done, y_ready, out_ready = s.sem("b_final_done"), s.sem("b_y_ready"), s.sem("b_out_ready")
        block = ctx.enter_context(nc.Block())

        def all_batches(eng, batch):
            for slot in range(4):
                batch(QuadBatch(0, slot), first=slot == 0)
            with eng.Fori(1, B // 4 - 1) as quad:
                for slot in range(4):
                    batch(QuadBatch(quad, slot))
            for slot in range(4):
                batch(QuadBatch(B // 4 - 1, slot), last=slot == 3)

        def exists(b):
            return not isinstance(b.n, int) or b.n < B

        end = QuadBatch(B // 4 - 1, 3)

        @block.sync
        def _(sp):
            def load_ctx(b):
                wait(sp, xk_ready, (b.n - 3) * MT)
                src = io.ctx[bass.ds(b.n, 1), :, :].rearrange("b m t -> (b m) t")
                whole = P * (MT - 1)
                sp.dma_start(cn[b.slot][:, 0:MT - 1, :], src[0:whole, :].rearrange("(t p) d -> p t d", p=P)).then_inc(ctx_loaded[b.slot], 16)
                sp.dma_start(cn[b.slot][0:LAST, MT - 1, :], src[whole:M, :]).then_inc(ctx_loaded[b.slot], 16)

            def load_rows(b):
                wait(sp, scores_done, b.n - 1)
                for hl in range(2):
                    sp.dma_start(tq[b.par][:, hl].bitcast(F32),
                                 keep.t_dram[hl, :, bass.ds(b.n * N, N)].rearrange("(c p) n -> p c n", p=P)).then_inc(t_loaded[b.par], 16)
                wait(sp, bias_ready, b.n - 1)
                sp.dma_start(cst[:, b.par:b.par + 1], keep.c_dram[bass.ds(b.n * N, N), :],
                             allow_slow_non_contiguous=True).then_inc(t_loaded[b.par], 16)
                wait(sp, out_ready, b.n - 1)
                sp.dma_start(x1[:, b.par, :], keep.x1_dram[bass.ds(b.n * N, N), :]).then_inc(x1_loaded[b.par], 16)

            def store(b):
                sp.wait_ge(out_ready, b.n + 1)
                sp.dma_start(io.out.rearrange("b n d -> (b n) d")[bass.ds(b.n * N, N), :], out[:, b.par, :]).then_inc(out_stored[b.par], 16)

            def batch(b, first=False, last=False):
                if exists(b.after(4)):
                    load_ctx(b.after(4))
                if not last:
                    load_rows(b.after(1))
                if not first:
                    store(b.after(-1))

            load_ctx(QuadBatch(0, 0))
            load_rows(QuadBatch(0, 0))
            load_ctx(QuadBatch(0, 1))
            sp.dma_start(bw[:].bitcast(F32), keep.B_dram.rearrange("h (c p) n -> p h c n", p=P)).then_inc(b_loaded, 16)
            for slot in range(2, 4):
                load_ctx(QuadBatch(0, slot))
            all_batches(sp, batch)
            store(end)
            for par in range(2):
                sp.wait_ge(out_stored[par], 16 * (B // 2))

        @block.gpsimd
        def _(pool):
            def inverse_std(b):
                wait_alone(pool, mv_ready, (b.n + 1) * MT, passed)
                nc.gpsimd.tensor_scalar(ve[:, b.par, :], mv[:, b.par, :, 1], EPS, 1.0, ALU.add, ALU.mult).then_inc(ve_ready, 1)
                nc.gpsimd.tensor_scalar(neg[:, b.par, :], mv[:, b.par, :, 0], -1.0, 0.0, ALU.mult, ALU.add).then_inc(neg_ready, 1)
                pool.wait_ge(ve_ready, b.n + 1)
                wait(pool, xk_ready, (b.n - 1) * MT)
                nc.gpsimd.tensor_tensor(rs[:, b.par, :], ve[:, b.par, :], keep.minus_half[:, 0:MT], ALU.pow).then_inc(rs_ready, 1)
                pool.wait_ge(rs_ready, b.n + 1)
                pool.wait_ge(neg_ready, b.n + 1)
                nc.gpsimd.tensor_tensor(shift[:, b.par, :], neg[:, b.par, :], rs[:, b.par, :], ALU.mult).then_inc(shift_ready, 1)

            def add(b):
                pool.wait_ge(y_ready, b.n + 1)
                pool.wait_ge(x1_loaded[b.par], (b.pair + 1) * 16)
                wait(pool, out_stored[b.par], b.pair * 16)
                nc.gpsimd.tensor_tensor(out[:, b.par, :], y[:, b.par, :], x1[:, b.par, :], ALU.add).then_inc(out_ready, 1)

            def batch(b, first=False, last=False):
                if exists(b.after(3)):
                    inverse_std(b.after(3))
                if not first:
                    add(b.after(-1))

            nc.gpsimd.memset(mv[:], 1.0).then_inc(zeroed, 1)
            for slot in range(3):
                inverse_std(QuadBatch(0, slot))
            all_batches(pool, batch)
            add(end)

        @block.tensor
        def _(pe):
            def fill(b, k):
                for n in range(2):
                    if k == 0:
                        pe.wait_ge(xk_ready, b.n * MT + TB * (n + 1))
                    wait(pe, xT_lo, b.n * FILLS + 2 * k + n - 1)
                    for t in range(TB * n, TB * (n + 1)):
                        at0, rows = P * (t - TB * n), rows_of(t)
                        last = nc.tensor.transpose(tp[n][:, at0:at0 + rows], xk[b.slot][0:rows, t, P * k:P * (k + 1)],
                                                   keep.ident[0:rows, 0:rows])
                    last.then_inc(filled, 1)

            def score(b):
                pe.wait_ge(t_loaded[b.par], (b.pair + 1) * 48)
                wait(pe, exp_done, b.n)
                for k in range(TC):
                    pe.wait_ge(xT_lo, b.n * FILLS + 2 * (k + 1))
                    for n in range(2):
                        m0 = n * (MH - 1)
                        for x, y_ in PASSES:
                            last = nc.tensor.matmul(sc[0:N, n * BANK:n * BANK + SW], tq[b.par][:, x, k, :],
                                                    xT[b.par][:, y_, k, m0:m0 + SW],
                                                    start=(k, x, y_) == (0, HI, HI), stop=(k, x, y_) == (TC - 1, LO, HI))
                last.then_inc(scores_done, 1)

            def turn(b):
                pe.wait_ge(exp_done, b.n + 1)
                pe.wait_ge(tail_zeroed, 1)
                for n in range(2):
                    wait(pe, pT_ready[n], b.n)
                    for t in range(TB * n, TB * (n + 1)):
                        at0 = N * (t - TB * n)
                        last = nc.tensor.transpose(tt[n][0:rows_of(t), at0:at0 + N], pr[:, b.par, P * t:P * t + rows_of(t)],
                                                   keep.ident[0:N, 0:N])
                last.then_inc(p_turned, 1)

            def values(b):
                for n in range(2):
                    pe.wait_ge(pT_ready[n], b.n + 1)
                wait(pe, uT_lo, b.n)
                for k in range(TC):
                    for t in range(MT):
                        last = nc.tensor.matmul(uu[:, N * k:N * (k + 1)], xk[b.slot][0:rows_of(t), t, P * k:P * (k + 1)],
                                                pT[0:rows_of(t), b.par, t, :], start=t == 0, stop=t == MT - 1)
                last.then_inc(values_done, 1)

            def final(b):
                pe.wait_ge(uT_lo, b.n + 1)
                wait(pe, y_ready, b.n)
                for k in range(TC):
                    for x, y_ in PASSES:
                        last = nc.tensor.matmul(ff[0:N, 0:E], uT[:, b.par, x, N * k:N * (k + 1)], bw[:, y_, k, :],
                                                start=(k, x, y_) == (0, HI, HI), stop=(k, x, y_) == (TC - 1, LO, HI))
                last.then_inc(final_done, 1)

            def batch(b, first=False, last=False):
                score(b)
                if not last:
                    fill(b.after(1), 0)
                if not first:
                    values(b.after(-1))
                if not last:
                    fill(b.after(1), 1)
                turn(b)
                if not first:
                    final(b.after(-1))
                if not last:
                    for k in range(2, TC):
                        fill(b.after(1), k)

            pe.wait_ge(b_loaded, 16)
            for k in range(TC):
                fill(QuadBatch(0, 0), k)
            all_batches(pe, batch)
            values(end)
            final(end)

        @block.scalar
        def _(act):
            def fill_hi(b, k):
                wait(act, scores_done, b.n - 1)
                for n, (m0, cols) in enumerate(SPLIT):
                    act.wait_ge(filled, b.n * FILLS + 2 * k + n + 1)
                    nc.scalar.activation(xT[b.par][:, HI, k, m0:m0 + cols], tp[n][:, 0:cols], ACT.Copy).then_inc(xT_hi, 1)

            def exp(b):
                act.wait_ge(bias_ready, b.n + 1)
                wait(act, p_turned, b.n - 1)
                nc.scalar.activation(pr[:, b.par, :].rearrange("n (c m) -> n c m", c=2), scores, ACT.Exp,
                                     bias=bias[:, b.par:b.par + 1], accum_out=sums[:, b.par:b.par + 1]).then_inc(exp_done, 1)

            def turned(b):
                act.wait_ge(p_turned, b.n + 1)
                for n in range(2):
                    nc.scalar.activation(pT[:, b.par, TB * n:TB * (n + 1), :],
                                         tt[n][:, 0:TB * N].rearrange("p (t n) -> p t n", n=N), ACT.Copy).then_inc(pT_ready[n], 1)

            def values_hi(b):
                act.wait_ge(values_done, b.n + 1)
                wait(act, final_done, b.n - 1)
                nc.scalar.activation(uT[:, b.par, HI, :], uu[:, 0:TC * N], ACT.Copy).then_inc(uT_hi, 1)

            def normalise(b):
                act.wait_ge(final_done, b.n + 1)
                act.wait_ge(inv_ready, b.n + 1)
                wait(act, out_ready, b.n - 1)
                nc.scalar.activation(y[:, b.par, :], ff[0:N, 0:E], ACT.Copy, scale=inv[:, b.par:b.par + 1]).then_inc(y_ready, 1)

            def layer_norm(b, tiles):
                act.wait_ge(shift_ready, b.n + 1)
                for t in tiles:
                    rows = rows_of(t)
                    wait(act, values_done, b.n - 3)
                    nc.scalar.activation(xk[b.slot][0:rows, t, :], cn[b.slot][0:rows, t, :], ACT.Identity,
                                         bias=shift[0:rows, b.par, t:t + 1], scale=rs[0:rows, b.par, t:t + 1]).then_inc(xk_ready, 1)

            def batch(b, first=False, last=False):
                if not last:
                    fill_hi(b.after(1), 0)
                exp(b)
                if exists(b.after(2)):
                    layer_norm(b.after(2), range(0, TB))
                if not first:
                    values_hi(b.after(-1))
                if not last:
                    fill_hi(b.after(1), 1)
                turned(b)
                if exists(b.after(2)):
                    layer_norm(b.after(2), range(TB, MT))
                if not first:
                    normalise(b.after(-1))
                if not last:
                    for k in range(2, TC):
                        fill_hi(b.after(1), k)

            layer_norm(QuadBatch(0, 0), range(MT))
            for k in range(TC):
                fill_hi(QuadBatch(0, 0), k)
            layer_norm(QuadBatch(0, 1), range(MT))
            act.wait_ge(tail_zeroed, 1)
            all_batches(act, batch)
            values_hi(end)
            normalise(end)

        @block.vector
        def _(dve):
            def stats(b, tiles):
                dve.wait_ge(ctx_loaded[b.slot], (b.quad + 1) * 32)
                for t in tiles:
                    nc.vector.bn_stats(st[0:rows_of(t), b.par, t, :], cn[b.slot][0:rows_of(t), t, :]).then_inc(st_ready, 1)

            def combine(b):
                wait(dve, shift_ready, b.n - 1)
                for t in range(MT):
                    wait_alone(dve, st_ready, b.n * MT + t + 1, passed)
                    nc.vector.bn_aggr(mv[0:rows_of(t), b.par, t, :], st[0:rows_of(t), b.par, t, :]).then_inc(mv_ready, 1)

            def fill_lo(b, k):
                for n, (m0, cols) in enumerate(SPLIT):
                    dve.wait_ge(xT_hi, b.n * FILLS + 2 * k + n + 1)
                    nc.vector.tensor_tensor(xT[b.par][:, LO, k, m0:m0 + cols], tp[n][:, 0:cols],
                                            xT[b.par][:, HI, k, m0:m0 + cols].bitcast(F32), ALU.subtract).then_inc(xT_lo, 1)

            def row_bias(b):
                p = slice(b.par, b.par + 1)
                dve.wait_ge(scores_done, b.n + 1)
                nc.vector.tensor_reduce(nmax[:, p], scores, AX.XY, ALU.max, negate=True).then_inc(max_ready, 1)
                dve.wait_ge(max_ready, b.n + 1)
                nc.vector.tensor_scalar(bias[:, p], nmax[:, p], cst[:, p], cst[:, p], ALU.subtract, ALU.add).then_inc(bias_ready, 1)

            def inverse(b):
                dve.wait_ge(exp_done, b.n + 1)
                nc.vector.reciprocal(inv[:, b.par:b.par + 1], sums[:, b.par:b.par + 1]).then_inc(inv_ready, 1)

            def values_lo(b):
                dve.wait_ge(uT_hi, b.n + 1)
                nc.vector.tensor_tensor(uT[:, b.par, LO, :], uu[:, 0:TC * N], uT[:, b.par, HI, :].bitcast(F32), ALU.subtract).then_inc(uT_lo, 1)

            def batch(b, first=False, last=False):
                row_bias(b)
                if not last:
                    fill_lo(b.after(1), 0)
                if exists(b.after(3)):
                    stats(b.after(3), range(0, TB))
                if not first:
                    values_lo(b.after(-1))
                if not last:
                    fill_lo(b.after(1), 1)
                if exists(b.after(3)):
                    stats(b.after(3), range(TB, MT))
                    combine(b.after(3))
                inverse(b)
                if not last:
                    for k in range(2, TC):
                        fill_lo(b.after(1), k)

            nc.vector.memset(tt[1][:, 0:TB * N], 0.0).then_inc(tail_zeroed, 1)
            dve.wait_ge(zeroed, 1)
            for slot in range(2):
                stats(QuadBatch(0, slot), range(MT))
                combine(QuadBatch(0, slot))
            for k in range(TC):
                fill_lo(QuadBatch(0, 0), k)
            stats(QuadBatch(0, 2), range(MT))
            combine(QuadBatch(0, 2))
            all_batches(dve, batch)
            values_lo(end)


def cross_attention_kernel(nc, io):
    d = Shapes(io)
    B, N, D, M, T = d.B, d.N, d.D, d.M, d.T
    tokens = B * N
    keep = Kept()

    def dram(name, shape):
        return nc.dram_tensor(name, shape, F32, kind="Internal").ap()

    keep.A_dram = dram("folded_A", (2, D, T))
    keep.b1_dram = dram("b1_folded", (1, d.F))
    keep.B_dram = dram("folded_B", (2, T, d.E))
    keep.W1_dram = dram("W1_scaled", (d.F // P, P, D // P, P))
    keep.q_dram = dram("queries", (2, D, tokens))
    keep.attn_dram = dram("attention", (D, tokens))
    keep.x1_dram = dram("x1", (tokens, D))
    keep.t_dram = dram("folded_queries", (2, T, tokens))
    keep.c_dram = dram("score_consts", (tokens, 1))
    with ExitStack() as ctx:
        s = Scope(nc, ctx)
        keep.ident = s.sb("ident", [P, P])
        keep.minus_half = s.sb("minus_half", [P, 8])
        keep.score_row, keep.score_const = s.sb("score_row", [P, D]), s.sb("score_const", [P, 1])
        keep.bd_row, keep.bo_row = s.sb("bd_row", [P, d.E]), s.sb("bo_row", [P, D])
        keep.t_bias = s.sb("t_bias", [P, T // P])
        keep.passed = s.sem("passed")
        with ExitStack() as inner:
            s = Scope(nc, inner)
            keep.wk_hl = s.sb("wk_hl", [P, 2, T // P, D], F32R)
            keep.wv_hl = s.sb("wv_hl", [P, 2, T // P, D], F32R)
            keep.bk0 = s.sb("bk0", [P, D // P])
            keep.bq0, keep.bqs0 = s.sb("bq0", [P, D // P]), s.sb("bqs0", [P, D // P])
            keep.wq_hl = s.sb("wq_hl", [P, 2, D // P, D], F32R)
            keep.cn = [s.sb(f"cn{i}", [P, -(-M // P), T]) for i in range(2)]
            keep.ctx_loaded = s.sems("ctx_loaded", 2)
            with ExitStack() as early:
                s = Scope(nc, early)
                keep.xn, keep.x_loads = s.sb("xn", [N, 2, PER_STEP, D]), s.sems("x_loads", 2)
                fold_phase(nc, d, io, keep)
                queries_phase(nc, d, io, keep)
            attention_phase(nc, d, io, keep)
        tokens_phase(nc, d, io, keep)
        attention1_phase(nc, d, io, keep)


NAMES = ["x", "ctx_768"] + [f"L0_xattn_{n}" for n in (
    "Wq", "bq", "Wk", "bk", "Wv", "bv", "Wo", "bo", "ln_g", "ln_b", "W1", "b1", "W2", "b2")] + [
    f"L1_xattn_{n}" for n in ("Wq", "bq", "Wk", "bk", "Wv", "bv", "Wd", "bd", "g_q", "be_q", "g_kv", "be_kv")]


def kernel(**inputs):
    import numpy as _np
    import concourse.bacc as _bacc
    from concourse import mybir as _mybir
    from concourse.bass_utils import run_bass_kernel_spmd as _run

    nc = _bacc.Bacc("TRN2", target_bir_lowering=False, num_devices=1)
    arrays, aps = {}, {}
    for name in NAMES:
        a = _np.ascontiguousarray(inputs[name])
        arrays[f"in_{name}_dram"] = a
        aps[name] = nc.dram_tensor(f"in_{name}_dram", a.shape, _mybir.dt.from_np(a.dtype), kind="ExternalInput").ap()
    x = arrays["in_x_dram"]
    aps["out"] = nc.dram_tensor("out_0_dram", x.shape, _mybir.dt.from_np(x.dtype), kind="ExternalOutput").ap()
    cross_attention_kernel(nc, Inputs(aps))
    r = _run(nc, [arrays], core_ids=[0])
    return r.results[0]["out_0_dram"]
```
